# Optimizing a Trainium2 kernel written in Bass

```python
import numpy as np
import jax
import jax.numpy as jnp

def _softmax(x, axis=-1):
    return jax.nn.softmax(x, axis=axis)

def _gelu(x):
    return jax.nn.gelu(x, approximate=True)

def _silu(x):
    return jax.nn.silu(x)

def _sigmoid(x):
    return jax.nn.sigmoid(x)

def _layernorm(x, axis=-1, eps=1e-05):
    m = jnp.mean(x, axis=axis, keepdims=True)
    v = jnp.var(x, axis=axis, keepdims=True)
    return (x - m) / jnp.sqrt(v + eps)

def _scatter_add(tgt, idx, src, axis=0):
    return tgt.at[idx].add(src)

def _segment_sum(src, seg, n):
    return jax.ops.segment_sum(src, seg, n)
kernel_name = 'mk_gnn_preln_d4_gnn_r32_c377ca'

def setup_inputs(seed: int=0):
    np.random.seed(seed)
    _w = jnp.asarray

    def _rec_inputs():
        import jax
        import jax.numpy as jnp
        _gk = jax.random.key(seed)
        x = -8.776e-05 + 1 * jax.random.normal(jax.random.fold_in(_gk, 1), (3125, 128), jnp.float32)
        src = jax.random.randint(jax.random.fold_in(_gk, 2), (100000,), 0, 3125, jnp.int32)
        dst = jax.random.randint(jax.random.fold_in(_gk, 3), (100000,), 0, 3125, jnp.int32)
        _o = jnp.argsort(dst, stable=True)
        src = src[_o]
        dst = dst[_o]
        edge_attr_8 = -0.00019784 + 0.999804 * jax.random.normal(jax.random.fold_in(_gk, 12), (100000, 8), jnp.float32)
        edge_type_2 = jax.random.randint(jax.random.fold_in(_gk, 14), (100000,), 0, 2, jnp.int32)
        return (x, src, dst, edge_attr_8, edge_type_2)
    x, src, dst, edge_attr_8, edge_type_2 = _rec_inputs()

    def _L0_gnn_setup():
        import jax, jax.numpy as jnp
        import numpy as np
        N_NODES = 1250
        N_EDGES = 20000
        IN_FEATS = 128
        H_FEATS = 128

        def _sage_conv(h, src, dst, W_self, W_neigh, b, num_nodes):
            msg = h[src]
            agg = jax.ops.segment_sum(msg, dst, num_segments=num_nodes)
            deg = jax.ops.segment_sum(jnp.ones((src.shape[0],), h.dtype), dst, num_segments=num_nodes)
            h_neigh = agg / jnp.maximum(deg, 1.0)[:, None]
            return h @ W_self + h_neigh @ W_neigh + b
        key = jax.random.key(seed)
        ks = jax.random.split(key, 9)
        s = 1.0 / np.sqrt(IN_FEATS)
        return {'in_feat': jax.random.normal(ks[0], (N_NODES, IN_FEATS), jnp.float32), 'src': jax.random.randint(ks[1], (N_EDGES,), 0, N_NODES), 'dst': jax.random.randint(ks[2], (N_EDGES,), 0, N_NODES), 'W_self1': jax.random.normal(ks[3], (IN_FEATS, H_FEATS), jnp.float32) * s, 'W_neigh1': jax.random.normal(ks[4], (IN_FEATS, H_FEATS), jnp.float32) * s, 'b1': jnp.zeros((H_FEATS,), jnp.float32), 'W_self2': jax.random.normal(ks[5], (H_FEATS, H_FEATS), jnp.float32) * s, 'W_neigh2': jax.random.normal(ks[6], (H_FEATS, H_FEATS), jnp.float32) * s, 'b2': jnp.zeros((H_FEATS,), jnp.float32)}
    _L0_gnn_all = _L0_gnn_setup()
    _L0_gnn_in = {k: v for k, v in _L0_gnn_all.items() if k in ('W_self1', 'W_neigh1', 'b1', 'W_self2', 'W_neigh2', 'b2')}
    del _L0_gnn_all

    def _L1_gnn_setup():
        import jax, jax.numpy as jnp
        import numpy as np
        N_NODES = 50000
        N_EDGES = 25000
        D = 128
        EDGE_D = 8
        NEG_SLOPE = 0.2
        EPS = 1e-12
        key = jax.random.key(seed)
        k1, k2, k3, k4, k5 = jax.random.split(key, 5)
        node_fts = jax.random.normal(k1, (N_NODES, D), dtype=jnp.float32)
        edge_fts = jax.random.normal(k2, (N_EDGES, EDGE_D), dtype=jnp.float32)
        edges = jax.random.randint(k3, (2, N_EDGES), 0, N_NODES, dtype=jnp.int64)
        limit = 1.414 * np.sqrt(6.0 / (D + D))
        W_self = jax.random.uniform(k4, (D, D), dtype=jnp.float32, minval=-limit, maxval=limit)
        W_neigh = jax.random.uniform(k5, (D, D), dtype=jnp.float32, minval=-limit, maxval=limit)
        return {'node_fts': node_fts, 'edge_fts': edge_fts, 'edges': edges, 'W_self': W_self, 'W_neigh': W_neigh}
    _L1_gnn_all = _L1_gnn_setup()
    _L1_gnn_in = {k: v for k, v in _L1_gnn_all.items() if k in ('W_self', 'W_neigh')}
    del _L1_gnn_all

    def _L2_gnn_setup():
        import jax, jax.numpy as jnp
        import numpy as np
        IN_DIM = 128
        OUT_DIM = 128
        N_NODES = 10000
        N_EDGES = 20000
        key = jax.random.key(seed)
        ks = jax.random.split(key, 9)
        X = jax.random.normal(ks[0], (N_NODES, IN_DIM), dtype=jnp.float32)
        edge_index = jax.random.randint(ks[1], (2, N_EDGES), 0, N_NODES, dtype=jnp.int64)
        edge_types = jax.random.randint(ks[2], (N_EDGES,), 0, 2, dtype=jnp.int64)
        s = 1.0 / np.sqrt(IN_DIM)
        W_data = jax.random.uniform(ks[3], (OUT_DIM, IN_DIM), minval=-s, maxval=s, dtype=jnp.float32)
        b_data = jax.random.uniform(ks[4], (OUT_DIM,), minval=-s, maxval=s, dtype=jnp.float32)
        W_control = jax.random.uniform(ks[5], (OUT_DIM, IN_DIM), minval=-s, maxval=s, dtype=jnp.float32)
        b_control = jax.random.uniform(ks[6], (OUT_DIM,), minval=-s, maxval=s, dtype=jnp.float32)
        W_self = jax.random.uniform(ks[7], (OUT_DIM, IN_DIM), minval=-s, maxval=s, dtype=jnp.float32)
        b_self = jax.random.uniform(ks[8], (OUT_DIM,), minval=-s, maxval=s, dtype=jnp.float32)
        return {'X': X, 'edge_index': edge_index, 'edge_types': edge_types, 'W_data': W_data, 'b_data': b_data, 'W_control': W_control, 'b_control': b_control, 'W_self': W_self, 'b_self': b_self}
    _L2_gnn_all = _L2_gnn_setup()
    _L2_gnn_in = {k: v for k, v in _L2_gnn_all.items() if k in ('W_data', 'b_data', 'W_control', 'b_control', 'W_self', 'b_self')}
    del _L2_gnn_all

    def _L3_gnn_setup():
        import jax, jax.numpy as jnp
        import numpy as np
        N, F_IN, C_OUT, H = (50000, 128, 32, 4)
        ALPHA = 0.5
        SLOPE = 0.2

        def _gat_conv(x, W, a_src, a_dst, b, src, dst):
            n = x.shape[0]
            h = (x @ W).reshape(n, H, C_OUT)
            e_src = jnp.sum(h * a_src[None], -1)
            e_dst = jnp.sum(h * a_dst[None], -1)
            e = jax.nn.leaky_relu(e_src[src] + e_dst[dst], SLOPE)
            m = jax.ops.segment_max(e, dst, num_segments=n)
            ex = jnp.exp(e - m[dst])
            denom = jax.ops.segment_sum(ex, dst, num_segments=n)
            att = ex / denom[dst]
            msg = h[src] * att[:, :, None]
            out = jax.ops.segment_sum(msg, dst, num_segments=n)
            return out.reshape(n, H * C_OUT) + b
        key = jax.random.key(seed)
        ks = jax.random.split(key, 12)
        x = jax.random.normal(ks[0], (N, F_IN), dtype=jnp.float32)
        edge_index = jax.random.randint(ks[1], (2, 50000), 0, N, dtype=jnp.int64)

        def gat_params(k):
            k1, k2, k3, k4 = jax.random.split(k, 4)
            W = jax.random.normal(k1, (F_IN, H * C_OUT), dtype=jnp.float32) * 0.1
            a_src = jax.random.normal(k2, (H, C_OUT), dtype=jnp.float32) * 0.1
            a_dst = jax.random.normal(k3, (H, C_OUT), dtype=jnp.float32) * 0.1
            b = jax.random.normal(k4, (H * C_OUT,), dtype=jnp.float32) * 0.1
            return (W, a_src, a_dst, b)
        W1, a_src1, a_dst1, b1 = gat_params(ks[2])
        W2, a_src2, a_dst2, b2 = gat_params(ks[3])
        return {'x': x, 'edge_index': edge_index, 'W1': W1, 'a_src1': a_src1, 'a_dst1': a_dst1, 'b1': b1, 'W2': W2, 'a_src2': a_src2, 'a_dst2': a_dst2, 'b2': b2}
    _L3_gnn_all = _L3_gnn_setup()
    _L3_gnn_in = {k: v for k, v in _L3_gnn_all.items() if k in ('W1', 'a_src1', 'a_dst1', 'b1', 'W2', 'a_src2', 'a_dst2', 'b2')}
    del _L3_gnn_all
    return {'x': x, 'src': src, 'dst': dst, 'edge_attr_8': edge_attr_8, 'edge_type_2': edge_type_2, 'L0_gnn_W_self1': _L0_gnn_in['W_self1'], 'L0_gnn_W_neigh1': _L0_gnn_in['W_neigh1'], 'L0_gnn_b1': _L0_gnn_in['b1'], 'L0_gnn_W_self2': _L0_gnn_in['W_self2'], 'L0_gnn_W_neigh2': _L0_gnn_in['W_neigh2'], 'L0_gnn_b2': _L0_gnn_in['b2'], 'L1_gnn_W_self': _L1_gnn_in['W_self'], 'L1_gnn_W_neigh': _L1_gnn_in['W_neigh'], 'L2_gnn_W_data': _L2_gnn_in['W_data'], 'L2_gnn_b_data': _L2_gnn_in['b_data'], 'L2_gnn_W_control': _L2_gnn_in['W_control'], 'L2_gnn_b_control': _L2_gnn_in['b_control'], 'L2_gnn_W_self': _L2_gnn_in['W_self'], 'L2_gnn_b_self': _L2_gnn_in['b_self'], 'L3_gnn_W1': _L3_gnn_in['W1'], 'L3_gnn_a_src1': _L3_gnn_in['a_src1'], 'L3_gnn_a_dst1': _L3_gnn_in['a_dst1'], 'L3_gnn_b1': _L3_gnn_in['b1'], 'L3_gnn_W2': _L3_gnn_in['W2'], 'L3_gnn_a_src2': _L3_gnn_in['a_src2'], 'L3_gnn_a_dst2': _L3_gnn_in['a_dst2'], 'L3_gnn_b2': _L3_gnn_in['b2']}

def reference(x, src, dst, edge_attr_8, edge_type_2, L0_gnn_W_self1, L0_gnn_W_neigh1, L0_gnn_b1, L0_gnn_W_self2, L0_gnn_W_neigh2, L0_gnn_b2, L1_gnn_W_self, L1_gnn_W_neigh, L2_gnn_W_data, L2_gnn_b_data, L2_gnn_W_control, L2_gnn_b_control, L2_gnn_W_self, L2_gnn_b_self, L3_gnn_W1, L3_gnn_a_src1, L3_gnn_a_dst1, L3_gnn_b1, L3_gnn_W2, L3_gnn_a_src2, L3_gnn_a_dst2, L3_gnn_b2):
    import jax
    import jax.numpy as jnp

    def _L0_gnn_ref(in_feat, src, dst, W_self1, W_neigh1, b1, W_self2, W_neigh2, b2):
        import jax, jax.numpy as jnp
        import numpy as np
        N_NODES = 1250
        N_EDGES = 20000
        IN_FEATS = 128
        H_FEATS = 128

        def _sage_conv(h, src, dst, W_self, W_neigh, b, num_nodes):
            msg = h[src]
            agg = jax.ops.segment_sum(msg, dst, num_segments=num_nodes)
            deg = jax.ops.segment_sum(jnp.ones((src.shape[0],), h.dtype), dst, num_segments=num_nodes)
            h_neigh = agg / jnp.maximum(deg, 1.0)[:, None]
            return h @ W_self + h_neigh @ W_neigh + b
        n = in_feat.shape[0]
        h = _sage_conv(in_feat, src, dst, W_self1, W_neigh1, b1, n)
        h = jax.nn.relu(h)
        h = _sage_conv(h, src, dst, W_self2, W_neigh2, b2, n)
        return h

    def _L1_gnn_ref(node_fts, edge_fts, edges, W_self, W_neigh):
        import jax, jax.numpy as jnp
        import numpy as np
        N_NODES = 50000
        N_EDGES = 25000
        D = 128
        EDGE_D = 8
        NEG_SLOPE = 0.2
        EPS = 1e-12
        edges_u = jnp.concatenate([edges, edges[::-1]], axis=1)
        src_idx, dst_idx = (edges_u[0], edges_u[1])
        n = node_fts.shape[0]
        src_node_fts = node_fts @ W_self.T
        gathered = node_fts[dst_idx]
        summed = jax.ops.segment_sum(gathered, src_idx, num_segments=n)
        counts = jax.ops.segment_sum(jnp.ones((gathered.shape[0],), dtype=node_fts.dtype), src_idx, num_segments=n)
        mean_agg = summed / jnp.maximum(counts, 1.0)[:, None]
        neigh = jax.nn.leaky_relu(mean_agg @ W_neigh.T, NEG_SLOPE)
        out = jax.nn.leaky_relu(src_node_fts + neigh, NEG_SLOPE)
        norm = jnp.linalg.norm(out, axis=1, keepdims=True)
        return out / jnp.maximum(norm, EPS)

    def _L2_gnn_ref(X, edge_index, edge_types, W_data, b_data, W_control, b_control, W_self, b_self):
        import jax, jax.numpy as jnp
        import numpy as np
        IN_DIM = 128
        OUT_DIM = 128
        N_NODES = 10000
        N_EDGES = 20000
        src, dst = (edge_index[0], edge_index[1])
        Xs = X[src]
        m_data = Xs @ W_data.T + b_data
        m_ctrl = Xs @ W_control.T + b_control
        msg = jnp.where((edge_types == 0)[:, None], m_data, m_ctrl)
        agg = jax.ops.segment_sum(msg, dst, num_segments=X.shape[0])
        out = agg + (X @ W_self.T + b_self)
        return jax.nn.relu(out)

    def _L3_gnn_ref(x, edge_index, W1, a_src1, a_dst1, b1, W2, a_src2, a_dst2, b2):
        import jax, jax.numpy as jnp
        import numpy as np
        N, F_IN, C_OUT, H = (50000, 128, 32, 4)
        ALPHA = 0.5
        SLOPE = 0.2

        def _gat_conv(x, W, a_src, a_dst, b, src, dst):
            n = x.shape[0]
            h = (x @ W).reshape(n, H, C_OUT)
            e_src = jnp.sum(h * a_src[None], -1)
            e_dst = jnp.sum(h * a_dst[None], -1)
            e = jax.nn.leaky_relu(e_src[src] + e_dst[dst], SLOPE)
            m = jax.ops.segment_max(e, dst, num_segments=n)
            ex = jnp.exp(e - m[dst])
            denom = jax.ops.segment_sum(ex, dst, num_segments=n)
            att = ex / denom[dst]
            msg = h[src] * att[:, :, None]
            out = jax.ops.segment_sum(msg, dst, num_segments=n)
            return out.reshape(n, H * C_OUT) + b
        n = x.shape[0]
        loops = jnp.arange(n, dtype=edge_index.dtype)
        src = jnp.concatenate([edge_index[0], loops])
        dst = jnp.concatenate([edge_index[1], loops])
        src_t = jnp.concatenate([edge_index[1], loops])
        dst_t = jnp.concatenate([edge_index[0], loops])
        out_fwd = _gat_conv(x, W1, a_src1, a_dst1, b1, src, dst)
        out_bwd = _gat_conv(x, W2, a_src2, a_dst2, b2, src_t, dst_t)
        return (1.0 - ALPHA) * out_fwd + ALPHA * out_bwd
    edge_index = jnp.stack([src, dst])
    h = jnp.maximum(_layernorm(x, axis=-1), 0.0)
    x = x + _L0_gnn_ref(h, src, dst, L0_gnn_W_self1, L0_gnn_W_neigh1, L0_gnn_b1, L0_gnn_W_self2, L0_gnn_W_neigh2, L0_gnn_b2)
    h = jnp.maximum(_layernorm(x, axis=-1), 0.0)
    x = x + _L1_gnn_ref(h, edge_attr_8, edge_index, L1_gnn_W_self, L1_gnn_W_neigh)
    h = jnp.maximum(_layernorm(x, axis=-1), 0.0)
    x = x + _L2_gnn_ref(h, edge_index, edge_type_2, L2_gnn_W_data, L2_gnn_b_data, L2_gnn_W_control, L2_gnn_b_control, L2_gnn_W_self, L2_gnn_b_self)
    h = jnp.maximum(_layernorm(x, axis=-1), 0.0)
    x = x + _L3_gnn_ref(h, edge_index, L3_gnn_W1, L3_gnn_a_src1, L3_gnn_a_dst1, L3_gnn_b1, L3_gnn_W2, L3_gnn_a_src2, L3_gnn_a_dst2, L3_gnn_b2)
    return x

_drawn_inputs = setup_inputs


def setup_inputs(seed=0):
    import zlib

    import numpy as np

    out = dict(_drawn_inputs(seed))
    spreads = {'L0_gnn_b1': (0.0, 0.1), 'L0_gnn_b2': (0.0, 0.1)}
    factors = {'L2_gnn_b_self': 7.745,
     'L3_gnn_a_src1': 24.904,
     'L3_gnn_a_dst1': 64.0,
     'L3_gnn_b1': 5.946,
     'L3_gnn_a_src2': 34.081,
     'L3_gnn_a_dst2': 43.149,
     'L3_gnn_b2': 5.974}
    for name, (base, spread) in spreads.items():
        noise = np.random.default_rng([zlib.crc32(name.encode()), seed]).standard_normal(out[name].shape)
        drawn = base * np.exp(spread * noise) if base else spread * noise
        out[name] = jnp.asarray(drawn.astype(out[name].dtype))
    for name, factor in factors.items():
        out[name] = (out[name] * factor).astype(out[name].dtype)
    return out
```

```python
from contextlib import ExitStack

import numpy as np
from concourse import bass, mybir

F32 = mybir.dt.float32
F16 = mybir.dt.float16
BF16 = mybir.dt.bfloat16
I32 = mybir.dt.int32
ALU = mybir.AluOpType
ACT = mybir.ActivationFunctionType
AX = mybir.AxisListType

P = 128
N = 3125
D = 128
E = 100000
NT = -(-N // P)
NPAD = NT * P
HEADS, CH = 4, 32
EPS_LN = 1e-5
EPS_NORM = 1e-12
SLOPE = 0.2
MILD_SCORE, MILD_FEATURE = 70.0, 1000.0
BIG = 1.0e30

ER = 112
ET = 7
EC = ER * ET
FULL_ROWS = E // P
REST = E - FULL_ROWS * P
LAST_ROWS = FULL_ROWS - ER * (ET - 1)
PAD_DST = 16383.0

WD = 8
WCOL = 4
WCELLS = WD * NT
QUAD = 4
WPG = P // WD
NW = NT * WPG
HALF = (16, NT - 16)

CHUNK = 640
NCHUNK = NPAD // CHUNK
CT_TILES = CHUNK // P
MMC = CHUNK // 2
BANK = 512
NBANK = -(-NPAD // BANK)
GROUPS = 5


def bank_cols(q):
    return min(BANK, NPAD - q * BANK)


class Mode:

    def __init__(self, fast):
        self.fast = fast
        self.dt = F16 if fast else F32
        self.slots = 2 if fast else 1
        self.banks = QUAD if fast else 1
        self.parts = 2 if fast else 1

    def view(self, ap):
        if not self.fast:
            return ap
        flat = ap.bitcast(F16)
        return flat[:, 0:flat.shape[1] // 2]


class Chain:

    def __init__(self, eng, sem):
        self.eng, self.sem, self.n = eng, sem, 0

    def __call__(self, ins):
        self.n += 1
        ins.then_inc(self.sem, 1)
        self.eng.wait_ge(self.sem, self.n)


def program(nc, a, out, dbg=None):
    fast, general = Mode(True), Mode(False)
    top = ExitStack()

    def dram(name, shape, dt=F32):
        return nc.dram_tensor(name, shape, dt, kind="Internal").ap()

    adj = {}
    for m in (fast, general):
        k = "f" if m.fast else "g"
        for what in ("t0", "t1", "sd", "ds"):
            adj[m, what] = dram(f"adj_{what}_{k}", [NPAD, NPAD], m.dt)
    rows_dram = dram("rows_dram", [8, HEADS, NPAD])

    def sb(ctx, name, shape, dt=F32):
        return ctx.enter_context(nc.sbuf_tensor(name, shape, dt))

    def pb(ctx, name, shape, dt=F32):
        return ctx.enter_context(nc.psum_tensor(name, shape, dt))

    def sem(name):
        return top.enter_context(nc.semaphore(name))

    X = sb(top, "X", [P, NT, D])
    hidden = ExitStack()
    ident = sb(top, "ident", [P, P])
    ident16 = sb(top, "ident16", [P, P], F16)
    ones = sb(top, "ones", [P, P])
    ones16 = sb(top, "ones16", [P, 1], F16)
    small = sb(top, "small", [P, 8])
    flag = sb(top, "flag", [1, 1], I32)
    MILD, HARSH, ANY_EDGES, NOT_MILD = range(4)
    path = sb(top, "path", [1, 4], I32)
    rdeg_in = sb(top, "rdeg_in", [P, NT])
    rdeg_all = sb(top, "rdeg_all", [P, NT])
    WN = ["L0_gnn_W_self1", "L0_gnn_W_neigh1", "L0_gnn_W_self2", "L0_gnn_W_neigh2", "L1_gnn_W_self",
          "L1_gnn_W_neigh", "L2_gnn_W_data", "L2_gnn_W_control", "L2_gnn_W_self", "L3_gnn_W1", "L3_gnn_W2"]
    TURNED = range(4, 9)
    W = sb(top, "W", [P, len(WN), D])
    w_of = {n: W[:, i, :] for i, n in enumerate(WN)}
    BN = ["L0_gnn_b1", "L0_gnn_b2", "L2_gnn_b_data", "L2_gnn_b_control", "L2_gnn_b_self", "L3_gnn_b1",
          "L3_gnn_b2", "L3_gnn_a_src1", "L3_gnn_a_dst1", "L3_gnn_a_src2", "L3_gnn_a_dst2"]
    B = sb(top, "B", [P, len(BN), D])
    b_of = {n: B[:, i, :] for i, n in enumerate(BN)}

    CH1 = CH + 1
    GE = sb(top, "GE", [P, 2, NT, HEADS, CH1])
    ES = sb(top, "ES", [P, 2, 2, HEADS, NT])
    ES2 = sb(top, "ES2", [P, 2, HEADS, NT])
    MX = sb(top, "MX", [P, 2, HEADS, NT])
    EM = sb(top, "EM", [P, 2, 2, HEADS, NT])
    XS = sb(top, "XS", [P, 2, NT, HEADS])
    rows = sb(top, "rows", [P, 6, P])

    def is_fast(eng):
        return eng.value_load(flag[0:1, 0:1], min_val=0, max_val=1)

    def on_path(eng, which, body):
        with eng.If(eng.value_load(path[0:1, which:which + 1], min_val=0, max_val=1)):
            body(eng)
            eng.nop()
        with eng.Else():
            eng.nop()

    def both(eng, body):
        with eng.If(is_fast(eng)):
            body(eng, fast)
            eng.nop()
        with eng.Else():
            body(eng, general)
            eng.nop()

    edges = ExitStack()
    EK = sb(edges, "EK", [P, 3, EC])
    CT = sb(edges, "CT", [1, NW], I32)
    with ExitStack() as ctx:
        edst = sb(ctx, "edst", [P, ET, P], I32)
        enext = sb(ctx, "enext", [P, ET, P], I32)
        esrc = sb(ctx, "esrc", [P, ET, P], I32)
        etyp = sb(ctx, "etyp", [P, ET, P], I32)
        ehi = sb(ctx, "ehi", [P, ET, P], I32)
        elo = sb(ctx, "elo", [P, ET, P], I32)
        keys = sb(ctx, "keys", [P, 3, ET, P])
        first8 = sb(ctx, "first8", [P, ET])
        last = sb(ctx, "last", [P, ET])
        junk = sb(ctx, "junk", [P, ET, P])
        unsorted = sb(ctx, "unsorted", [P, 1])
        thr = sb(ctx, "thr", [P, NW])
        cnt = sb(ctx, "cnt", [P, 2, NW])
        spans = sb(ctx, "spans", [1, NW])
        crow = sb(ctx, "crow", [1, 2, NW])
        fl = sb(ctx, "fl", [1, 4])
        pkeys = pb(ctx, "pkeys", [P, 4, BANK])
        pcnt = pb(ctx, "pcnt", [P, 3, BANK])
        pw = pb(ctx, "pw", [P, BANK])
        ready = {k: sem(f"p1_{k}") for k in ("loads", "weights", "const", "keys", "cnt", "turned", "copied", "dve", "wt", "wtc", "x", "pre")}

        with nc.Block() as block:
            @block.sync
            def _(sp):
                sp.wait_ge(ready["pre"], 5)
                for dst, src in ((edst, a["dst"]), (esrc, a["src"]), (etyp, a["edge_type_2"])):
                    body = ER * (ET - 1) * P
                    sp.dma_start(dst[0:ER, 0:ET - 1, :], src[0:body].rearrange("(t r q) -> r t q", t=ET - 1, q=P)).then_inc(ready["loads"], 16)
                    sp.dma_start(dst[0:LAST_ROWS, ET - 1, :], src[body:body + LAST_ROWS * P].rearrange("(r q) -> r q", q=P)).then_inc(ready["loads"], 16)
                    sp.dma_start(dst[LAST_ROWS:LAST_ROWS + 1, ET - 1, 0:REST], src[FULL_ROWS * P:E].rearrange("(r q) -> r q", r=1)).then_inc(ready["loads"], 16)
                body = ER * (ET - 1) * P
                src = a["dst"]
                sp.dma_start(enext[0:ER, 0:ET - 1, :], src[1:1 + body].rearrange("(t r q) -> r t q", t=ET - 1, q=P)).then_inc(ready["loads"], 16)
                sp.dma_start(enext[0:LAST_ROWS, ET - 1, :], src[1 + body:1 + body + LAST_ROWS * P].rearrange("(r q) -> r q", q=P)).then_inc(ready["loads"], 16)
                sp.dma_start(enext[LAST_ROWS:LAST_ROWS + 1, ET - 1, 0:REST - 1], src[1 + FULL_ROWS * P:E].rearrange("(r q) -> r q", r=1)).then_inc(ready["loads"], 16)

            @block.scalar
            def _(act):
                for i, n in enumerate(WN):
                    act.dma_start(W[:, i, :], a[n]).then_inc(ready["weights"], 16)
                for i, n in enumerate(BN):
                    v = a[n] if len(a[n].shape) == 1 else a[n].rearrange("h c -> (h c)")
                    act.dma_start(B[:, i, :], v.partition_broadcast(P)).then_inc(ready["weights"], 16)
                act.wait_ge(ready["pre"], 5)
                act.dma_start(X[:, 0:NT - 1, :], a["x"][0:(NT - 1) * P, :].rearrange("(t p) d -> p t d", p=P)).then_inc(ready["x"], 16)
                act.dma_start(X[0:N - (NT - 1) * P, NT - 1, :], a["x"][(NT - 1) * P:N, :]).then_inc(ready["x"], 16)
                act.wait_ge(ready["x"], 32)

            @block.gpsimd
            def _(pool):
                pool.memset(edst[:, :, :], int(PAD_DST)).then_inc(ready["pre"], 1)
                pool.memset(enext[:, :, :], int(PAD_DST)).then_inc(ready["pre"], 1)
                pool.memset(esrc[:, :, :], 0).then_inc(ready["pre"], 1)
                pool.memset(etyp[:, :, :], 0).then_inc(ready["pre"], 1)
                pool.memset(X[:, NT - 1, :], 0.0).then_inc(ready["pre"], 1)
                pool.memset(ident[:, :], 0.0).then_inc(ready["const"], 1)
                pool.memset(ones[:, :], 1.0).then_inc(ready["const"], 1)
                pool.memset(ones16[:, :], 1.0).then_inc(ready["const"], 1)
                pool.memset(small[:, 0:1], EPS_LN).then_inc(ready["const"], 1)
                pool.wait_ge(ready["const"], 4)
                pool.affine_select(out=ident[:, :], in_=ident[:, :], compare_op=ALU.not_equal, fill=1.0, base=0,
                                   pattern=[[-1, P]], channel_multiplier=1).then_inc(ready["const"], 1)
                pool.wait_ge(ready["const"], 5)
                pool.tensor_copy(ident16[:, :], ident[:, :]).then_inc(ready["const"], 1)
                pool.iota(thr[:, :], pattern=[[WD, NW]], base=0, channel_multiplier=0,
                          allow_small_or_imprecise_dtypes=True).then_inc(ready["const"], 1)

            @block.vector
            def _(dve):
                step = Chain(dve, ready["dve"])
                dve.wait_ge(ready["loads"], 12 * 16)
                step(nc.vector.tensor_tensor(junk[:, :, :], enext[:, :, :], edst[:, :, :], ALU.is_lt))
                step(nc.vector.reduce_sum(unsorted[:, :], junk[:, :, :].rearrange("p t q -> p (t q)"), axis=AX.X))
                step(nc.vector.tensor_scalar(ehi[:, :, :], esrc[:, :, :], 7, None, ALU.logical_shift_right))
                step(nc.vector.tensor_scalar(elo[:, :, :], esrc[:, :, :], P - 1, None, ALU.bitwise_and))
                step(nc.vector.scalar_tensor_tensor(out=keys[:, 0, :, :].rearrange("p t q -> p (t q)"), in0=edst[:, :, :].rearrange("p t q -> p (t q)"), scalar=float(NT), in1=ehi[:, :, :].rearrange("p t q -> p (t q)"),
                                                    op0=ALU.mult, op1=ALU.add))
                step(nc.vector.scalar_tensor_tensor(out=keys[:, 1, :, :].rearrange("p t q -> p (t q)"), in0=etyp[:, :, :].rearrange("p t q -> p (t q)"), scalar=1000.0, in1=elo[:, :, :].rearrange("p t q -> p (t q)"),
                                                    op0=ALU.mult, op1=ALU.add))
                step(nc.vector.tensor_scalar(junk[:, :, :], etyp[:, :, :], -1000.0, 1000.0, ALU.mult, ALU.add))
                nc.vector.tensor_tensor(keys[:, 2, :, :], junk[:, :, :], elo[:, :, :], ALU.add).then_inc(ready["keys"], 1)
                step(nc.vector.tensor_copy(last[:, :], edst[:, :, P - 1]))
                step(nc.vector.tensor_scalar(first8[:, :], edst[:, :, 0], -float(WD), None, ALU.add))
                dve.wait_ge(ready["const"], 7)
                step(nc.vector.memset(cnt[:, :, :], 0.0))
                for i, edge in enumerate((last, first8)):
                    for t in range(ET):
                        step(nc.vector.scalar_tensor_tensor(out=cnt[:, i, :], in0=thr[:, :], scalar=edge[:, t:t + 1],
                                                            in1=cnt[:, i, :], op0=ALU.is_gt, op1=ALU.add))
                nc.vector.memset(fl[:, :], 0.0).then_inc(ready["cnt"], 1)
                for b in range(3 * ET):
                    dve.wait_ge(ready["turned"], b + 1)
                    i, t = b // ET, b % ET
                    nc.vector.tensor_copy(EK[:, i, t * ER:(t + 1) * ER], pkeys[:, b % 4, 0:ER]).then_inc(ready["copied"], 1)
                dve.wait_ge(ready["turned"], 3 * ET + 1)
                step(nc.vector.tensor_copy(crow[:, 0, :], pcnt[0:1, 0, 0:NW]))
                step(nc.vector.tensor_scalar(crow[:, 0, :], crow[:, 0, :], float(EC - WCOL), None, ALU.min))
                step(nc.vector.tensor_tensor(spans[:, :], pcnt[0:1, 1, 0:NW], crow[:, 0, :], ALU.subtract))
                step(nc.vector.tensor_copy(CT[:, :], crow[:, 0, :]))
                step(nc.vector.reduce_max(fl[:, 0:1], spans[:, :], axis=AX.X))
                step(nc.vector.tensor_scalar(fl[:, 1:2], fl[:, 0:1], float(WCOL), None, ALU.is_le))
                step(nc.vector.tensor_scalar(fl[:, 2:3], pcnt[0:1, 2, 0:1], 0.0, None, ALU.is_equal))
                step(nc.vector.tensor_tensor(flag[:, :], fl[:, 1:2], fl[:, 2:3], ALU.mult))
                for b, i in enumerate(TURNED):
                    dve.wait_ge(ready["wt"], b + 1)
                    nc.vector.tensor_copy(W[:, i, :], pw[:, 0:P]).then_inc(ready["wtc"], 1)

            @block.tensor
            def _(pe):
                pe.wait_ge(ready["keys"], 1)
                pe.wait_ge(ready["const"], 5)
                for b in range(3 * ET):
                    i, t = b // ET, b % ET
                    if b >= 4:
                        pe.wait_ge(ready["copied"], b - 3)
                    nc.tensor.transpose(pkeys[:, b % 4, 0:ER], keys[0:ER, i, t, :], ident[0:ER, 0:ER]).then_inc(ready["turned"], 1)
                pe.wait_ge(ready["cnt"], 1)
                nc.tensor.matmul(pcnt[0:1, 0, 0:NW], ones[0:ER, 0:1], cnt[0:ER, 0, :], start=True, stop=True)
                nc.tensor.matmul(pcnt[0:1, 1, 0:NW], ones[0:ER, 0:1], cnt[0:ER, 1, :], start=True, stop=True)
                nc.tensor.matmul(pcnt[0:1, 2, 0:1], ones[0:ER, 0:1], unsorted[0:ER, 0:1], start=True, stop=True).then_inc(ready["turned"], 1)
                pe.wait_ge(ready["weights"], 16 * (len(WN) + len(BN)))
                for b, i in enumerate(TURNED):
                    if b:
                        pe.wait_ge(ready["wtc"], b)
                    nc.tensor.transpose(pw[:, 0:P], W[:, i, :], ident[:, :]).then_inc(ready["wt"], 1)

    with ExitStack() as ctx:
        SG = sb(ctx, "SG", [P, 2, 2 * NPAD])
        SS = sb(ctx, "SS", [P, 2, NPAD])
        SDS = sb(ctx, "SDS", [P, 2, NPAD])
        iota_w = sb(ctx, "iota_w", [P, WCELLS, WCOL], F16)
        iota_l = sb(ctx, "iota_l", [P, P, WCOL], F16)
        base_w = sb(ctx, "base_w", [P, NW])
        KZ = sb(ctx, "KZ", [P, BANK], F16)
        KW = sb(ctx, "KW", [P, 1])
        RAW = sb(ctx, "RAW", [P, 2, WPG, 3, WCOL])
        KD = sb(ctx, "KD", [P, WPG, WCOL])
        KC = sb(ctx, "KC", [P, 2, WPG, WCOL], F16)
        KL = sb(ctx, "KL", [P, 2, 2, WPG, WCOL], F16)
        OH = sb(ctx, "OH", [P, 2, 2, QUAD, P, WCOL], F16)
        MV = sb(ctx, "MV", [P, 2, QUAD, WCELLS, WCOL], F16)
        iota_g = SDS[:, 1, :]
        PW = pb(ctx, "PW", [P, 2, BANK])
        PT = pb(ctx, "PT", [P, 2, BANK])
        PDI = pb(ctx, "PDI", [P, BANK])
        PDO = pb(ctx, "PDO", [P, BANK])
        PGX = pb(ctx, "PGX", [P, 2, BANK])
        s = {k: sem(f"p2_{k}") for k in ("const", "kw", "raw", "keyed", "onehot", "window", "free_oh", "evac", "sum", "turned", "tevac", "deg", "st_out0", "group", "free_st", "dve")}

        def view2(m, t, slot):
            return m.view(t[:, slot, :])

        def rest(slot, m):
            return view2(m, SG, slot).rearrange("p (y b d) -> p y b d", y=2, b=NT), view2(m, SS, slot), view2(m, SDS, slot)

        with nc.Block() as block:
            def loop_groups(eng, windows, finish):
                windows(0, 0)
                with eng.Fori(0, (NT - 1) // 2) as pair:
                    g = pair * 2
                    windows(g + 1, 1)
                    finish(g, 0)
                    windows(g + 2, 0)
                    finish(g + 1, 1)
                finish(NT - 1, 0)

            def serial_groups(eng, windows, finish):
                with eng.Fori(0, NT) as g:
                    windows(g, 0)
                    finish(g, 0)

            def run(eng, m, windows, finish):
                (loop_groups if m.fast else serial_groups)(eng, windows, finish)

            @block.gpsimd
            def _(pool):
                pool.memset(KZ[:, :], 0.0).then_inc(s["const"], 1)
                pool.iota(iota_w[:, :, :].rearrange("p (b d) c -> p b d c", b=NT), pattern=[[1, NT], [NT, WD], [0, WCOL]], base=0, channel_multiplier=0,
                          allow_small_or_imprecise_dtypes=True).then_inc(s["const"], 1)
                pool.iota(iota_l[:, :, :], pattern=[[1, P], [0, WCOL]], base=0, channel_multiplier=0,
                          allow_small_or_imprecise_dtypes=True).then_inc(s["const"], 1)
                pool.iota(base_w[:, :], pattern=[[WCELLS, NW]], base=0, channel_multiplier=0,
                          allow_small_or_imprecise_dtypes=True).then_inc(s["const"], 1)

                def body(pool, m):
                    if not m.fast:
                        pool.iota(iota_g.rearrange("p (b d) -> p b d", b=NT), pattern=[[1, NT], [NT, P]], base=0, channel_multiplier=0,
                                  allow_small_or_imprecise_dtypes=True).then_inc(s["const"], 1)

                    def finish(g, slot):
                        st, both_types, _ = rest(slot, m)
                        pool.wait_ge(s["evac"], m.banks + (g + 1) * (WPG if m.fast else 4))
                        pool.wait_ge(s["group"], g + 1)
                        flat = st.rearrange("p y b d -> p y (b d)")
                        nc.gpsimd.tensor_tensor(both_types, flat[:, 0, :], flat[:, 1, :], ALU.add).then_inc(s["sum"], 1)

                    def windows(g, slot):
                        if m.fast:
                            with pool.Fori(0, WPG) as w:
                                pool.wait_ge(s["keyed"], g * 2 + 2)
                                c0 = pool.value_load(CT[0:1, bass.ds(g * WPG + w, 1)], min_val=0, max_val=EC - WCOL)
                                nc.gpsimd.tensor_copy(RAW[:, slot, bass.ds(w, 1), :, :].rearrange("p o y c -> p (o y) c"), EK[:, :, bass.ds(c0, WCOL)]).then_inc(s["raw"], 1)
                    run(pool, m, windows, finish)
                both(pool, body)

            @block.vector
            def _(dve):
                def body(dve, m):
                    dve.sem_inc(s["keyed"], 4)
                    dve.wait_ge(s["const"], 4 if m.fast else 5)

                    def quad(n4, q, u, slot, g):
                        w0 = bass.ds(q * QUAD, QUAD)
                        dve.wait_ge(s["keyed"], g * 2 + 6)
                        dve.wait_ge(s["window"], n4 * QUAD + QUAD)
                        for y in range(2):
                            nc.vector.tensor_tensor(OH[:, u, y, :, :, :], iota_l[:, :, :].unsqueeze(1).to_broadcast([P, QUAD, P, WCOL]),
                                                    KL[:, slot, y, w0, :].unsqueeze(2).to_broadcast([P, QUAD, P, WCOL]), ALU.is_equal)
                        nc.vector.tensor_tensor(MV[:, u, :, :, :], iota_w[:, :, :].unsqueeze(1).to_broadcast([P, QUAD, WCELLS, WCOL]),
                                                KC[:, slot, w0, :].unsqueeze(2).to_broadcast([P, QUAD, WCELLS, WCOL]), ALU.is_equal).then_inc(s["onehot"], 1)

                    if m.fast:
                        def windows(g, slot):
                            dve.wait_ge(s["raw"], g * WPG + WPG)
                            nc.vector.tensor_tensor(KD[:, :, :], RAW[:, slot, :, 0, :], base_w[:, bass.ds(g * WPG, WPG)].unsqueeze(2).to_broadcast([P, WPG, WCOL]),
                                                    ALU.subtract).then_inc(s["kw"], 1)
                            dve.wait_ge(s["kw"], g + 1)
                            nc.vector.tensor_scalar(KC[:, slot, :, :], KD[:, :, :], 1000.0, -1000.0, ALU.min, ALU.max).then_inc(s["keyed"], 1)
                            nc.vector.tensor_copy(KL[:, slot, :, :, :], RAW[:, slot, :, 1:3, :].rearrange("p w y c -> p y w c")).then_inc(s["keyed"], 1)
                            with dve.Fori(0, WPG // QUAD // 2) as q2:
                                for u in range(2):
                                    quad(g * (WPG // QUAD) + q2 * 2 + u, q2 * 2 + u, u, slot, g)
                        run(dve, m, windows, lambda g, slot: None)
                    else:
                        OHG = OH[:, 0, 0, 0, :, :].rearrange("p l c -> p (l c)")

                        def column(y, g, half, c, i):
                            dve.wait_ge(s["free_oh"], i + 1)
                            b0, nb = half * HALF[0], HALF[half]
                            nc.vector.tensor_scalar(KW[:, 0:1], EK[:, 0, bass.ds(c, 1)], base_w[:, bass.ds(g * WPG, 1)], None, ALU.subtract).then_inc(s["kw"], 1)
                            nc.vector.tensor_scalar(OHG[:, 0:P], iota_l[:, :, 0], EK[:, 1 + y, bass.ds(c, 1)], None, ALU.is_equal)
                            dve.wait_ge(s["kw"], i + 1)
                            nc.vector.tensor_scalar(genmv[:, 0:nb * P], iota_g[:, b0 * P:(b0 + nb) * P], KW[:, 0:1], None, ALU.is_equal).then_inc(s["onehot"], 1)
                        with dve.Fori(0, NT) as g:
                            for y in range(2):
                                for half in range(2):
                                    with dve.Fori(0, EC) as c:
                                        column(y, g, half, c, ((g * 4 + y * 2 + half) * EC + c))
                genmv = SG[:, 1, :].bitcast(F16)
                both(dve, body)
                dve.wait_ge(s["deg"], 1)
                step = Chain(dve, s["dve"])
                step(nc.vector.tensor_copy(rdeg_in[:, :], PDI[:, 0:NT]))
                step(nc.vector.tensor_tensor(rdeg_all[:, :], rdeg_in[:, :], PDO[:, 0:NT], ALU.add))
                for r in (rdeg_in, rdeg_all):
                    step(nc.vector.tensor_scalar(r[:, :], r[:, :], 1.0, None, ALU.max))
                    step(nc.vector.reciprocal(r[:, :], r[:, :]))

            @block.tensor
            def _(pe):
                def body(pe, m):
                    idm = ident16 if m.fast else ident
                    one = ones16[:, 0:1] if m.fast else ones[:, 0:1]
                    pe.sem_inc(s["free_oh"], 1)
                    pe.sem_inc(s["window"], 2 * QUAD if m.fast else 1)
                    nc.tensor.matmul(PDO[:, 0:NT], KZ[:, 0:P], KZ[:, 0:NT], start=True, stop=True)

                    def finish(g, slot):
                        _, ss, sds = rest(slot, m)
                        pe.wait_ge(s["sum"], g + 1)
                        for q in range(NBANK):
                            i = 7 * g + q
                            pe.wait_ge(s["tevac"], i + 1)
                            ts = (q + slot) % 2 if m.fast else 0
                            pt = PT[:, ts, :]
                            pt = pt.bitcast(F16) if m.fast else pt
                            nb = bank_cols(q) // P
                            for b in range(nb):
                                ins = nc.tensor.transpose(pt[:, b * P:(b + 1) * P], ss[:, (4 * q + b) * P:(4 * q + b + 1) * P], idm[:, :])
                            ins.then_inc(s["turned"], 1)
                        for b in range(NT):
                            nc.tensor.matmul(PDI[:, bass.ds(g, 1)], ss[:, b * P:(b + 1) * P], one, start=(b == 0), stop=(b == NT - 1))
                        pe.wait_ge(s["tevac"], m.slots + NBANK * (g + 1))
                        for b in range(NT):
                            ins = nc.tensor.matmul(PDO[:, b:b + 1], sds[:, b * P:(b + 1) * P], one, start=False, stop=False, skip_group_check=True)
                        ins.then_inc(s["free_st"], 1)

                    if m.fast:
                        def windows(g, slot):
                            with pe.Fori(0, WPG // QUAD // 2) as q2:
                                for u in range(2):
                                    pe.wait_ge(s["onehot"], g * (WPG // QUAD) + q2 * 2 + (u + 1))
                                    for v in range(QUAD):
                                        n = g * WPG + q2 * (2 * QUAD) + (u * QUAD + v)
                                        pe.wait_ge(s["evac"], n + 1)
                                        for y in range(2):
                                            for t in range(WCOL):
                                                ins = nc.tensor.matmul(GB[v][:, y * WCELLS:(y + 1) * WCELLS], OH[:, u, y, v, :, t], MV[:, u, v, :, t],
                                                                       start=(t == 0), stop=(t == WCOL - 1))
                                        ins.then_inc(s["window"], 1)
                    else:
                        def windows(g, slot):
                            OHG = OH[:, 0, 0, 0, :, :].rearrange("p l c -> p (l c)")
                            genmv = SG[:, 1, :].bitcast(F16)
                            for y in range(2):
                                for half in range(2):
                                    nb = HALF[half]
                                    base = (g * 4 + y * 2 + half) * EC
                                    pe.wait_ge(s["evac"], g * 4 + y * 2 + half + 1)
                                    for q in range(4):
                                        cols = min(BANK, nb * P - q * BANK)
                                        if cols > 0:
                                            nc.tensor.matmul(GB[q][:, 0:cols], KZ[:, 0:P], KZ[:, 0:cols], start=True, stop=True)
                                    with pe.Fori(0, EC) as c:
                                        pe.wait_ge(s["onehot"], base + c + 1)
                                        for q in range(4):
                                            cols = min(BANK, nb * P - q * BANK)
                                            if cols > 0:
                                                ins = nc.tensor.matmul(GB[q][:, 0:cols], OHG[:, 0:P], genmv[:, q * BANK:q * BANK + cols],
                                                                       start=False, stop=False, skip_group_check=True)
                                        ins.then_inc(s["free_oh"], 1)
                                    nc.tensor.matmul(PDI[0:1, 40:41], KZ[:, 0:1], KZ[:, 0:1], start=True, stop=True).then_inc(s["window"], 1)
                    run(pe, m, windows, finish)
                GB = [PW[:, 0, :], PW[:, 1, :], PGX[:, 0, :], PGX[:, 1, :]]
                pe.wait_ge(s["const"], 4)
                both(pe, body)
                nc.tensor.matmul(PDI[0:1, 41:42], KZ[:, 0:1], KZ[:, 0:1], start=True, stop=True).then_inc(s["deg"], 1)

            @block.scalar
            def _(act):
                def body(act, m):
                    act.sem_inc(s["evac"], m.banks)
                    act.sem_inc(s["tevac"], m.slots)

                    def finish(g, slot):
                        _, _, sds = rest(slot, m)
                        act.wait_ge(s["group"], g + 1)
                        for q in range(NBANK):
                            act.wait_ge(s["turned"], NBANK * g + q + 1)
                            ts = (q + slot) % 2 if m.fast else 0
                            pt = PT[:, ts, :]
                            pt = pt.bitcast(F16) if m.fast else pt
                            nc.scalar.activation(sds[:, q * BANK:q * BANK + bank_cols(q)], pt[:, 0:bank_cols(q)], ACT.Copy).then_inc(s["tevac"], 1)

                    if m.fast:
                        def windows(g, slot):
                            st, _, _ = rest(slot, m)
                            act.wait_ge(s["group"], g + 1)
                            with act.Fori(0, WPG // QUAD) as q:
                                for v in range(QUAD):
                                    n = g * WPG + q * QUAD + v
                                    act.wait_ge(s["window"], 2 * QUAD + n + 1)
                                    src = GB2[v][:, 0:2 * WCELLS].rearrange("p (y b d) -> p y b d", y=2, b=NT)
                                    nc.scalar.activation(st[:, :, :, bass.ds(q * (QUAD * WD) + v * WD, WD)], src, ACT.Copy).then_inc(s["evac"], 1)
                    else:
                        def windows(g, slot):
                            st, _, _ = rest(slot, m)
                            flat = st.rearrange("p y b d -> p y (b d)")
                            act.wait_ge(s["group"], g + 1)
                            for y in range(2):
                                for half in range(2):
                                    n = g * 4 + y * 2 + half
                                    act.wait_ge(s["window"], n + 2)
                                    for q in range(4):
                                        cols = min(BANK, HALF[half] * P - q * BANK)
                                        if cols > 0:
                                            at = half * HALF[0] * P + q * BANK
                                            ins = nc.scalar.activation(flat[:, y, at:at + cols], GB2[q][:, 0:cols], ACT.Copy)
                                    ins.then_inc(s["evac"], 1)
                    run(act, m, windows, finish)
                GB2 = [PW[:, 0, :], PW[:, 1, :], PGX[:, 0, :], PGX[:, 1, :]]
                both(act, body)

            @block.sync
            def _(sp):
                def body(sp, m):
                    sp.sem_inc(s["group"], m.slots)

                    def finish(g, slot):
                        st, ss, sds = rest(slot, m)
                        sp.wait_ge(s["sum"], g + 1)
                        cols = bass.ds(g * P, P)
                        for y, what in enumerate(("t0", "t1")):
                            sp.dma_start(adj[m, what][:, cols].rearrange("(b p) d -> p b d", p=P), st[:, y, :, :]).then_inc(s["st_out0"], 16)
                        sp.dma_start(adj[m, "sd"][:, cols].rearrange("(b p) d -> p b d", p=P), ss.rearrange("p (b d) -> p b d", b=NT)).then_inc(s["st_out0"], 16)
                        sp.wait_ge(s["tevac"], m.slots + NBANK * (g + 1))
                        sp.dma_start(adj[m, "ds"][bass.ds(g * P, P), :], sds).then_inc(s["st_out0"], 16)
                        sp.wait_ge(s["st_out0"], 64 * (g + 1))
                        sp.wait_ge(s["free_st"], g + 1)
                        sp.sem_inc(s["group"], 1)
                    run(sp, m, lambda g, slot: None, finish)
                both(sp, body)
    edges.close()
    H = sb(hidden, "H", [P, NT, D])
    HT = sb(hidden, "HT", [P, NPAD])

    def inner(v, k):
        return v.unsqueeze(2).to_broadcast([P, v.shape[1], k])

    def outer(v, n):
        return v.unsqueeze(1).to_broadcast([P, n, v.shape[1]])

    flat = "p t d -> p (t d)"

    CK = NT // GROUPS
    HSCALE = 2048.0

    def chunk_of(v, c):
        return v[:, c * CK:(c + 1) * CK, :]

    norm = {k: sem(f"norm_{k}") for k in ("sums", "mean", "centred", "squared", "vars", "deviation", "h")}

    def norm_vector(dve, r, T1, T2, mu, var, std):
        for c in range(GROUPS):
            nc.vector.reduce_sum(mu[:, c * CK:(c + 1) * CK], chunk_of(X, c), axis=AX.X).then_inc(norm["sums"], 1)
        dve.wait_ge(norm["sums"], (r + 1) * GROUPS)
        nc.vector.tensor_scalar(mu[:, :], mu[:, :], -1.0 / D, None, ALU.mult).then_inc(norm["mean"], 1)
        dve.wait_ge(norm["mean"], 2 * r + 1)
        for c in range(GROUPS):
            nc.vector.tensor_tensor(chunk_of(T1, c), chunk_of(X, c), inner(mu[:, c * CK:(c + 1) * CK], D), ALU.add).then_inc(norm["centred"], 1)
        for c in range(GROUPS):
            dve.wait_ge(norm["squared"], r * GROUPS + c + 1)
            nc.vector.reduce_sum(var[:, c * CK:(c + 1) * CK], chunk_of(T2, c), axis=AX.X).then_inc(norm["vars"], 1)
        dve.wait_ge(norm["deviation"], r + 1)
        nc.vector.reciprocal(std[:, :], std[:, :]).then_inc(norm["mean"], 1)
        dve.wait_ge(norm["mean"], 2 * r + 2)
        for c in range(GROUPS):
            nc.vector.scalar_tensor_tensor(out=chunk_of(H, c), in0=chunk_of(T1, c), scalar=0.0, in1=inner(std[:, c * CK:(c + 1) * CK], D),
                                           op0=ALU.max, op1=ALU.mult).then_inc(norm["h"], 1)

    def norm_scalar(act, r, T1, T2, var, std):
        for c in range(GROUPS):
            act.wait_ge(norm["centred"], r * GROUPS + c + 1)
            nc.scalar.activation(chunk_of(T2, c), chunk_of(T1, c), ACT.Square).then_inc(norm["squared"], 1)
        act.wait_ge(norm["vars"], (r + 1) * GROUPS)
        nc.scalar.activation(std[:, :], var[:, :], ACT.Sqrt, bias=small[:, 0:1], scale=1.0 / D).then_inc(norm["deviation"], 1)

    with ExitStack() as ctx:
        HS = sb(ctx, "HS", [P, 2 * NPAD])
        AB = sb(ctx, "AB", [P, 3, NPAD])
        AG = sb(ctx, "AG", [P, NPAD])
        T1 = sb(ctx, "T1", [P, NT, D])
        T2 = sb(ctx, "T2", [P, NT, D])
        mu = sb(ctx, "mu", [P, NT])
        var = sb(ctx, "var", [P, NT])
        std = sb(ctx, "std", [P, NT])
        reach = sb(ctx, "reach", [P, 4])
        SC = sb(ctx, "SC", [P, 2])
        PA = pb(ctx, "PA", [P, NBANK, BANK])
        PZ = pb(ctx, "PZ", [P, BANK])
        PF = PA[:, :, :].rearrange("p b n -> p (b n)")
        parts = HS[:, :].bitcast(F16).rearrange("p (y k n) -> p y k n", y=2, k=2)
        whole = HS[:, :].rearrange("p (y n) -> p y n", y=2)
        SET = 3 * BANK

        def layer(name, r, sources, kind):
            typed = kind == "typed"
            ranging = typed or r is None
            summands = (T1, T2) if typed else (H,)
            ny = len(summands)
            w_self, w_neigh, b_own = {"relu": ("L0_gnn_W_self1", "L0_gnn_W_neigh1", "L0_gnn_b1"), "sage": ("L0_gnn_W_self2", "L0_gnn_W_neigh2", "L0_gnn_b2"),
                                      "normed": ("L1_gnn_W_self", "L1_gnn_W_neigh", None), "typed": ("L2_gnn_W_self", None, "L2_gnn_b_self")}[kind]
            loaded = [sem(f"{name}_loaded{i}") for i in range(3)]
            turned, moved, scaled, hi, ready, used, summed, staged, dense, share, own, sd = (
                sem(f"{name}_{k}") for k in ("turned", "moved", "scaled", "hi", "ready", "used", "summed", "staged", "dense", "share", "own", "vector"))
            if typed:
                mapped, biased = sem(f"{name}_mapped"), sem(f"{name}_biased")
            else:
                free = sem(f"{name}_free")
            if ranging:
                reached, everywhere = sem(f"{name}_reached"), sem(f"{name}_everywhere")
            total = NT * len(sources)

            def cols(v, c):
                return v[:, c * CK * P:(c + 1) * CK * P]

            def flat_of(v, c):
                return chunk_of(v, c).rearrange("p t d -> p (t d)")

            def steps(eng, one, before_loop=lambda: None):
                for i, _ in enumerate(sources):
                    at = NT * i
                    for k in range(3):
                        one(i, k, at + k, (at + k) % 3, (at + k) // 3 + 1)
                    if i == 0:
                        before_loop()
                    with eng.Fori(0, (NT - 4) // 3) as j:
                        for u in range(3):
                            one(i, j * 3 + (3 + u), j * 3 + (at + 3 + u), (at + 3 + u) % 3, j + ((at + 3 + u) // 3 + 1))
                    one(i, NT - 1, at + NT - 1, (at + NT - 1) % 3, (at + NT - 1) // 3 + 1)

            def groups(eng, one):
                one(0, 0)
                with eng.Fori(0, (GROUPS - 1) // 2) as j:
                    one(j * 2 + 1, 1)
                    one(j * 2 + 2, 0)

            def results(u, part):
                return PF[:, u * SET:u * SET + CK * 2 * D].rearrange("p (t k) -> p t k", k=2 * D)[:, :, part * D:(part + 1) * D]

            with nc.Block() as block:
                @block.sync
                def _(sp):
                    def body(sp, m):
                        def one(i, k, index, slot, _):
                            if not isinstance(index, int) or index >= 3:
                                sp.wait_ge(used, index - 2)
                            sp.dma_start(m.view(AB[:, slot, :]), adj[m, sources[i][0]][bass.ds(k * P, P), :]).then_inc(loaded[slot], 16)
                        steps(sp, one)
                    both(sp, body)

                if ranging:
                    @block.gpsimd
                    def _(pool):
                        pool.wait_ge(reached, ny)
                        nc.gpsimd.partition_all_reduce(reach[:, 2:2 + ny], reach[:, 0:ny], P, bass.bass_isa.ReduceOp.max).then_inc(everywhere, 1)

                @block.vector
                def _(dve):
                    if r is not None:
                        norm_vector(dve, r, T1, T2, mu, var, std)
                    if typed:
                        dve.wait_ge(norm["h"], (r + 1) * GROUPS)
                        for y, b in enumerate(("L2_gnn_b_data", "L2_gnn_b_control")):
                            for c in range(GROUPS):
                                dve.wait_ge(mapped, y * GROUPS + c + 1)
                                nc.vector.tensor_tensor(chunk_of(summands[y], c), results((y * GROUPS + c) % 2, 0), outer(b_of[b], CK), ALU.add).then_inc(biased, 1)
                        dve.wait_ge(biased, 2 * GROUPS)
                    if ranging:
                        for y, v in enumerate(summands):
                            nc.vector.tensor_reduce(reach[:, y:y + 1], v[:, :, :].rearrange("p t d -> p (t d)"), axis=AX.X, op=ALU.max,
                                                    apply_absolute_value=True).then_inc(reached, 1)
                    n = 0

                    def step(ins):
                        nonlocal n
                        n += 1
                        ins.then_inc(sd, 1)
                        dve.wait_ge(sd, n)
                    if ranging:
                        dve.wait_ge(everywhere, 1)
                        step(nc.vector.tensor_tensor(reach[:, 0:1], reach[:, 2:3], reach[:, 1 + ny:2 + ny], ALU.max))
                        step(nc.vector.tensor_scalar(reach[:, 1:2], reach[:, 0:1], 1e-30, None, ALU.max))
                        step(nc.vector.tensor_scalar(reach[:, 2:3].bitcast(I32), reach[:, 1:2].bitcast(I32), 0x7F800000, None, ALU.bitwise_and))
                        step(nc.vector.tensor_scalar(SC[:, 1:2], reach[:, 2:3], 1.0 / 8192.0, None, ALU.mult))
                        step(nc.vector.reciprocal(SC[:, 0:1], SC[:, 1:2]))
                    else:
                        step(nc.vector.memset(SC[:, 0:1], HSCALE))
                        step(nc.vector.memset(SC[:, 1:2], 1.0 / HSCALE))
                    n_scaled = n

                    def body(dve, m):
                        if m.fast:
                            dve.sem_inc(scaled, 1)
                            for y, v in enumerate(summands):
                                for c in range(GROUPS):
                                    dve.wait_ge(hi, y * GROUPS + c + 1)
                                    nc.vector.scalar_tensor_tensor(out=cols(parts[:, y, 1, :], c), in0=flat_of(v, c), scalar=SC[:, 0:1],
                                                                   in1=cols(parts[:, y, 0, :], c), op0=ALU.mult, op1=ALU.subtract).then_inc(ready, 1)
                        else:
                            nc.vector.memset(SC[:, :], 1.0).then_inc(scaled, 1)
                            if r is not None:
                                dve.wait_ge(norm["h"], (r + 1) * GROUPS)
                            for y, v in enumerate(summands):
                                for c in range(GROUPS):
                                    nc.vector.tensor_copy(cols(whole[:, y, :], c), flat_of(v, c)).then_inc(ready, 1)
                    both(dve, body)
                    dve.wait_ge(summed, 1)
                    dve.wait_ge(scaled, 1)
                    for b in range(3):
                        ins = nc.vector.tensor_scalar(AG[:, b * BANK:(b + 1) * BANK], PA[:, b, :], SC[:, 1:2], None, ALU.mult)
                    ins.then_inc(staged, 1)
                    per = {"relu": 0, "sage": 1, "normed": 2, "typed": 0}[kind]

                    def one(g, u):
                        tiles = bass.ds(g * CK, CK)
                        t1, t2 = T1[:, u * CK:(u + 1) * CK, :], T2[:, u * CK:(u + 1) * CK, :]
                        at = 0

                        def then(ins):
                            nonlocal at
                            at += 1
                            ins.then_inc(sd, 1)
                            dve.wait_ge(sd, g * per + (n_scaled + at))
                        if typed:
                            dve.wait_ge(share, g + 1)
                            nc.vector.tensor_tensor(X[:, tiles, :], X[:, tiles, :], t1, ALU.add).then_inc(own, 1)
                            return
                        dve.wait_ge(share, g + 1)
                        if kind == "normed":
                            then(nc.vector.scalar_tensor_tensor(out=t2, in0=t1, scalar=SLOPE, in1=t1, op0=ALU.mult, op1=ALU.max))
                            nc.vector.tensor_tensor(t1, t2, results(u, 0), ALU.add).then_inc(free, 1)
                            then(nc.vector.tensor_copy(var[:, 0:1], mu[:, 0:1]))
                            dve.wait_ge(free, g + 2)
                            nc.vector.scalar_tensor_tensor(out=H[:, tiles, :], in0=t1, scalar=SLOPE, in1=t1, op0=ALU.mult, op1=ALU.max).then_inc(own, 1)
                        else:
                            nc.vector.tensor_tensor(t2, t1, results(u, 0), ALU.add).then_inc(free, 1)
                            if kind == "sage":
                                dve.wait_ge(free, g + 2)
                                then(nc.vector.tensor_tensor(X[:, tiles, :], X[:, tiles, :], t2, ALU.add))
                    if not typed:
                        dve.sem_inc(free, 1)
                    groups(dve, one)
                    if kind == "normed":
                        n = n_scaled + per * GROUPS
                        dve.wait_ge(own, GROUPS + 1)
                        step(nc.vector.reduce_sum(mu[:, :], T1[:, :, :], axis=AX.X))
                        nc.vector.tensor_scalar(var[:, :], mu[:, :], EPS_NORM * EPS_NORM, None, ALU.max).then_inc(own, 1)
                        dve.wait_ge(own, GROUPS + 3)
                        step(nc.vector.reciprocal(std[:, :], std[:, :]))
                        step(nc.vector.tensor_tensor(T2[:, :, :], H[:, :, :], inner(std[:, :], D), ALU.mult))
                        step(nc.vector.tensor_tensor(X[:, :, :], X[:, :, :], T2[:, :, :], ALU.add))

                @block.scalar
                def _(act):
                    if r is not None:
                        norm_scalar(act, r, T1, T2, var, std)

                    def turned_out(c):
                        act.wait_ge(turned, c + 1)
                        nc.scalar.activation(cols(HT, c), PF[:, (c % 3) * 2 * BANK:(c % 3) * 2 * BANK + CK * P], ACT.Copy).then_inc(moved, 1)
                    if typed:
                        for c in range(GROUPS):
                            turned_out(c)

                    def body(act, m):
                        if m.fast:
                            act.wait_ge(scaled, 1)
                        for y, v in enumerate(summands):
                            for c in range(GROUPS):
                                if m.fast:
                                    if r is not None and not typed:
                                        act.wait_ge(norm["h"], r * GROUPS + c + 1)
                                    nc.scalar.activation(cols(parts[:, y, 0, :], c), flat_of(v, c), ACT.Copy, scale=SC[:, 0:1]).then_inc(hi, 1)
                                if not typed:
                                    turned_out(c)
                    both(act, body)
                    act.wait_ge(summed, 1)
                    act.wait_ge(scaled, 1)
                    for b in range(3, NBANK):
                        ins = nc.scalar.activation(AG[:, b * BANK:b * BANK + bank_cols(b)], PA[:, b, 0:bank_cols(b)], ACT.Copy, scale=SC[:, 1:2])
                    ins.then_inc(staged, 1)

                    def one(g, u):
                        tiles = bass.ds(g * CK, CK)
                        t1 = T1[:, u * CK:(u + 1) * CK, :]
                        act.wait_ge(dense, g + 1)
                        if typed:
                            act.wait_ge(own, g + 1)
                            nc.scalar.activation(t1, results(u, 0), ACT.Relu).then_inc(share, 1)
                            return
                        if kind != "relu":
                            act.wait_ge(free, g + 1)
                        rdeg = rdeg_all if kind == "normed" else rdeg_in
                        for i in range(CK):
                            ins = nc.scalar.activation(T1[:, u * CK + i, :], results(u, 1)[:, i, :], ACT.Copy, scale=rdeg[:, bass.ds(g * CK + i, 1)])
                        ins.then_inc(share, 1)
                        if kind == "relu":
                            act.wait_ge(free, g + 2)
                            nc.scalar.activation(H[:, tiles, :], T2[:, u * CK:(u + 1) * CK, :], ACT.Relu).then_inc(own, 1)
                    if typed:
                        act.sem_inc(own, 2)
                    groups(act, one)
                    if kind == "normed":
                        act.wait_ge(own, GROUPS)
                        nc.scalar.activation(T1[:, :, :], H[:, :, :], ACT.Square).then_inc(own, 1)
                        act.wait_ge(own, GROUPS + 2)
                        nc.scalar.activation(std[:, :], var[:, :], ACT.Sqrt).then_inc(own, 1)

                @block.tensor
                def _(pe):
                    for c in range(GROUPS):
                        if r is not None:
                            pe.wait_ge(norm["h"], r * GROUPS + c + 1)
                        if c >= 3:
                            pe.wait_ge(moved, c - 2)
                        for i in range(CK):
                            ins = nc.tensor.transpose(PF[:, (c % 3) * 2 * BANK + i * P:(c % 3) * 2 * BANK + (i + 1) * P], H[:, c * CK + i, :], ident[:, :])
                        ins.then_inc(turned, 1)
                    pe.wait_ge(moved, GROUPS)
                    if typed:
                        for y, w in enumerate(("L2_gnn_W_data", "L2_gnn_W_control")):
                            for c in range(GROUPS):
                                u = (y * GROUPS + c) % 2
                                if y * GROUPS + c >= 2:
                                    pe.wait_ge(biased, y * GROUPS + c - 1)
                                for i in range(CK):
                                    t = c * CK + i
                                    ins = nc.tensor.matmul(PF[:, u * SET + i * 2 * D:u * SET + i * 2 * D + D],
                                                           HT[:, t * P:(t + 1) * P], w_of[w], start=True, stop=True)
                                ins.then_inc(mapped, 1)
                        pe.wait_ge(biased, 2 * GROUPS)

                    def body(pe, m):
                        pe.wait_ge(ready, 1)

                        def one(i, k, index, slot, count):
                            pe.wait_ge(loaded[slot], count * 16)
                            rows = m.view(AB[:, slot, :])
                            y = sources[i][1]
                            for part in range(m.parts):
                                src = parts[:, y, part, :] if m.fast else whole[:, y, :]
                                first = isinstance(index, int) and index == 0 and part == 0
                                last = isinstance(index, int) and index == total - 1 and part == m.parts - 1
                                for b in range(NBANK):
                                    ins = nc.tensor.matmul(PA[:, b, 0:bank_cols(b)], src[:, bass.ds(k * P, P)], rows[:, b * BANK:b * BANK + bank_cols(b)],
                                                           start=first, stop=last)
                            ins.then_inc(used, 1)
                        if m.fast:
                            steps(pe, one, lambda: pe.wait_ge(ready, GROUPS * ny))
                        else:
                            pe.wait_ge(ready, GROUPS * ny)
                            for i in range(len(sources)):
                                for k in range(NT):
                                    index = i * NT + k
                                    one(i, k, index, index % 3, index // 3 + 1)
                    both(pe, body)
                    nc.tensor.matmul(PZ[0:1, 0:1], ident16[:, 0:1], ident16[:, 0:1], start=True, stop=True).then_inc(summed, 1)
                    pe.wait_ge(staged, 2)
                    for g in range(GROUPS):
                        u = g % 2
                        if g >= 2:
                            if typed:
                                pe.wait_ge(share, g - 1)
                            else:
                                pe.wait_ge(free, g)
                        for i in range(CK):
                            at = slice((g * CK + i) * P, (g * CK + i + 1) * P)
                            mine = PF[:, u * SET + i * 2 * D:u * SET + i * 2 * D + D]
                            neigh = PF[:, u * SET + i * 2 * D + D:u * SET + (i + 1) * 2 * D]
                            ins = nc.tensor.matmul(mine, HT[:, at], w_of[w_self], start=True, stop=b_own is None)
                            if typed:
                                nc.tensor.matmul(mine, AG[:, at], ident[:, :], start=False, stop=False)
                            if b_own:
                                ins = nc.tensor.matmul(mine, ones[0:1, :], b_of[b_own][0:1, :], start=False, stop=True)
                            if not typed:
                                ins = nc.tensor.matmul(neigh, AG[:, at], w_of[w_neigh], start=True, stop=True)
                        ins.then_inc(dense, 1)

        layer("L0a", 0, [("sd", 0)], "relu")
        layer("L0b", None, [("sd", 0)], "sage")
        layer("L1", 1, [("sd", 0), ("ds", 0)], "normed")
        layer("L2", 2, [("t0", 0), ("t1", 1)], "typed")


    WAYS = ({"w": "L3_gnn_W1", "a": ("L3_gnn_a_src1", "L3_gnn_a_dst1"), "b": "L3_gnn_b1", "mask": "ds", "adj": "sd"},
            {"w": "L3_gnn_W2", "a": ("L3_gnn_a_src2", "L3_gnn_a_dst2"), "b": "L3_gnn_b2", "mask": "sd", "adj": "ds"})
    with ExitStack() as ctx:
        with ExitStack() as inner_ctx:
            T1 = sb(inner_ctx, "gT1", [P, NT, D])
            T2 = sb(inner_ctx, "gT2", [P, NT, D])
            mu = sb(inner_ctx, "gmu", [P, NT])
            var = sb(inner_ctx, "gvar", [P, NT])
            std = sb(inner_ctx, "gstd", [P, NT])
            PA = pb(inner_ctx, "gPA", [P, NBANK, BANK])
            sd, mapped, moved, scored, stored = (sem(f"l3_{k}") for k in ("vector", "mapped", "moved", "scored", "stored"))
            with nc.Block() as block:
                @block.vector
                def _(dve):
                    step = Chain(dve, sd)
                    norm_vector(dve, 3, T1, T2, mu, var, std)
                    dve.wait_ge(mapped, 1)
                    for q in range(3):
                        ins = nc.vector.tensor_copy(HT[:, q * BANK:(q + 1) * BANK], PA[:, q, :])
                    ins.then_inc(moved, 1)
                    nc.vector.memset(GE[:, :, :, :, CH:CH1], 1.0)
                    for w, way in enumerate(WAYS):
                        for g in range(GROUPS):
                            dve.wait_ge(mapped, 2 + w * GROUPS + g)
                            nc.vector.tensor_copy(GE[:, w, g * GROUPS:(g + 1) * GROUPS, :, 0:CH],
                                                  PA[:, 0:GROUPS, 0:D].rearrange("p t (h c) -> p t h c", c=CH)).then_inc(moved, 1)
                        dve.wait_ge(moved, 2 + (w + 1) * GROUPS)
                        for i, vec in enumerate(way["a"]):
                            av = outer(b_of[vec], NT).rearrange("p t (h c) -> p t h c", c=CH)
                            t4 = T1[:, :, :].rearrange("p t (h c) -> p t h c", c=CH)
                            step(nc.vector.tensor_tensor(t4, GE[:, w, :, :, 0:CH], av, ALU.mult))
                            step(nc.vector.reduce_sum(ES[:, w, i, :, :].rearrange("p h t -> p t h"), t4, axis=AX.X))
                    step(nc.vector.tensor_scalar(ES2[:, :, :, :], ES[:, :, 0, :, :], SLOPE, None, ALU.mult))
                    nc.vector.memset(mu[:, :], 0.0).then_inc(scored, 1)
                    for w in range(2):
                        dve.wait_ge(mapped, 2 + 2 * GROUPS + w)
                        nc.vector.tensor_copy(rows[0:HEADS * NT, w, :], PA[0:HEADS * NT, w, 0:P]).then_inc(scored, 1)

                @block.scalar
                def _(act):
                    norm_scalar(act, 3, T1, T2, var, std)
                    act.wait_ge(mapped, 1)
                    for q in range(3, NBANK):
                        ins = nc.scalar.activation(HT[:, q * BANK:q * BANK + bank_cols(q)], PA[:, q, 0:bank_cols(q)], ACT.Copy)
                    ins.then_inc(moved, 1)

                @block.tensor
                def _(pe):
                    pe.wait_ge(norm["h"], 4 * GROUPS)
                    for t in range(NT):
                        ins = nc.tensor.transpose(PA[:, t // 4, (t % 4) * P:(t % 4 + 1) * P], H[:, t, :], ident[:, :])
                    ins.then_inc(mapped, 1)
                    for w, way in enumerate(WAYS):
                        for g in range(GROUPS):
                            pe.wait_ge(moved, 2 + w * GROUPS + g)
                            for i in range(GROUPS):
                                t = g * GROUPS + i
                                ins = nc.tensor.matmul(PA[:, i, 0:D], HT[:, t * P:(t + 1) * P], w_of[way["w"]], start=True, stop=True)
                            ins.then_inc(mapped, 1)
                    pe.wait_ge(scored, 1)
                    for w in range(2):
                        nc.tensor.transpose(PA[0:HEADS * NT, w, 0:P], ES[:, w, 0, :, :].rearrange("p h t -> p (h t)"), ident[:, :]).then_inc(mapped, 1)

                @block.sync
                def _(sp):
                    for w in range(2):
                        sp.wait_ge(scored, 2 + w)
                        sp.dma_start(rows_dram[w].rearrange("h (t q) -> (h t) q", q=P), rows[0:HEADS * NT, w, :]).then_inc(stored, 16)
                    sp.wait_ge(stored, 32)

        hidden.close()

        with ExitStack() as inner_ctx:
            ESB = sb(inner_ctx, "ESB", [P, HEADS, NPAD])
            MB = sb(inner_ctx, "MB", [P, 2, NPAD])
            FAR = sb(inner_ctx, "FAR", [P, 2, NPAD], BF16)
            junk = sb(inner_ctx, "mjunk", [P, HEADS, NPAD], BF16)
            mt = sb(inner_ctx, "mt", [P, 2, HEADS])
            bigc = sb(inner_ctx, "bigc", [P, 1])
            loaded = [sem(f"m_loaded{i}") for i in range(2)]
            rowed, far, maxed, copied, setup = (sem(f"m_{k}") for k in ("rows", "far", "maxed", "copied", "setup"))
            with nc.Block() as block:
                def blocks(eng, one):
                    for w in range(2):
                        base = w * NT
                        one(w, 0, base, base % 2, base // 2 + 1)
                        with eng.Fori(0, (NT - 1) // 2) as j:
                            for u in (1, 2):
                                one(w, j * 2 + u, j * 2 + (base + u), (base + u) % 2, j + ((base + u) // 2 + 1))

                @block.sync
                def _(sp):

                    def body(sp, m):
                        def one(w, j, n, slot, count):
                            if isinstance(j, int):
                                for h in range(HEADS):
                                    if w:
                                        sp.wait_ge(maxed, (NT - 1) * HEADS + h + 1)
                                    sp.dma_start(ESB[:, h, :], rows_dram[w, h].partition_broadcast(P)).then_inc(rowed, 16)
                            sp.wait_ge(far, n + 1)
                            sp.dma_start(m.view(MB[:, slot, :]), adj[m, WAYS[w]["mask"]][bass.ds(j * P, P), :]).then_inc(loaded[slot], 16)
                        blocks(sp, one)
                    both(sp, body)

                @block.scalar
                def _(act):
                    act.sem_inc(far, 2)
                    act.wait_ge(setup, 1)

                    def body(act, m):
                        def one(w, j, n, slot, count):
                            act.wait_ge(loaded[slot], count * 16)
                            act.wait_ge(copied, n + 1)
                            nc.scalar.activation(FAR[:, slot, :], m.view(MB[:, slot, :]), ACT.Relu, bias=bigc[:, 0:1], scale=-BIG).then_inc(far, 1)
                        blocks(act, one)
                    both(act, body)

                @block.vector
                def _(dve):
                    nc.vector.memset(bigc[:, :], BIG).then_inc(setup, 1)
                    dve.sem_inc(copied, 2)

                    def keep(w, j, n, slot):
                        dve.wait_ge(maxed, n * HEADS + HEADS)
                        nc.vector.tensor_copy(MX[:, w, :, bass.ds(j, 1)], mt[:, slot, :].unsqueeze(2)).then_inc(copied, 1)

                    def one(w, j, n, slot, count):
                        if not isinstance(j, int):
                            dve.wait_ge(far, n + 3)
                            keep(w, j - 1, n - 1, 1 - slot)
                        else:
                            if w:
                                keep(0, NT - 1, NT - 1, 1 - slot)
                            dve.wait_ge(far, n + 3)
                            dve.wait_ge(rowed, (w + 1) * 16 * HEADS)
                        for h in range(HEADS):
                            nc.vector.tensor_tensor_reduce(out=junk[:, h, :], in0=ESB[:, h, :], in1=FAR[:, slot, :], scale=1.0,
                                                           scalar=-3.0e38, op0=ALU.subtract, op1=ALU.max, accum_out=mt[:, slot, h:h + 1]).then_inc(maxed, 1)
                    blocks(dve, one)
                    keep(1, NT - 1, 2 * NT - 1, (2 * NT - 1) % 2)

        with ExitStack() as inner_ctx:
            Z1 = sb(inner_ctx, "Z1", [P, 2, HEADS, NT])
            Z2 = sb(inner_ctx, "Z2", [P, 2, HEADS, NT])
            Z3 = sb(inner_ctx, "Z3", [P, 2, HEADS, NT])
            PT = pb(inner_ctx, "ePT", [P, 6, BANK])
            reach = sb(inner_ctx, "ereach", [P, 4])
            within = sb(inner_ctx, "ewithin", [1, 4])
            sd, own, turned, moved, stored = (sem(f"e_{k}") for k in ("vector", "own", "turned", "moved", "stored"))
            reached, everywhere = sem("e_reached"), sem("e_everywhere")
            with nc.Block() as block:
                @block.vector
                def _(dve):
                    step = Chain(dve, sd)
                    nc.vector.tensor_reduce(reach[:, 0:1], ES[:, :, 0, :, :], axis=AX.XYZ, op=ALU.max, apply_absolute_value=True).then_inc(reached, 1)
                    nc.vector.tensor_reduce(reach[:, 1:2], GE[:, :, :, :, :].rearrange("p w t h c -> p (w t h c)"), axis=AX.X, op=ALU.max,
                                            apply_absolute_value=True).then_inc(reached, 1)
                    src, dst = ES[:, :, 0, :, :], ES[:, :, 1, :, :]
                    step(nc.vector.tensor_tensor(Z1[:, :, :, :], MX[:, :, :, :], src, ALU.max))
                    step(nc.vector.tensor_tensor(Z1[:, :, :, :], Z1[:, :, :, :], dst, ALU.add))
                    step(nc.vector.tensor_scalar(Z2[:, :, :, :], Z1[:, :, :, :], SLOPE, None, ALU.mult))
                    step(nc.vector.tensor_tensor(Z1[:, :, :, :], Z1[:, :, :, :], Z2[:, :, :, :], ALU.max))
                    step(nc.vector.tensor_tensor(EM[:, :, 0, :, :], dst, Z1[:, :, :, :], ALU.subtract))
                    step(nc.vector.tensor_scalar(Z2[:, :, :, :], dst, SLOPE, None, ALU.mult))
                    step(nc.vector.tensor_tensor(EM[:, :, 1, :, :], Z2[:, :, :, :], Z1[:, :, :, :], ALU.subtract))
                    step(nc.vector.tensor_tensor(Z2[:, :, :, :], src, dst, ALU.add))
                    step(nc.vector.tensor_scalar(Z3[:, :, :, :], Z2[:, :, :, :], SLOPE, None, ALU.mult))
                    step(nc.vector.tensor_tensor(Z2[:, :, :, :], Z2[:, :, :, :], Z3[:, :, :, :], ALU.max))
                    step(nc.vector.tensor_tensor(Z2[:, :, :, :], Z2[:, :, :, :], Z1[:, :, :, :], ALU.subtract))
                    dve.wait_ge(everywhere, 1)
                    step(nc.vector.tensor_scalar(within[:, 0:1], reach[0:1, 2:3], MILD_SCORE, None, ALU.is_le))
                    step(nc.vector.tensor_scalar(within[:, 1:2], reach[0:1, 3:4], MILD_FEATURE, None, ALU.is_le))
                    step(nc.vector.tensor_copy(within[:, 2:3], flag[:, :]))
                    step(nc.vector.tensor_tensor(within[:, 3:4], within[:, 0:1], within[:, 1:2], ALU.mult))
                    step(nc.vector.tensor_tensor(path[:, MILD:MILD + 1], within[:, 2:3], within[:, 3:4], ALU.mult))
                    step(nc.vector.tensor_tensor(within[:, 0:1], within[:, 2:3], within[:, 3:4], ALU.mult))
                    step(nc.vector.tensor_tensor(path[:, HARSH:HARSH + 1], within[:, 2:3], within[:, 0:1], ALU.subtract))
                    step(nc.vector.tensor_scalar(path[:, ANY_EDGES:ANY_EDGES + 1], within[:, 2:3], -1.0, 1.0, ALU.mult, ALU.add))
                    step(nc.vector.tensor_scalar(path[:, NOT_MILD:NOT_MILD + 1], within[:, 0:1], -1.0, 1.0, ALU.mult, ALU.add))
                    for i in range(6):
                        dve.wait_ge(turned, i + 1)
                        nc.vector.tensor_copy(rows[0:HEADS * NT, i, :], PT[0:HEADS * NT, i, 0:P]).then_inc(moved, 1)

                @block.gpsimd
                def _(pool):
                    pool.wait_ge(reached, 2)
                    nc.gpsimd.partition_all_reduce(reach[:, 2:4], reach[:, 0:2], P, bass.bass_isa.ReduceOp.max).then_inc(everywhere, 1)

                @block.scalar
                def _(act):
                    act.wait_ge(sd, 11)
                    for w in range(2):
                        nc.scalar.activation(XS[:, w, :, :].rearrange("p t h -> p h t"), Z2[:, w, :, :], ACT.Exp).then_inc(own, 1)

                @block.tensor
                def _(pe):
                    pe.wait_ge(sd, 7)
                    for i in range(6):
                        what = EM[:, i // 2, i % 2, :, :] if i < 4 else ES[:, i - 4, 1, :, :]
                        nc.tensor.transpose(PT[0:HEADS * NT, i, 0:P], what.rearrange("p h t -> p (h t)"), ident[:, :]).then_inc(turned, 1)

                @block.sync
                def _(sp):
                    for i in range(6):
                        sp.wait_ge(moved, i + 1)
                        sp.dma_start(rows_dram[2 + i].rearrange("h (t q) -> (h t) q", q=P), rows[0:HEADS * NT, i, :]).then_inc(stored, 16)
                    sp.wait_ge(stored, 96)

        with ExitStack() as inner_ctx:
            SLOTS = 5
            ROUNDS = NT // SLOTS
            C2 = 2 * CH1
            ROW = HEADS * C2 + HEADS * CH1
            AROW = sb(inner_ctx, "AROW", [P, 2, HEADS, CHUNK])
            AC = sb(inner_ctx, "fAC", [P, SLOTS, CHUNK], F16)
            MA = sb(inner_ctx, "MA", [P, SLOTS, HEADS, CHUNK], F16)
            NEG = sb(inner_ctx, "NEG", [P, 2, HEADS, NT])
            QS = sb(inner_ctx, "QS", [P, 2, 2, NT, HEADS])
            PR = sb(inner_ctx, "PR", [P, 2, 2, NT, HEADS])
            V = sb(inner_ctx, "V", [P, NT, HEADS, C2])
            VAL = sb(inner_ctx, "VAL", [P, 3, NT, HEADS, C2], BF16)
            F = sb(inner_ctx, "F", [P, 2, GROUPS, ROW])
            T3 = sb(inner_ctx, "fT3", [P, GROUPS, HEADS, CH1])
            U3 = sb(inner_ctx, "fU3", [P, GROUPS, HEADS, CH1])
            RC = sb(inner_ctx, "fRC", [P, GROUPS, HEADS])
            O = sb(inner_ctx, "fO", [P, GROUPS, D])
            KZ = sb(inner_ctx, "fKZ", [P, BANK], F16)
            PN = pb(inner_ctx, "fPN", [P, GROUPS, BANK])
            VF = VAL[:, :, :, :, :].rearrange("p a t h c -> p a (t h c)")
            VH = VAL[:, :, :, :, :].rearrange("p a t h c -> p a (t h) c")
            loaded = [sem(f"f_loaded{i}") for i in range(SLOTS)]
            rowed = [sem(f"f_rows{i}") for i in range(2)]
            zeros, factors, product, high, rest1, middle, valued, masked, weighed, staged, finished, added, sd = (
                sem(f"f_{k}") for k in ("zeros", "factors", "product", "high", "rest", "middle", "valued", "masked", "weighed", "staged", "finished", "added", "vector"))

            def chunks(eng, one, at_way=lambda w: None):
                for w in range(2):
                    at_way(w)
                    base = w * NCHUNK
                    one(w, 0, base, base % 2, base // 2 + 1)
                    with eng.Fori(0, (NCHUNK - 1) // 2) as i:
                        for u in (1, 2):
                            one(w, i * 2 + u, i * 2 + (base + u), (base + u) % 2, i + ((base + u) // 2 + 1))

            def group_of(v, g):
                return v[:, g * GROUPS:(g + 1) * GROUPS, :, :]

            with nc.Block() as block:
                @block.sync
                def _(sp):
                    def program_of(sp):
                        def chunk(w, c, n, rs, count):
                            sp.wait_ge(finished, n + 1)
                            for h in range(HEADS):
                                sp.dma_start(AROW[:, rs, h, :], rows_dram[6 + w, h, bass.ds(c * CHUNK, CHUNK)].partition_broadcast(P)).then_inc(rowed[rs], 16)
                            with sp.Fori(0, ROUNDS) as j:
                                for slot in range(SLOTS):
                                    k = j * SLOTS + slot
                                    source = adj[fast, WAYS[w]["adj"]][bass.ds(k * P, P), bass.ds(c * CHUNK, CHUNK)]
                                    sp.compute_val(source.offset * mybir.dt.size(fast.dt))
                                    sp.wait_ge(weighed, n * NT + k + 1)
                                    sp.dma_start(AC[:, slot, :], source).then_inc(loaded[slot], 16)
                        chunks(sp, chunk)
                    on_path(sp, MILD, program_of)

                @block.scalar
                def _(act):
                    def program_of(act):
                        for w in range(2):
                            for i, v in enumerate((ES[:, w, 0, :, :], ES2[:, w, :, :])):
                                nc.scalar.activation(QS[:, w, i, :, :].rearrange("p t h -> p h t"), v, ACT.Exp).then_inc(factors, 1)
                        for w in range(2):
                            for i in range(2):
                                nc.scalar.activation(PR[:, w, i, :, :].rearrange("p t h -> p h t"), EM[:, w, i, :, :], ACT.Exp).then_inc(factors, 1)

                        def parts(w):
                            if w:
                                act.wait_ge(weighed, NCHUNK * NT + SLOTS)
                            for g in range(GROUPS):
                                act.wait_ge(product, w * GROUPS + g + 1)
                                nc.scalar.activation(group_of(VAL[:, 0, :, :, :], g), group_of(V, g), ACT.Copy).then_inc(high, 1)
                            for g in range(GROUPS):
                                act.wait_ge(rest1, w * GROUPS + g + 1)
                                nc.scalar.activation(group_of(VAL[:, 1, :, :, :], g), group_of(V, g), ACT.Copy).then_inc(middle, 1)

                        def stage(w, c, n, rs, count):
                            act.wait_ge(weighed, n * NT + (NT + SLOTS))
                            act.wait_ge(finished, n + 1)
                            for t in range(GROUPS):
                                ins = nc.scalar.activation(F[:, rs, t, :], PN[:, t, 0:ROW], ACT.Copy)
                            ins.then_inc(staged, 1)
                        chunks(act, stage, parts)
                    on_path(act, MILD, program_of)

                @block.vector
                def _(dve):
                    def program_of(dve):
                        dve.sem_inc(finished, 2)
                        nc.vector.memset(KZ[:, :], 0.0).then_inc(zeros, 1)
                        nc.vector.tensor_scalar(NEG[:, :, :, :], ES[:, :, 0, :, :], -1.0, None, ALU.mult).then_inc(zeros, 1)

                        def parts(w):
                            if w:
                                dve.wait_ge(weighed, NCHUNK * NT + SLOTS)
                            dve.wait_ge(factors, 2 * w + 2)
                            for g in range(GROUPS):
                                tiles = slice(g * GROUPS, (g + 1) * GROUPS)
                                for i in range(2):
                                    ins = nc.vector.tensor_tensor(group_of(V, g)[:, :, :, i * CH1:(i + 1) * CH1], GE[:, w, tiles, :, :],
                                                                  QS[:, w, i, tiles, :].unsqueeze(3).to_broadcast([P, GROUPS, HEADS, CH1]), ALU.mult)
                                ins.then_inc(product, 1)
                            for g in range(GROUPS):
                                dve.wait_ge(high, w * GROUPS + g + 1)
                                nc.vector.tensor_tensor(group_of(V, g), group_of(V, g), group_of(VAL[:, 0, :, :, :], g), ALU.subtract).then_inc(rest1, 1)
                            for g in range(GROUPS):
                                dve.wait_ge(middle, w * GROUPS + g + 1)
                                nc.vector.tensor_tensor(group_of(VAL[:, 2, :, :, :], g), group_of(V, g), group_of(VAL[:, 1, :, :, :], g), ALU.subtract).then_inc(valued, 1)
                            if not w:
                                dve.wait_ge(factors, 8)
                                dve.wait_ge(zeros, 2)

                        def before(w, c, n):
                            return None if isinstance(c, int) else (w, c - 1, n - 1)

                        def chunk(w, c, n, rs, count):
                            def mask(k, slot, rnd):
                                dve.wait_ge(loaded[slot], (n * ROUNDS + rnd + 1) * 16)
                                for h in range(HEADS):
                                    ins = nc.vector.scalar_tensor_tensor(out=MA[:, slot, h, :], in0=AROW[:, rs, h, :], scalar=NEG[:, w, h, bass.ds(k, 1)],
                                                                         in1=AC[:, slot, :], op0=ALU.is_gt, op1=ALU.mult)
                                ins.then_inc(masked, 1)
                            dve.wait_ge(rowed[rs], count * (16 * HEADS))
                            for slot in range(SLOTS):
                                mask(slot, slot, 0)
                            if not isinstance(c, int):
                                final(w, c - 1, n - 1, 1 - rs)
                            with dve.Fori(1, ROUNDS) as j:
                                for slot in range(SLOTS):
                                    mask(j * SLOTS + slot, slot, j)
                            if isinstance(c, int) is False and rs == (w * NCHUNK + 2) % 2:
                                pass

                        def final(w, c, n, fs):
                            tiles = bass.ds(c * CT_TILES, CT_TILES)
                            at = 0

                            def then(ins):
                                nonlocal at
                                at += 1
                                ins.then_inc(sd, 1)
                                dve.wait_ge(sd, n * 7 + at)

                            def by_head(v):
                                return v.unsqueeze(3).to_broadcast([P, GROUPS, HEADS, CH1])
                            chosen = F[:, fs, :, 0:HEADS * C2].rearrange("p t (h c) -> p t h c", c=C2)
                            every = F[:, fs, :, HEADS * C2:ROW].rearrange("p t (h c) -> p t h c", c=CH1)
                            dve.wait_ge(staged, n + 1)
                            then(nc.vector.tensor_tensor(T3[:, :, :, :], every, chosen[:, :, :, CH1:C2], ALU.subtract))
                            nc.vector.tensor_tensor(U3[:, :, :, :], chosen[:, :, :, 0:CH1], by_head(PR[:, w, 0, tiles, :]), ALU.mult)
                            then(nc.vector.tensor_tensor(T3[:, :, :, :], T3[:, :, :, :], by_head(PR[:, w, 1, tiles, :]), ALU.mult))
                            then(nc.vector.tensor_tensor(T3[:, :, :, :], T3[:, :, :, :], U3[:, :, :, :], ALU.add))
                            then(nc.vector.tensor_tensor(U3[:, :, :, :], GE[:, w, tiles, :, :], by_head(XS[:, w, tiles, :]), ALU.mult))
                            then(nc.vector.tensor_tensor(T3[:, :, :, :], T3[:, :, :, :], U3[:, :, :, :], ALU.add))
                            then(nc.vector.reciprocal(RC[:, :, :], T3[:, :, :, CH]))
                            then(nc.vector.tensor_tensor(O[:, :, :].rearrange("p t (h c) -> p t h c", c=CH), T3[:, :, :, 0:CH], RC[:, :, :].unsqueeze(3).to_broadcast([P, GROUPS, HEADS, CH]), ALU.mult))
                            nc.vector.tensor_tensor(O[:, :, :], O[:, :, :], outer(b_of[WAYS[w]["b"]], GROUPS), ALU.add).then_inc(added, 1)
                            dve.wait_ge(added, n + 1)
                            nc.vector.scalar_tensor_tensor(out=X[:, tiles, :], in0=O[:, :, :], scalar=0.5, in1=X[:, tiles, :], op0=ALU.mult, op1=ALU.add).then_inc(finished, 1)

                        def way(w):
                            if w:
                                final(w - 1, NCHUNK - 1, w * NCHUNK - 1, (w * NCHUNK - 1) % 2)
                            parts(w)
                        chunks(dve, chunk, way)
                        final(1, NCHUNK - 1, 2 * NCHUNK - 1, (2 * NCHUNK - 1) % 2)
                    on_path(dve, MILD, program_of)

                @block.tensor
                def _(pe):
                    def program_of(pe):
                        pe.sem_inc(weighed, SLOTS)

                        def chunk(w, c, n, rs, count):
                            if not (isinstance(n, int) and n == 0):
                                pe.wait_ge(staged, n)
                            for t in range(GROUPS):
                                nc.tensor.matmul(PN[:, t, 0:ROW], KZ[:, 0:P], KZ[:, 0:ROW], start=True, stop=True)
                            with pe.Fori(0, ROUNDS) as j:
                                for slot in range(SLOTS):
                                    k = j * SLOTS + slot
                                    pe.wait_ge(masked, n * NT + k + 1)
                                    for t in range(GROUPS):
                                        at = slice(t * P, (t + 1) * P)
                                        for h in range(HEADS):
                                            for part in range(3):
                                                nc.tensor.matmul(PN[:, t, h * C2:(h + 1) * C2], MA[:, slot, h, at], VF[:, part, bass.ds(k * (HEADS * C2) + h * C2, C2)],
                                                                 start=False, stop=False, skip_group_check=True)
                                        for part in range(3):
                                            ins = nc.tensor.matmul(PN[:, t, HEADS * C2:ROW].rearrange("p (h c) -> p h c", c=CH1), AC[:, slot, at],
                                                                   VH[:, part, bass.ds(k * HEADS, HEADS), CH1:C2], start=False, stop=False, skip_group_check=True)
                                    ins.then_inc(weighed, 1)

                        def way(w):
                            if not w:
                                pe.wait_ge(zeros, 1)
                            pe.wait_ge(valued, (w + 1) * GROUPS)
                        chunks(pe, chunk, way)
                    on_path(pe, MILD, program_of)

        with ExitStack() as inner_ctx:
            SLOTS = 5
            ROUNDS = NT // SLOTS
            EMB = sb(inner_ctx, "EMB", [P, 2, 2, HEADS, CHUNK])
            AC = sb(inner_ctx, "AC", [P, SLOTS, CHUNK])
            Z = sb(inner_ctx, "Z", [P, SLOTS, HEADS, CHUNK])
            NUM = sb(inner_ctx, "NUM", [P, HEADS, CHUNK])
            T3 = sb(inner_ctx, "T3", [P, GROUPS, HEADS, CH1])
            RC = sb(inner_ctx, "RC", [P, GROUPS, HEADS])
            O = sb(inner_ctx, "O", [P, GROUPS, D])
            PN = pb(inner_ctx, "PN", [P, 2 * HEADS, BANK])
            under, exponent, exps, weight, turned, sd = (
                sem(f"b_{k}") for k in ("under", "exponent", "exps", "weight", "turned", "vector"))

            def chunks(eng, one):
                for w in range(2):
                    base = w * NCHUNK
                    one(w, 0, base, base % 2, base // 2 + 1)
                    with eng.Fori(0, (NCHUNK - 1) // 2) as i:
                        for u in (1, 2):
                            one(w, i * 2 + u, i * 2 + (base + u), (base + u) % 2, i + ((base + u) // 2 + 1))

            def before(w, c, n):
                if isinstance(c, int):
                    return (w - 1, NCHUNK - 1, n - 1) if w else None
                return (w, c - 1, n - 1)

            def staggered(eng, front, back, between):
                front(0, 0)
                for u in range(SLOTS):
                    front(u + 1, (u + 1) % SLOTS)
                    back(u, u, 0)
                    if u == 2:
                        between()
                with eng.Fori(1, ROUNDS - 1) as j:
                    for u in range(SLOTS):
                        front(j * SLOTS + (u + 1), (u + 1) % SLOTS)
                        back(j * SLOTS + u, u, j)
                for k in range(NT - SLOTS, NT):
                    if k + 1 < NT:
                        front(k + 1, (k + 1) % SLOTS)
                    back(k, k % SLOTS, k // SLOTS)

            with nc.Block() as block:
                @block.sync
                def _(sp):
                    def program_of(sp, m):
                        def body(sp, m):
                            def chunk(w, c, n, rs, count):
                                sp.wait_ge(finished, n + 1)
                                for kind in range(2):
                                    for h in range(HEADS):
                                        sp.dma_start(EMB[:, rs, kind, h, :], rows_dram[2 + 2 * w + kind, h, bass.ds(c * CHUNK, CHUNK)].partition_broadcast(P)).then_inc(rowed[rs], 16)
                                with sp.Fori(0, ROUNDS) as j:
                                    for slot in range(SLOTS):
                                        k = j * SLOTS + slot
                                        source = adj[m, WAYS[w]["adj"]][bass.ds(k * P, P), bass.ds(c * CHUNK, CHUNK)]
                                        sp.compute_val(source.offset * mybir.dt.size(m.dt))
                                        sp.wait_ge(weight, n * NT + k + 1)
                                        a_c = AC[:, slot, :]
                                        a_c = a_c if not m.fast else a_c.bitcast(F16)[:, 0:CHUNK]
                                        sp.dma_start(a_c, source).then_inc(loaded[slot], 16)
                            chunks(sp, chunk)
                        body(sp, m)
                    on_path(sp, HARSH, lambda sp: program_of(sp, fast))
                    on_path(sp, ANY_EDGES, lambda sp: program_of(sp, general))

                @block.scalar
                def _(act):
                    def program_of(act):
                        def stage(n):
                            act.wait_ge(weighed, n * NT + (NT + SLOTS))
                            for i in range(2 * HEADS):
                                ins = nc.scalar.activation(NUM[0:CH1, i // 2, (i % 2) * MMC:(i % 2 + 1) * MMC], PN[0:CH1, i, 0:MMC], ACT.Copy)
                            ins.then_inc(staged, 1)

                        def chunk(w, c, n, rs, count):
                            def low(k, slot):
                                act.wait_ge(weighed, n * NT + k + 1)
                                for h in range(HEADS):
                                    ins = nc.scalar.activation(Z[:, slot, h, :], EMB[:, rs, 1, h, :], ACT.Identity, bias=ES2[:, w, h, bass.ds(k, 1)])
                                ins.then_inc(under, 1)

                            def exp(k, slot, rnd):
                                act.wait_ge(exponent, n * NT + k + 1)
                                nc.scalar.activation(Z[:, slot, :, :], Z[:, slot, :, :], ACT.Exp).then_inc(exps, 1)
                            act.wait_ge(rowed[rs], count * (16 * 2 * HEADS))
                            last = before(w, c, n)
                            staggered(act, low, exp, lambda: stage(last[2]) if last else None)
                        chunks(act, chunk)
                        stage(2 * NCHUNK - 1)
                    on_path(act, NOT_MILD, program_of)

                @block.vector
                def _(dve):
                    def program_of(dve, m):
                        dve.sem_inc(finished, 2)
                        dve.sem_inc(weight, SLOTS)

                        def body(dve, m):
                            def chunk(w, c, n, rs, count):
                                def top_of(k, slot):
                                    dve.wait_ge(under, n * NT + k + 1)
                                    for h in range(HEADS):
                                        ins = nc.vector.scalar_tensor_tensor(out=Z[:, slot, h, :], in0=EMB[:, rs, 0, h, :], scalar=ES[:, w, 0, h, bass.ds(k, 1)],
                                                                             in1=Z[:, slot, h, :], op0=ALU.add, op1=ALU.max)
                                    ins.then_inc(exponent, 1)

                                def times(k, slot, rnd):
                                    dve.wait_ge(exps, n * NT + k + 1)
                                    dve.wait_ge(loaded[slot], (n * ROUNDS + rnd + 1) * 16)
                                    a_c = AC[:, slot, :]
                                    a_c = a_c if not m.fast else a_c.bitcast(F16)[:, 0:CHUNK]
                                    nc.vector.scalar_tensor_tensor(out=Z[:, slot, :, :], in0=Z[:, slot, :, :], scalar=1.0, in1=outer(a_c, HEADS),
                                                                   op0=ALU.min, op1=ALU.mult).then_inc(weight, 1)
                                dve.wait_ge(rowed[rs], count * (16 * 2 * HEADS))
                                last = before(w, c, n)
                                staggered(dve, top_of, times, lambda: final(*last) if last else None)

                            def final(w, c, n):
                                tiles = bass.ds(c * CT_TILES, CT_TILES)
                                nc.vector.tensor_tensor(T3[:, :, :, :], GE[:, w, tiles, :, :], XS[:, w, tiles, :].unsqueeze(3).to_broadcast([P, GROUPS, HEADS, CH1]), ALU.mult).then_inc(sd, 1)
                                dve.wait_ge(sd, n * 5 + 1)
                                dve.wait_ge(turned, n + 1)
                                nc.vector.tensor_tensor(T3[:, :, :, :], PN[:, 0:GROUPS, 0:HEADS * CH1].rearrange("p t (h c) -> p t h c", c=CH1), T3[:, :, :, :], ALU.add).then_inc(sd, 1)
                                dve.wait_ge(sd, n * 5 + 2)
                                nc.vector.reciprocal(RC[:, :, :], T3[:, :, :, CH]).then_inc(sd, 1)
                                dve.wait_ge(sd, n * 5 + 3)
                                nc.vector.tensor_tensor(O[:, :, :].rearrange("p t (h c) -> p t h c", c=CH), T3[:, :, :, 0:CH], RC[:, :, :].unsqueeze(3).to_broadcast([P, GROUPS, HEADS, CH]), ALU.mult).then_inc(sd, 1)
                                dve.wait_ge(sd, n * 5 + 4)
                                nc.vector.tensor_tensor(O[:, :, :], O[:, :, :], outer(b_of[WAYS[w]["b"]], GROUPS), ALU.add).then_inc(sd, 1)
                                dve.wait_ge(sd, n * 5 + 5)
                                nc.vector.scalar_tensor_tensor(out=X[:, tiles, :], in0=O[:, :, :], scalar=0.5, in1=X[:, tiles, :], op0=ALU.mult, op1=ALU.add).then_inc(finished, 1)
                            chunks(dve, chunk)
                            final(1, NCHUNK - 1, 2 * NCHUNK - 1)
                        body(dve, m)
                    on_path(dve, HARSH, lambda dve: program_of(dve, fast))
                    on_path(dve, ANY_EDGES, lambda dve: program_of(dve, general))

                @block.tensor
                def _(pe):
                    def program_of(pe):
                        pe.sem_inc(weighed, SLOTS)

                        def chunk(w, c, n, rs, count):
                            pe.wait_ge(finished, n + 2)
                            for k in range(NT):
                                pe.wait_ge(weight, n * NT + k + (1 + SLOTS))
                                for h in range(HEADS):
                                    for half in range(2):
                                        ins = nc.tensor.matmul(PN[0:CH1, 2 * h + half, 0:MMC], GE[:, w, k, h, :], Z[:, k % SLOTS, h, half * MMC:(half + 1) * MMC],
                                                               start=(k == 0), stop=(k == NT - 1))
                                ins.then_inc(weighed, 1)
                            pe.wait_ge(staged, n + 1)
                            for t in range(GROUPS):
                                for h in range(HEADS):
                                    turned_to, num, unit = PN[:, t, h * CH1:(h + 1) * CH1], NUM[0:CH1, h, t * P:(t + 1) * P], ident[0:CH1, 0:CH1]
                                    if t == h == 0:
                                        nc.tensor.matmul(turned_to, num, unit, start=True, stop=True)
                                    else:
                                        ins = nc.tensor.transpose(turned_to, num, unit)
                            ins.then_inc(turned, 1)
                        chunks(pe, chunk)
                    on_path(pe, NOT_MILD, program_of)

    with ExitStack() as ctx:
        done = sem("stored")
        with nc.Block() as block:
            @block.sync
            def _(sp):
                sp.dma_start(out[0:(NT - 1) * P, :].rearrange("(t p) d -> p t d", p=P), X[:, 0:NT - 1, :]).then_inc(done, 16)
                sp.dma_start(out[(NT - 1) * P:N, :], X[0:N - (NT - 1) * P, NT - 1, :]).then_inc(done, 16)
                sp.wait_ge(done, 32)
    top.close()


_INS = ["x", "src", "dst", "edge_type_2", "L0_gnn_W_self1", "L0_gnn_W_neigh1", "L0_gnn_b1", "L0_gnn_W_self2",
        "L0_gnn_W_neigh2", "L0_gnn_b2", "L1_gnn_W_self", "L1_gnn_W_neigh", "L2_gnn_W_data", "L2_gnn_b_data",
        "L2_gnn_W_control", "L2_gnn_b_control", "L2_gnn_W_self", "L2_gnn_b_self", "L3_gnn_W1", "L3_gnn_a_src1",
        "L3_gnn_a_dst1", "L3_gnn_b1", "L3_gnn_W2", "L3_gnn_a_src2", "L3_gnn_a_dst2", "L3_gnn_b2"]


def kernel(**inputs):
    import concourse.bacc as _bacc
    from concourse.bass_utils import run_bass_kernel_spmd as _run

    nc = _bacc.Bacc("TRN2", target_bir_lowering=False, num_devices=1)
    arrays, aps = {}, {}
    for name in _INS:
        v = np.ascontiguousarray(inputs[name])
        arrays[f"in_{name}_dram"] = v
        aps[name] = nc.dram_tensor(f"in_{name}_dram", v.shape, mybir.dt.from_np(v.dtype), kind="ExternalInput").ap()
    out = nc.dram_tensor("out_0_dram", (N, D), F32, kind="ExternalOutput").ap()
    program(nc, aps, out)
    r = _run(nc, [arrays], core_ids=[0])
    return r.results[0]["out_0_dram"]
```

```python
from contextlib import ExitStack

import numpy as np
from concourse import bass, mybir

F32 = mybir.dt.float32
F16 = mybir.dt.float16
BF16 = mybir.dt.bfloat16
I32 = mybir.dt.int32
ALU = mybir.AluOpType
ACT = mybir.ActivationFunctionType
AX = mybir.AxisListType

P = 128
N = 3125
D = 128
E = 100000
NT = -(-N // P)
NPAD = NT * P
HEADS, CH = 4, 32
EPS_LN = 1e-5
EPS_NORM = 1e-12
SLOPE = 0.2
MILD_SCORE, MILD_FEATURE = 70.0, 1000.0
BIG = 1.0e30

ER = 112
ET = 7
EC = ER * ET
FULL_ROWS = E // P
REST = E - FULL_ROWS * P
LAST_ROWS = FULL_ROWS - ER * (ET - 1)
PAD_DST = 16383.0

WD = 8
WCOL = 4
WCELLS = WD * NT
QUAD = 4
WPG = P // WD
NW = NT * WPG
HALF = (16, NT - 16)

CHUNK = 640
NCHUNK = NPAD // CHUNK
CT_TILES = CHUNK // P
MMC = CHUNK // 2
BANK = 512
NBANK = -(-NPAD // BANK)
GROUPS = 5


def bank_cols(q):
    return min(BANK, NPAD - q * BANK)


class Mode:

    def __init__(self, fast):
        self.fast = fast
        self.dt = F16 if fast else F32
        self.slots = 2 if fast else 1
        self.banks = QUAD if fast else 1
        self.parts = 2 if fast else 1

    def view(self, ap):
        if not self.fast:
            return ap
        flat = ap.bitcast(F16)
        return flat[:, 0:flat.shape[1] // 2]


class Chain:

    def __init__(self, eng, sem):
        self.eng, self.sem, self.n = eng, sem, 0

    def __call__(self, ins):
        self.n += 1
        ins.then_inc(self.sem, 1)
        self.eng.wait_ge(self.sem, self.n)


def program(nc, a, out):
    fast, general = Mode(True), Mode(False)
    top = ExitStack()

    def dram(name, shape, dt=F32):
        return nc.dram_tensor(name, shape, dt, kind="Internal").ap()

    adj = {}
    for m in (fast, general):
        k = "f" if m.fast else "g"
        for what in ("t0", "t1", "sd", "ds"):
            adj[m, what] = dram(f"adj_{what}_{k}", [NPAD, NPAD], m.dt)
    sums_dram = dram("sums_dram", [2 * NCHUNK, P, GROUPS * HEADS * 3 * (CH + 1)])
    rows_dram = dram("rows_dram", [8, HEADS, NPAD])

    def sb(ctx, name, shape, dt=F32):
        return ctx.enter_context(nc.sbuf_tensor(name, shape, dt))

    def pb(ctx, name, shape, dt=F32):
        return ctx.enter_context(nc.psum_tensor(name, shape, dt))

    def sem(name):
        return top.enter_context(nc.semaphore(name))

    X = sb(top, "X", [P, NT, D])
    hidden = ExitStack()
    ident = sb(top, "ident", [P, P])
    ident16 = sb(top, "ident16", [P, P], F16)
    ones = sb(top, "ones", [P, P])
    ones16 = sb(top, "ones16", [P, 1], F16)
    small = sb(top, "small", [P, 8])
    flag = sb(top, "flag", [1, 1], I32)
    MILD, HARSH, ANY_EDGES, NOT_MILD = range(4)
    path = sb(top, "path", [1, 4], I32)
    rdeg_in = sb(top, "rdeg_in", [P, NT])
    rdeg_all = sb(top, "rdeg_all", [P, NT])
    WN = ["L0_gnn_W_self1", "L0_gnn_W_neigh1", "L0_gnn_W_self2", "L0_gnn_W_neigh2", "L1_gnn_W_self",
          "L1_gnn_W_neigh", "L2_gnn_W_data", "L2_gnn_W_control", "L2_gnn_W_self", "L3_gnn_W1", "L3_gnn_W2"]
    TURNED = range(4, 9)
    W = sb(top, "W", [P, len(WN), D])
    w_of = {n: W[:, i, :] for i, n in enumerate(WN)}
    BN = ["L0_gnn_b1", "L0_gnn_b2", "L2_gnn_b_data", "L2_gnn_b_control", "L2_gnn_b_self", "L3_gnn_b1",
          "L3_gnn_b2", "L3_gnn_a_src1", "L3_gnn_a_dst1", "L3_gnn_a_src2", "L3_gnn_a_dst2"]
    B = sb(top, "B", [P, len(BN), D])
    b_of = {n: B[:, i, :] for i, n in enumerate(BN)}

    CH1 = CH + 1
    def is_fast(eng):
        return eng.value_load(flag[0:1, 0:1], min_val=0, max_val=1)

    def on_path(eng, which, body):
        with eng.If(eng.value_load(path[0:1, which:which + 1], min_val=0, max_val=1)):
            body(eng)
            eng.nop()
        with eng.Else():
            eng.nop()

    def both(eng, body):
        with eng.If(is_fast(eng)):
            body(eng, fast)
            eng.nop()
        with eng.Else():
            body(eng, general)
            eng.nop()

    edges = ExitStack()
    EK = sb(edges, "EK", [P, 3, EC])
    CT = sb(edges, "CT", [1, NW], I32)
    with ExitStack() as ctx:
        edst = sb(ctx, "edst", [P, ET, P], I32)
        enext = sb(ctx, "enext", [P, ET, P], I32)
        esrc = sb(ctx, "esrc", [P, ET, P], I32)
        etyp = sb(ctx, "etyp", [P, ET, P], I32)
        ehi = sb(ctx, "ehi", [P, ET, P], I32)
        elo = sb(ctx, "elo", [P, ET, P], I32)
        keys = sb(ctx, "keys", [P, 3, ET, P])
        first8 = sb(ctx, "first8", [P, ET])
        last = sb(ctx, "last", [P, ET])
        junk = sb(ctx, "junk", [P, ET, P])
        unsorted = sb(ctx, "unsorted", [P, 1])
        thr = sb(ctx, "thr", [P, NW])
        cnt = sb(ctx, "cnt", [P, 2, NW])
        spans = sb(ctx, "spans", [1, NW])
        crow = sb(ctx, "crow", [1, 2, NW])
        fl = sb(ctx, "fl", [1, 4])
        pkeys = pb(ctx, "pkeys", [P, 4, BANK])
        pcnt = pb(ctx, "pcnt", [P, 3, BANK])
        pw = pb(ctx, "pw", [P, BANK])
        ready = {k: sem(f"p1_{k}") for k in ("loads", "weights", "const", "keys", "cnt", "turned", "copied", "dve", "wt", "wtc", "x", "pre")}

        with nc.Block() as block:
            @block.sync
            def _(sp):
                sp.wait_ge(ready["pre"], 5)
                for dst, src in ((edst, a["dst"]), (esrc, a["src"]), (etyp, a["edge_type_2"])):
                    body = ER * (ET - 1) * P
                    sp.dma_start(dst[0:ER, 0:ET - 1, :], src[0:body].rearrange("(t r q) -> r t q", t=ET - 1, q=P)).then_inc(ready["loads"], 16)
                    sp.dma_start(dst[0:LAST_ROWS, ET - 1, :], src[body:body + LAST_ROWS * P].rearrange("(r q) -> r q", q=P)).then_inc(ready["loads"], 16)
                    sp.dma_start(dst[LAST_ROWS:LAST_ROWS + 1, ET - 1, 0:REST], src[FULL_ROWS * P:E].rearrange("(r q) -> r q", r=1)).then_inc(ready["loads"], 16)
                body = ER * (ET - 1) * P
                src = a["dst"]
                sp.dma_start(enext[0:ER, 0:ET - 1, :], src[1:1 + body].rearrange("(t r q) -> r t q", t=ET - 1, q=P)).then_inc(ready["loads"], 16)
                sp.dma_start(enext[0:LAST_ROWS, ET - 1, :], src[1 + body:1 + body + LAST_ROWS * P].rearrange("(r q) -> r q", q=P)).then_inc(ready["loads"], 16)
                sp.dma_start(enext[LAST_ROWS:LAST_ROWS + 1, ET - 1, 0:REST - 1], src[1 + FULL_ROWS * P:E].rearrange("(r q) -> r q", r=1)).then_inc(ready["loads"], 16)

            @block.scalar
            def _(act):
                for i, n in enumerate(WN):
                    act.dma_start(W[:, i, :], a[n]).then_inc(ready["weights"], 16)
                for i, n in enumerate(BN):
                    v = a[n] if len(a[n].shape) == 1 else a[n].rearrange("h c -> (h c)")
                    act.dma_start(B[:, i, :], v.partition_broadcast(P)).then_inc(ready["weights"], 16)
                act.wait_ge(ready["pre"], 5)
                act.dma_start(X[:, 0:NT - 1, :], a["x"][0:(NT - 1) * P, :].rearrange("(t p) d -> p t d", p=P)).then_inc(ready["x"], 16)
                act.dma_start(X[0:N - (NT - 1) * P, NT - 1, :], a["x"][(NT - 1) * P:N, :]).then_inc(ready["x"], 16)
                act.wait_ge(ready["x"], 32)

            @block.gpsimd
            def _(pool):
                pool.memset(edst[:, :, :], int(PAD_DST)).then_inc(ready["pre"], 1)
                pool.memset(enext[:, :, :], int(PAD_DST)).then_inc(ready["pre"], 1)
                pool.memset(esrc[:, :, :], 0).then_inc(ready["pre"], 1)
                pool.memset(etyp[:, :, :], 0).then_inc(ready["pre"], 1)
                pool.memset(X[:, NT - 1, :], 0.0).then_inc(ready["pre"], 1)
                pool.memset(ident[:, :], 0.0).then_inc(ready["const"], 1)
                pool.memset(ones[:, :], 1.0).then_inc(ready["const"], 1)
                pool.memset(ones16[:, :], 1.0).then_inc(ready["const"], 1)
                pool.memset(small[:, 0:1], EPS_LN).then_inc(ready["const"], 1)
                pool.wait_ge(ready["const"], 4)
                pool.affine_select(out=ident[:, :], in_=ident[:, :], compare_op=ALU.not_equal, fill=1.0, base=0,
                                   pattern=[[-1, P]], channel_multiplier=1).then_inc(ready["const"], 1)
                pool.wait_ge(ready["const"], 5)
                pool.tensor_copy(ident16[:, :], ident[:, :]).then_inc(ready["const"], 1)
                pool.iota(thr[:, :], pattern=[[WD, NW]], base=0, channel_multiplier=0,
                          allow_small_or_imprecise_dtypes=True).then_inc(ready["const"], 1)

            @block.vector
            def _(dve):
                step = Chain(dve, ready["dve"])
                dve.wait_ge(ready["loads"], 12 * 16)
                step(nc.vector.tensor_tensor(junk[:, :, :], enext[:, :, :], edst[:, :, :], ALU.is_lt))
                step(nc.vector.reduce_sum(unsorted[:, :], junk[:, :, :].rearrange("p t q -> p (t q)"), axis=AX.X))
                step(nc.vector.tensor_scalar(ehi[:, :, :], esrc[:, :, :], 7, None, ALU.logical_shift_right))
                step(nc.vector.tensor_scalar(elo[:, :, :], esrc[:, :, :], P - 1, None, ALU.bitwise_and))
                step(nc.vector.scalar_tensor_tensor(out=keys[:, 0, :, :].rearrange("p t q -> p (t q)"), in0=edst[:, :, :].rearrange("p t q -> p (t q)"), scalar=float(NT), in1=ehi[:, :, :].rearrange("p t q -> p (t q)"),
                                                    op0=ALU.mult, op1=ALU.add))
                step(nc.vector.scalar_tensor_tensor(out=keys[:, 1, :, :].rearrange("p t q -> p (t q)"), in0=etyp[:, :, :].rearrange("p t q -> p (t q)"), scalar=1000.0, in1=elo[:, :, :].rearrange("p t q -> p (t q)"),
                                                    op0=ALU.mult, op1=ALU.add))
                step(nc.vector.tensor_scalar(junk[:, :, :], etyp[:, :, :], -1000.0, 1000.0, ALU.mult, ALU.add))
                nc.vector.tensor_tensor(keys[:, 2, :, :], junk[:, :, :], elo[:, :, :], ALU.add).then_inc(ready["keys"], 1)
                step(nc.vector.tensor_copy(last[:, :], edst[:, :, P - 1]))
                step(nc.vector.tensor_scalar(first8[:, :], edst[:, :, 0], -float(WD), None, ALU.add))
                dve.wait_ge(ready["const"], 7)
                step(nc.vector.memset(cnt[:, :, :], 0.0))
                for i, edge in enumerate((last, first8)):
                    for t in range(ET):
                        step(nc.vector.scalar_tensor_tensor(out=cnt[:, i, :], in0=thr[:, :], scalar=edge[:, t:t + 1],
                                                            in1=cnt[:, i, :], op0=ALU.is_gt, op1=ALU.add))
                nc.vector.memset(fl[:, :], 0.0).then_inc(ready["cnt"], 1)
                for b in range(3 * ET):
                    dve.wait_ge(ready["turned"], b + 1)
                    i, t = b // ET, b % ET
                    nc.vector.tensor_copy(EK[:, i, t * ER:(t + 1) * ER], pkeys[:, b % 4, 0:ER]).then_inc(ready["copied"], 1)
                dve.wait_ge(ready["turned"], 3 * ET + 1)
                step(nc.vector.tensor_copy(crow[:, 0, :], pcnt[0:1, 0, 0:NW]))
                step(nc.vector.tensor_scalar(crow[:, 0, :], crow[:, 0, :], float(EC - WCOL), None, ALU.min))
                step(nc.vector.tensor_tensor(spans[:, :], pcnt[0:1, 1, 0:NW], crow[:, 0, :], ALU.subtract))
                step(nc.vector.tensor_copy(CT[:, :], crow[:, 0, :]))
                step(nc.vector.reduce_max(fl[:, 0:1], spans[:, :], axis=AX.X))
                step(nc.vector.tensor_scalar(fl[:, 1:2], fl[:, 0:1], float(WCOL), None, ALU.is_le))
                step(nc.vector.tensor_scalar(fl[:, 2:3], pcnt[0:1, 2, 0:1], 0.0, None, ALU.is_equal))
                step(nc.vector.tensor_tensor(flag[:, :], fl[:, 1:2], fl[:, 2:3], ALU.mult))
                for b, i in enumerate(TURNED):
                    dve.wait_ge(ready["wt"], b + 1)
                    nc.vector.tensor_copy(W[:, i, :], pw[:, 0:P]).then_inc(ready["wtc"], 1)

            @block.tensor
            def _(pe):
                pe.wait_ge(ready["keys"], 1)
                pe.wait_ge(ready["const"], 5)
                for b in range(3 * ET):
                    i, t = b // ET, b % ET
                    if b >= 4:
                        pe.wait_ge(ready["copied"], b - 3)
                    nc.tensor.transpose(pkeys[:, b % 4, 0:ER], keys[0:ER, i, t, :], ident[0:ER, 0:ER]).then_inc(ready["turned"], 1)
                pe.wait_ge(ready["cnt"], 1)
                nc.tensor.matmul(pcnt[0:1, 0, 0:NW], ones[0:ER, 0:1], cnt[0:ER, 0, :], start=True, stop=True)
                nc.tensor.matmul(pcnt[0:1, 1, 0:NW], ones[0:ER, 0:1], cnt[0:ER, 1, :], start=True, stop=True)
                nc.tensor.matmul(pcnt[0:1, 2, 0:1], ones[0:ER, 0:1], unsorted[0:ER, 0:1], start=True, stop=True).then_inc(ready["turned"], 1)
                pe.wait_ge(ready["weights"], 16 * (len(WN) + len(BN)))
                for b, i in enumerate(TURNED):
                    if b:
                        pe.wait_ge(ready["wtc"], b)
                    nc.tensor.transpose(pw[:, 0:P], W[:, i, :], ident[:, :]).then_inc(ready["wt"], 1)

    with ExitStack() as ctx:
        SG = sb(ctx, "SG", [P, 2, 2 * NPAD])
        SS = sb(ctx, "SS", [P, 2, NPAD])
        SDS = sb(ctx, "SDS", [P, 2, NPAD])
        SETS = WPG // QUAD
        iota_w = sb(ctx, "iota_w", [P, WCELLS, WCOL], F16)
        iota_l = sb(ctx, "iota_l", [P, P, WCOL], F16)
        base_w = sb(ctx, "base_w", [P, NW])
        KZ = sb(ctx, "KZ", [P, BANK], F16)
        KW = sb(ctx, "KW", [P, 1])
        RAW = sb(ctx, "RAW", [P, 2, WPG, 3, WCOL])
        KD = sb(ctx, "KD", [P, WPG, WCOL])
        KC = sb(ctx, "KC", [P, 2, WPG, WCOL], F16)
        KL = sb(ctx, "KL", [P, 2, 2, WPG, WCOL], F16)
        OH = sb(ctx, "OH", [P, SETS, 2, QUAD, P, WCOL], F16)
        MV = sb(ctx, "MV", [P, SETS, QUAD, WCELLS, WCOL], F16)
        iota_g = SDS[:, 1, :]
        PW = pb(ctx, "PW", [P, 2, BANK])
        PT = pb(ctx, "PT", [P, 2, BANK])
        PDI = pb(ctx, "PDI", [P, BANK])
        PDO = pb(ctx, "PDO", [P, BANK])
        PX = pb(ctx, "PX", [P, 2, BANK])
        s = {k: sem(f"p2_{k}") for k in ("const", "kw", "raw", "keyed", "onehot", "window", "free_oh", "evac", "sum", "turned", "tevac", "deg", "stored", "group", "free_st", "dve")}

        def view2(m, t, slot):
            return m.view(t[:, slot, :])

        def rest(slot, m):
            return view2(m, SG, slot).rearrange("p (y b d) -> p y b d", y=2, b=NT), view2(m, SS, slot), view2(m, SDS, slot)

        with nc.Block() as block:
            def loop_groups(eng, windows, finish):
                windows(0, 0)
                with eng.Fori(0, (NT - 1) // 2) as pair:
                    g = pair * 2
                    windows(g + 1, 1)
                    finish(g, 0)
                    windows(g + 2, 0)
                    finish(g + 1, 1)
                finish(NT - 1, 0)

            def serial_groups(eng, windows, finish):
                with eng.Fori(0, NT) as g:
                    windows(g, 0)
                    finish(g, 0)

            def run(eng, m, windows, finish):
                (loop_groups if m.fast else serial_groups)(eng, windows, finish)

            @block.gpsimd
            def _(pool):
                pool.memset(KZ[:, :], 0.0).then_inc(s["const"], 1)
                pool.iota(iota_w[:, :, :].rearrange("p (b d) c -> p b d c", b=NT), pattern=[[1, NT], [NT, WD], [0, WCOL]], base=0, channel_multiplier=0,
                          allow_small_or_imprecise_dtypes=True).then_inc(s["const"], 1)
                pool.iota(iota_l[:, :, :], pattern=[[1, P], [0, WCOL]], base=0, channel_multiplier=0,
                          allow_small_or_imprecise_dtypes=True).then_inc(s["const"], 1)
                pool.iota(base_w[:, :], pattern=[[WCELLS, NW]], base=0, channel_multiplier=0,
                          allow_small_or_imprecise_dtypes=True).then_inc(s["const"], 1)

                def body(pool, m):
                    if not m.fast:
                        pool.iota(iota_g.rearrange("p (b d) -> p b d", b=NT), pattern=[[1, NT], [NT, P]], base=0, channel_multiplier=0,
                                  allow_small_or_imprecise_dtypes=True).then_inc(s["const"], 1)

                    def finish(g, slot):
                        st, both_types, _ = rest(slot, m)
                        pool.wait_ge(s["evac"], m.banks + (g + 1) * (WPG if m.fast else 4))
                        pool.wait_ge(s["group"], g + 1)
                        flat = st.rearrange("p y b d -> p y (b d)")
                        nc.gpsimd.tensor_tensor(both_types, flat[:, 0, :], flat[:, 1, :], ALU.add).then_inc(s["sum"], 1)

                    def windows(g, slot):
                        if m.fast:
                            with pool.Fori(0, WPG) as w:
                                pool.wait_ge(s["keyed"], g * 2 + 2)
                                c0 = pool.value_load(CT[0:1, bass.ds(g * WPG + w, 1)], min_val=0, max_val=EC - WCOL)
                                nc.gpsimd.tensor_copy(RAW[:, slot, bass.ds(w, 1), :, :].rearrange("p o y c -> p (o y) c"), EK[:, :, bass.ds(c0, WCOL)]).then_inc(s["raw"], 1)
                    run(pool, m, windows, finish)
                both(pool, body)

            @block.vector
            def _(dve):
                def body(dve, m):
                    dve.sem_inc(s["keyed"], 4)
                    dve.wait_ge(s["const"], 4 if m.fast else 5)

                    def quad(n4, q, u, slot, g):
                        w0 = bass.ds(q * QUAD, QUAD)
                        dve.wait_ge(s["keyed"], g * 2 + 6)
                        dve.wait_ge(s["window"], n4 * QUAD + QUAD)
                        for y in range(2):
                            nc.vector.tensor_tensor(OH[:, u, y, :, :, :], iota_l[:, :, :].unsqueeze(1).to_broadcast([P, QUAD, P, WCOL]),
                                                    KL[:, slot, y, w0, :].unsqueeze(2).to_broadcast([P, QUAD, P, WCOL]), ALU.is_equal)
                        nc.vector.tensor_tensor(MV[:, u, :, :, :], iota_w[:, :, :].unsqueeze(1).to_broadcast([P, QUAD, WCELLS, WCOL]),
                                                KC[:, slot, w0, :].unsqueeze(2).to_broadcast([P, QUAD, WCELLS, WCOL]), ALU.is_equal).then_inc(s["onehot"], 1)

                    if m.fast:
                        def windows(g, slot):
                            dve.wait_ge(s["raw"], g * WPG + WPG)
                            nc.vector.tensor_tensor(KD[:, :, :], RAW[:, slot, :, 0, :], base_w[:, bass.ds(g * WPG, WPG)].unsqueeze(2).to_broadcast([P, WPG, WCOL]),
                                                    ALU.subtract).then_inc(s["kw"], 1)
                            dve.wait_ge(s["kw"], g + 1)
                            nc.vector.tensor_scalar(KC[:, slot, :, :], KD[:, :, :], 1000.0, -1000.0, ALU.min, ALU.max).then_inc(s["keyed"], 1)
                            nc.vector.tensor_copy(KL[:, slot, :, :, :], RAW[:, slot, :, 1:3, :].rearrange("p w y c -> p y w c")).then_inc(s["keyed"], 1)
                            for u in range(SETS):
                                quad(g * SETS + u, u, u, slot, g)
                        run(dve, m, windows, lambda g, slot: None)
                    else:
                        OHG = OH[:, 0, 0, 0, :, :].rearrange("p l c -> p (l c)")

                        def column(y, g, half, c, i):
                            dve.wait_ge(s["free_oh"], i + 1)
                            b0, nb = half * HALF[0], HALF[half]
                            nc.vector.tensor_scalar(KW[:, 0:1], EK[:, 0, bass.ds(c, 1)], base_w[:, bass.ds(g * WPG, 1)], None, ALU.subtract).then_inc(s["kw"], 1)
                            nc.vector.tensor_scalar(OHG[:, 0:P], iota_l[:, :, 0], EK[:, 1 + y, bass.ds(c, 1)], None, ALU.is_equal)
                            dve.wait_ge(s["kw"], i + 1)
                            nc.vector.tensor_scalar(genmv[:, 0:nb * P], iota_g[:, b0 * P:(b0 + nb) * P], KW[:, 0:1], None, ALU.is_equal).then_inc(s["onehot"], 1)
                        with dve.Fori(0, NT) as g:
                            for y in range(2):
                                for half in range(2):
                                    with dve.Fori(0, EC) as c:
                                        column(y, g, half, c, ((g * 4 + y * 2 + half) * EC + c))
                genmv = SG[:, 1, :].bitcast(F16)
                both(dve, body)
                dve.wait_ge(s["deg"], 1)
                step = Chain(dve, s["dve"])
                step(nc.vector.tensor_copy(rdeg_in[:, :], PDI[:, 0:NT]))
                step(nc.vector.tensor_tensor(rdeg_all[:, :], rdeg_in[:, :], PDO[:, 0:NT], ALU.add))
                for r in (rdeg_in, rdeg_all):
                    step(nc.vector.tensor_scalar(r[:, :], r[:, :], 1.0, None, ALU.max))
                    step(nc.vector.reciprocal(r[:, :], r[:, :]))

            @block.tensor
            def _(pe):
                def body(pe, m):
                    idm = ident16 if m.fast else ident
                    one = ones16[:, 0:1] if m.fast else ones[:, 0:1]
                    pe.sem_inc(s["free_oh"], 1)
                    pe.sem_inc(s["window"], SETS * QUAD if m.fast else 1)
                    nc.tensor.matmul(PDO[:, 0:NT], KZ[:, 0:P], KZ[:, 0:NT], start=True, stop=True)

                    def finish(g, slot):
                        _, ss, sds = rest(slot, m)
                        pe.wait_ge(s["sum"], g + 1)
                        for q in range(NBANK):
                            i = 7 * g + q
                            pe.wait_ge(s["tevac"], i + 1)
                            ts = (q + slot) % 2 if m.fast else 0
                            pt = PT[:, ts, :]
                            pt = pt.bitcast(F16) if m.fast else pt
                            nb = bank_cols(q) // P
                            for b in range(nb):
                                ins = nc.tensor.transpose(pt[:, b * P:(b + 1) * P], ss[:, (4 * q + b) * P:(4 * q + b + 1) * P], idm[:, :])
                            ins.then_inc(s["turned"], 1)
                        for b in range(NT):
                            nc.tensor.matmul(PDI[:, bass.ds(g, 1)], ss[:, b * P:(b + 1) * P], one, start=(b == 0), stop=(b == NT - 1))
                        pe.wait_ge(s["tevac"], m.slots + NBANK * (g + 1))
                        for b in range(NT):
                            ins = nc.tensor.matmul(PDO[:, b:b + 1], sds[:, b * P:(b + 1) * P], one, start=False, stop=False, skip_group_check=True)
                        ins.then_inc(s["free_st"], 1)

                    if m.fast:
                        def windows(g, slot):
                            for u in range(SETS):
                                pe.wait_ge(s["onehot"], g * SETS + (u + 1))
                                for v in range(QUAD):
                                    pe.wait_ge(s["evac"], g * WPG + (u * QUAD + v + 1))
                                    for y in range(2):
                                        for t in range(WCOL):
                                            ins = nc.tensor.matmul(GB[v][:, y * WCELLS:(y + 1) * WCELLS], OH[:, u, y, v, :, t], MV[:, u, v, :, t],
                                                                   start=(t == 0), stop=(t == WCOL - 1))
                                    ins.then_inc(s["window"], 1)
                    else:
                        def windows(g, slot):
                            OHG = OH[:, 0, 0, 0, :, :].rearrange("p l c -> p (l c)")
                            genmv = SG[:, 1, :].bitcast(F16)
                            for y in range(2):
                                for half in range(2):
                                    nb = HALF[half]
                                    base = (g * 4 + y * 2 + half) * EC
                                    pe.wait_ge(s["evac"], g * 4 + y * 2 + half + 1)
                                    for q in range(4):
                                        cols = min(BANK, nb * P - q * BANK)
                                        if cols > 0:
                                            nc.tensor.matmul(GB[q][:, 0:cols], KZ[:, 0:P], KZ[:, 0:cols], start=True, stop=True)
                                    with pe.Fori(0, EC) as c:
                                        pe.wait_ge(s["onehot"], base + c + 1)
                                        for q in range(4):
                                            cols = min(BANK, nb * P - q * BANK)
                                            if cols > 0:
                                                ins = nc.tensor.matmul(GB[q][:, 0:cols], OHG[:, 0:P], genmv[:, q * BANK:q * BANK + cols],
                                                                       start=False, stop=False, skip_group_check=True)
                                        ins.then_inc(s["free_oh"], 1)
                                    nc.tensor.matmul(PDI[0:1, 40:41], KZ[:, 0:1], KZ[:, 0:1], start=True, stop=True).then_inc(s["window"], 1)
                    run(pe, m, windows, finish)
                GB = [PW[:, 0, :], PW[:, 1, :], PX[:, 0, :], PX[:, 1, :]]
                pe.wait_ge(s["const"], 4)
                both(pe, body)
                nc.tensor.matmul(PDI[0:1, 41:42], KZ[:, 0:1], KZ[:, 0:1], start=True, stop=True).then_inc(s["deg"], 1)

            @block.scalar
            def _(act):
                def body(act, m):
                    act.sem_inc(s["evac"], m.banks)
                    act.sem_inc(s["tevac"], m.slots)

                    def finish(g, slot):
                        _, _, sds = rest(slot, m)
                        act.wait_ge(s["group"], g + 1)
                        for q in range(NBANK):
                            act.wait_ge(s["turned"], NBANK * g + q + 1)
                            ts = (q + slot) % 2 if m.fast else 0
                            pt = PT[:, ts, :]
                            pt = pt.bitcast(F16) if m.fast else pt
                            nc.scalar.activation(sds[:, q * BANK:q * BANK + bank_cols(q)], pt[:, 0:bank_cols(q)], ACT.Copy).then_inc(s["tevac"], 1)

                    if m.fast:
                        def windows(g, slot):
                            st, _, _ = rest(slot, m)
                            act.wait_ge(s["group"], g + 1)
                            with act.Fori(0, WPG // QUAD) as q:
                                for v in range(QUAD):
                                    n = g * WPG + q * QUAD + v
                                    act.wait_ge(s["window"], SETS * QUAD + n + 1)
                                    src = GB2[v][:, 0:2 * WCELLS].rearrange("p (y b d) -> p y b d", y=2, b=NT)
                                    nc.scalar.activation(st[:, :, :, bass.ds(q * (QUAD * WD) + v * WD, WD)], src, ACT.Copy).then_inc(s["evac"], 1)
                    else:
                        def windows(g, slot):
                            st, _, _ = rest(slot, m)
                            flat = st.rearrange("p y b d -> p y (b d)")
                            act.wait_ge(s["group"], g + 1)
                            for y in range(2):
                                for half in range(2):
                                    n = g * 4 + y * 2 + half
                                    act.wait_ge(s["window"], n + 2)
                                    for q in range(4):
                                        cols = min(BANK, HALF[half] * P - q * BANK)
                                        if cols > 0:
                                            at = half * HALF[0] * P + q * BANK
                                            ins = nc.scalar.activation(flat[:, y, at:at + cols], GB2[q][:, 0:cols], ACT.Copy)
                                    ins.then_inc(s["evac"], 1)
                    run(act, m, windows, finish)
                GB2 = [PW[:, 0, :], PW[:, 1, :], PX[:, 0, :], PX[:, 1, :]]
                both(act, body)

            @block.sync
            def _(sp):
                def body(sp, m):
                    sp.sem_inc(s["group"], m.slots)

                    def finish(g, slot):
                        st, ss, sds = rest(slot, m)
                        sp.wait_ge(s["sum"], g + 1)
                        cols = bass.ds(g * P, P)
                        for y, what in enumerate(("t0", "t1")):
                            sp.dma_start(adj[m, what][:, cols].rearrange("(b p) d -> p b d", p=P), st[:, y, :, :]).then_inc(s["stored"], 16)
                        sp.dma_start(adj[m, "sd"][:, cols].rearrange("(b p) d -> p b d", p=P), ss.rearrange("p (b d) -> p b d", b=NT)).then_inc(s["stored"], 16)
                        sp.wait_ge(s["tevac"], m.slots + NBANK * (g + 1))
                        sp.dma_start(adj[m, "ds"][bass.ds(g * P, P), :], sds).then_inc(s["stored"], 16)
                        sp.wait_ge(s["stored"], 64 * (g + 1))
                        sp.wait_ge(s["free_st"], g + 1)
                        sp.sem_inc(s["group"], 1)
                    run(sp, m, lambda g, slot: None, finish)
                both(sp, body)
    edges.close()
    GE = sb(top, "GE", [P, 2, NT, HEADS, CH1])
    ES = sb(top, "ES", [P, 2, 2, HEADS, NT])
    ES2 = sb(top, "ES2", [P, 2, HEADS, NT])
    MX = sb(top, "MX", [P, 2, HEADS, NT])
    EM = sb(top, "EM", [P, 2, 2, HEADS, NT])
    XS = sb(top, "XS", [P, 2, NT, HEADS])
    rows = sb(top, "rows", [P, 4, P])

    H = sb(hidden, "H", [P, NT, D])
    HT = sb(hidden, "HT", [P, NPAD])

    def inner(v, k):
        return v.unsqueeze(2).to_broadcast([P, v.shape[1], k])

    def outer(v, n):
        return v.unsqueeze(1).to_broadcast([P, n, v.shape[1]])

    CK = NT // GROUPS
    HSCALE = 2048.0

    def chunk_of(v, c):
        return v[:, c * CK:(c + 1) * CK, :]

    norm = {k: sem(f"norm_{k}") for k in ("sums", "mean", "centred", "squared", "vars", "deviation", "h")}

    def norm_vector(dve, r, T1, T2, mu, var, std):
        for c in range(GROUPS):
            nc.vector.reduce_sum(mu[:, c * CK:(c + 1) * CK], chunk_of(X, c), axis=AX.X).then_inc(norm["sums"], 1)
        dve.wait_ge(norm["sums"], (r + 1) * GROUPS)
        nc.vector.tensor_scalar(mu[:, :], mu[:, :], -1.0 / D, None, ALU.mult).then_inc(norm["mean"], 1)
        dve.wait_ge(norm["mean"], 2 * r + 1)
        for c in range(GROUPS):
            nc.vector.tensor_tensor(chunk_of(T1, c), chunk_of(X, c), inner(mu[:, c * CK:(c + 1) * CK], D), ALU.add).then_inc(norm["centred"], 1)
        for c in range(GROUPS):
            dve.wait_ge(norm["squared"], r * GROUPS + c + 1)
            nc.vector.reduce_sum(var[:, c * CK:(c + 1) * CK], chunk_of(T2, c), axis=AX.X).then_inc(norm["vars"], 1)
        dve.wait_ge(norm["deviation"], r + 1)
        nc.vector.reciprocal(std[:, :], std[:, :]).then_inc(norm["mean"], 1)
        dve.wait_ge(norm["mean"], 2 * r + 2)
        for c in range(GROUPS):
            nc.vector.scalar_tensor_tensor(out=chunk_of(H, c), in0=chunk_of(T1, c), scalar=0.0, in1=inner(std[:, c * CK:(c + 1) * CK], D),
                                           op0=ALU.max, op1=ALU.mult).then_inc(norm["h"], 1)

    def norm_scalar(act, r, T1, T2, var, std):
        for c in range(GROUPS):
            act.wait_ge(norm["centred"], r * GROUPS + c + 1)
            nc.scalar.activation(chunk_of(T2, c), chunk_of(T1, c), ACT.Square).then_inc(norm["squared"], 1)
        act.wait_ge(norm["vars"], (r + 1) * GROUPS)
        nc.scalar.activation(std[:, :], var[:, :], ACT.Sqrt, bias=small[:, 0:1], scale=1.0 / D).then_inc(norm["deviation"], 1)

    with ExitStack() as ctx:
        HS = sb(ctx, "HS", [P, 2 * NPAD])
        AB = sb(ctx, "AB", [P, 3, NPAD])
        AG = sb(ctx, "AG", [P, NPAD])
        T1 = sb(ctx, "T1", [P, NT, D])
        T2 = sb(ctx, "T2", [P, NT, D])
        mu = sb(ctx, "mu", [P, NT])
        var = sb(ctx, "var", [P, NT])
        std = sb(ctx, "std", [P, NT])
        reach = sb(ctx, "reach", [P, 4])
        SC = sb(ctx, "SC", [P, 2])
        PA = pb(ctx, "PA", [P, NBANK, BANK])
        PZ = pb(ctx, "PZ", [P, BANK])
        PF = PA[:, :, :].rearrange("p b n -> p (b n)")
        parts = HS[:, :].bitcast(F16).rearrange("p (y k n) -> p y k n", y=2, k=2)
        whole = HS[:, :].rearrange("p (y n) -> p y n", y=2)
        SET = 3 * BANK

        def layer(name, r, sources, kind):
            typed = kind == "typed"
            ranging = typed or r is None
            summands = (T1, T2) if typed else (H,)
            ny = len(summands)
            w_self, w_neigh, b_own = {"relu": ("L0_gnn_W_self1", "L0_gnn_W_neigh1", "L0_gnn_b1"), "sage": ("L0_gnn_W_self2", "L0_gnn_W_neigh2", "L0_gnn_b2"),
                                      "normed": ("L1_gnn_W_self", "L1_gnn_W_neigh", None), "typed": ("L2_gnn_W_self", None, "L2_gnn_b_self")}[kind]
            loaded = [sem(f"{name}_loaded{i}") for i in range(3)]
            turned, moved, scaled, hi, ready, used, summed, staged, dense, share, own, sd = (
                sem(f"{name}_{k}") for k in ("turned", "moved", "scaled", "hi", "ready", "used", "summed", "staged", "dense", "share", "own", "vector"))
            if typed:
                mapped, biased = sem(f"{name}_mapped"), sem(f"{name}_biased")
            else:
                free = sem(f"{name}_free")
            if ranging:
                reached, everywhere = sem(f"{name}_reached"), sem(f"{name}_everywhere")
            if kind == "normed":
                paired = sem(f"{name}_paired")

            def passes(m):
                return [("pair", 0)] if m.fast and kind == "normed" else sources

            def cols(v, c):
                return v[:, c * CK * P:(c + 1) * CK * P]

            def flat_of(v, c):
                return chunk_of(v, c).rearrange("p t d -> p (t d)")

            def steps(eng, m, one, before_loop=lambda: None):
                for i, _ in enumerate(passes(m)):
                    at = NT * i
                    for k in range(3):
                        one(i, k, at + k, (at + k) % 3, (at + k) // 3 + 1)
                    if i == 0:
                        before_loop()
                    with eng.Fori(0, (NT - 4) // 3) as j:
                        for u in range(3):
                            one(i, j * 3 + (3 + u), j * 3 + (at + 3 + u), (at + 3 + u) % 3, j + ((at + 3 + u) // 3 + 1))
                    one(i, NT - 1, at + NT - 1, (at + NT - 1) % 3, (at + NT - 1) // 3 + 1)

            def groups(eng, one):
                one(0, 0)
                with eng.Fori(0, (GROUPS - 1) // 2) as j:
                    one(j * 2 + 1, 1)
                    one(j * 2 + 2, 0)

            def results(u, part):
                return PF[:, u * SET:u * SET + CK * 2 * D].rearrange("p (t k) -> p t k", k=2 * D)[:, :, part * D:(part + 1) * D]

            def pair_of(slot):
                return AB[:, slot, :].bitcast(F16).rearrange("p (o n) -> p o n", o=2)

            with nc.Block() as block:
                @block.sync
                def _(sp):
                    def body(sp, m):
                        def one(i, k, index, slot, _):
                            if not isinstance(index, int) or index >= 3:
                                sp.wait_ge(used, index - 2)
                            what = passes(m)[i][0]
                            if what == "pair":
                                for half, (each, _) in enumerate(sources):
                                    sp.dma_start(pair_of(slot)[:, half, :], adj[m, each][bass.ds(k * P, P), :]).then_inc(loaded[slot], 16)
                            else:
                                sp.dma_start(m.view(AB[:, slot, :]), adj[m, what][bass.ds(k * P, P), :]).then_inc(loaded[slot], 16)
                        steps(sp, m, one)
                    both(sp, body)

                if ranging:
                    @block.gpsimd
                    def _(pool):
                        pool.wait_ge(reached, ny)
                        nc.gpsimd.partition_all_reduce(reach[:, 2:2 + ny], reach[:, 0:ny], P, bass.bass_isa.ReduceOp.max).then_inc(everywhere, 1)

                @block.vector
                def _(dve):
                    if r is not None:
                        norm_vector(dve, r, T1, T2, mu, var, std)
                    if typed:
                        dve.wait_ge(norm["h"], (r + 1) * GROUPS)
                        for y, b in enumerate(("L2_gnn_b_data", "L2_gnn_b_control")):
                            for c in range(GROUPS):
                                dve.wait_ge(mapped, y * GROUPS + c + 1)
                                nc.vector.tensor_tensor(chunk_of(summands[y], c), results((y * GROUPS + c) % 2, 0), outer(b_of[b], CK), ALU.add).then_inc(biased, 1)
                        dve.wait_ge(biased, 2 * GROUPS)
                    if ranging:
                        for y, v in enumerate(summands):
                            nc.vector.tensor_reduce(reach[:, y:y + 1], v[:, :, :].rearrange("p t d -> p (t d)"), axis=AX.X, op=ALU.max,
                                                    apply_absolute_value=True).then_inc(reached, 1)
                    n = 0

                    def step(ins):
                        nonlocal n
                        n += 1
                        ins.then_inc(sd, 1)
                        dve.wait_ge(sd, n)
                    if ranging:
                        dve.wait_ge(everywhere, 1)
                        step(nc.vector.tensor_tensor(reach[:, 0:1], reach[:, 2:3], reach[:, 1 + ny:2 + ny], ALU.max))
                        step(nc.vector.tensor_scalar(reach[:, 1:2], reach[:, 0:1], 1e-30, None, ALU.max))
                        step(nc.vector.tensor_scalar(reach[:, 2:3].bitcast(I32), reach[:, 1:2].bitcast(I32), 0x7F800000, None, ALU.bitwise_and))
                        step(nc.vector.tensor_scalar(SC[:, 1:2], reach[:, 2:3], 1.0 / 8192.0, None, ALU.mult))
                        step(nc.vector.reciprocal(SC[:, 0:1], SC[:, 1:2]))
                    else:
                        step(nc.vector.memset(SC[:, 0:1], HSCALE))
                        step(nc.vector.memset(SC[:, 1:2], 1.0 / HSCALE))
                    n_scaled = n

                    def body(dve, m):
                        if m.fast:
                            dve.sem_inc(scaled, 1)
                            for y, v in enumerate(summands):
                                for c in range(GROUPS):
                                    dve.wait_ge(hi, y * GROUPS + c + 1)
                                    nc.vector.scalar_tensor_tensor(out=cols(parts[:, y, 1, :], c), in0=flat_of(v, c), scalar=SC[:, 0:1],
                                                                   in1=cols(parts[:, y, 0, :], c), op0=ALU.mult, op1=ALU.subtract).then_inc(ready, 1)

                            def add(i, k, index, slot, count):
                                dve.wait_ge(loaded[slot], count * 32)
                                pair = pair_of(slot)
                                nc.vector.tensor_tensor(pair[:, 0, :], pair[:, 0, :], pair[:, 1, :], ALU.add).then_inc(paired, 1)
                            if kind == "normed":
                                steps(dve, m, add)
                        else:
                            nc.vector.memset(SC[:, :], 1.0).then_inc(scaled, 1)
                            if r is not None:
                                dve.wait_ge(norm["h"], (r + 1) * GROUPS)
                            for y, v in enumerate(summands):
                                for c in range(GROUPS):
                                    nc.vector.tensor_copy(cols(whole[:, y, :], c), flat_of(v, c)).then_inc(ready, 1)
                    both(dve, body)
                    dve.wait_ge(summed, 1)
                    dve.wait_ge(scaled, 1)
                    for b in range(3):
                        ins = nc.vector.tensor_scalar(AG[:, b * BANK:(b + 1) * BANK], PA[:, b, :], SC[:, 1:2], None, ALU.mult)
                    ins.then_inc(staged, 1)
                    per = {"relu": 0, "sage": 1, "normed": 2, "typed": 0}[kind]

                    def one(g, u):
                        tiles = bass.ds(g * CK, CK)
                        t1, t2 = T1[:, u * CK:(u + 1) * CK, :], T2[:, u * CK:(u + 1) * CK, :]
                        at = 0

                        def then(ins):
                            nonlocal at
                            at += 1
                            ins.then_inc(sd, 1)
                            dve.wait_ge(sd, g * per + (n_scaled + at))
                        if typed:
                            dve.wait_ge(share, g + 1)
                            nc.vector.tensor_tensor(X[:, tiles, :], X[:, tiles, :], t1, ALU.add).then_inc(own, 1)
                            return
                        dve.wait_ge(share, g + 1)
                        if kind == "normed":
                            then(nc.vector.scalar_tensor_tensor(out=t2, in0=t1, scalar=SLOPE, in1=t1, op0=ALU.mult, op1=ALU.max))
                            nc.vector.tensor_tensor(t1, t2, results(u, 0), ALU.add).then_inc(free, 1)
                            then(nc.vector.tensor_copy(var[:, 0:1], mu[:, 0:1]))
                            dve.wait_ge(free, g + 2)
                            nc.vector.scalar_tensor_tensor(out=H[:, tiles, :], in0=t1, scalar=SLOPE, in1=t1, op0=ALU.mult, op1=ALU.max).then_inc(own, 1)
                        else:
                            nc.vector.tensor_tensor(t2, t1, results(u, 0), ALU.add).then_inc(free, 1)
                            if kind == "sage":
                                dve.wait_ge(free, g + 2)
                                then(nc.vector.tensor_tensor(X[:, tiles, :], X[:, tiles, :], t2, ALU.add))
                    if not typed:
                        dve.sem_inc(free, 1)
                    groups(dve, one)
                    if kind == "normed":
                        n = n_scaled + per * GROUPS
                        dve.wait_ge(own, GROUPS + 1)
                        step(nc.vector.reduce_sum(mu[:, :], T1[:, :, :], axis=AX.X))
                        nc.vector.tensor_scalar(var[:, :], mu[:, :], EPS_NORM * EPS_NORM, None, ALU.max).then_inc(own, 1)
                        dve.wait_ge(own, GROUPS + 3)
                        step(nc.vector.reciprocal(std[:, :], std[:, :]))
                        step(nc.vector.tensor_tensor(T2[:, :, :], H[:, :, :], inner(std[:, :], D), ALU.mult))
                        step(nc.vector.tensor_tensor(X[:, :, :], X[:, :, :], T2[:, :, :], ALU.add))

                @block.scalar
                def _(act):
                    if r is not None:
                        norm_scalar(act, r, T1, T2, var, std)

                    def turned_out(c):
                        act.wait_ge(turned, c + 1)
                        nc.scalar.activation(cols(HT, c), PF[:, (c % 3) * 2 * BANK:(c % 3) * 2 * BANK + CK * P], ACT.Copy).then_inc(moved, 1)
                    if typed:
                        for c in range(GROUPS):
                            turned_out(c)

                    def body(act, m):
                        if m.fast:
                            act.wait_ge(scaled, 1)
                        for y, v in enumerate(summands):
                            for c in range(GROUPS):
                                if m.fast:
                                    if r is not None and not typed:
                                        act.wait_ge(norm["h"], r * GROUPS + c + 1)
                                    nc.scalar.activation(cols(parts[:, y, 0, :], c), flat_of(v, c), ACT.Copy, scale=SC[:, 0:1]).then_inc(hi, 1)
                                if not typed:
                                    turned_out(c)
                    both(act, body)
                    act.wait_ge(summed, 1)
                    act.wait_ge(scaled, 1)
                    for b in range(3, NBANK):
                        ins = nc.scalar.activation(AG[:, b * BANK:b * BANK + bank_cols(b)], PA[:, b, 0:bank_cols(b)], ACT.Copy, scale=SC[:, 1:2])
                    ins.then_inc(staged, 1)

                    def one(g, u):
                        tiles = bass.ds(g * CK, CK)
                        t1 = T1[:, u * CK:(u + 1) * CK, :]
                        act.wait_ge(dense, g + 1)
                        if typed:
                            act.wait_ge(own, g + 1)
                            nc.scalar.activation(t1, results(u, 0), ACT.Relu).then_inc(share, 1)
                            return
                        if kind != "relu":
                            act.wait_ge(free, g + 1)
                        rdeg = rdeg_all if kind == "normed" else rdeg_in
                        for i in range(CK):
                            ins = nc.scalar.activation(T1[:, u * CK + i, :], results(u, 1)[:, i, :], ACT.Copy, scale=rdeg[:, bass.ds(g * CK + i, 1)])
                        ins.then_inc(share, 1)
                        if kind == "relu":
                            act.wait_ge(free, g + 2)
                            nc.scalar.activation(H[:, tiles, :], T2[:, u * CK:(u + 1) * CK, :], ACT.Relu).then_inc(own, 1)
                    if typed:
                        act.sem_inc(own, 2)
                    groups(act, one)
                    if kind == "normed":
                        act.wait_ge(own, GROUPS)
                        nc.scalar.activation(T1[:, :, :], H[:, :, :], ACT.Square).then_inc(own, 1)
                        act.wait_ge(own, GROUPS + 2)
                        nc.scalar.activation(std[:, :], var[:, :], ACT.Sqrt).then_inc(own, 1)

                @block.tensor
                def _(pe):
                    for c in range(GROUPS):
                        if r is not None:
                            pe.wait_ge(norm["h"], r * GROUPS + c + 1)
                        if c >= 3:
                            pe.wait_ge(moved, c - 2)
                        for i in range(CK):
                            ins = nc.tensor.transpose(PF[:, (c % 3) * 2 * BANK + i * P:(c % 3) * 2 * BANK + (i + 1) * P], H[:, c * CK + i, :], ident[:, :])
                        ins.then_inc(turned, 1)
                    pe.wait_ge(moved, GROUPS)
                    if typed:
                        for y, w in enumerate(("L2_gnn_W_data", "L2_gnn_W_control")):
                            for c in range(GROUPS):
                                u = (y * GROUPS + c) % 2
                                if y * GROUPS + c >= 2:
                                    pe.wait_ge(biased, y * GROUPS + c - 1)
                                for i in range(CK):
                                    t = c * CK + i
                                    ins = nc.tensor.matmul(PF[:, u * SET + i * 2 * D:u * SET + i * 2 * D + D],
                                                           HT[:, t * P:(t + 1) * P], w_of[w], start=True, stop=True)
                                ins.then_inc(mapped, 1)
                        pe.wait_ge(biased, 2 * GROUPS)

                    def body(pe, m):
                        pe.wait_ge(ready, 1)

                        def one(i, k, index, slot, count):
                            if passes(m)[i][0] == "pair":
                                pe.wait_ge(paired, index + 1)
                            else:
                                pe.wait_ge(loaded[slot], count * 16)
                            rows = m.view(AB[:, slot, :])
                            y = passes(m)[i][1]
                            for part in range(m.parts):
                                src = parts[:, y, part, :] if m.fast else whole[:, y, :]
                                first = isinstance(index, int) and index == 0 and part == 0
                                last = isinstance(index, int) and index == NT * len(passes(m)) - 1 and part == m.parts - 1
                                for b in range(NBANK):
                                    ins = nc.tensor.matmul(PA[:, b, 0:bank_cols(b)], src[:, bass.ds(k * P, P)], rows[:, b * BANK:b * BANK + bank_cols(b)],
                                                           start=first, stop=last)
                            ins.then_inc(used, 1)
                        if m.fast:
                            steps(pe, m, one, lambda: pe.wait_ge(ready, GROUPS * ny))
                        else:
                            pe.wait_ge(ready, GROUPS * ny)
                            for i in range(len(passes(m))):
                                for k in range(NT):
                                    index = i * NT + k
                                    one(i, k, index, index % 3, index // 3 + 1)
                    both(pe, body)
                    nc.tensor.matmul(PZ[0:1, 0:1], ident16[:, 0:1], ident16[:, 0:1], start=True, stop=True).then_inc(summed, 1)
                    pe.wait_ge(staged, 2)
                    for g in range(GROUPS):
                        u = g % 2
                        if g >= 2:
                            if typed:
                                pe.wait_ge(share, g - 1)
                            else:
                                pe.wait_ge(free, g)
                        for i in range(CK):
                            at = slice((g * CK + i) * P, (g * CK + i + 1) * P)
                            mine = PF[:, u * SET + i * 2 * D:u * SET + i * 2 * D + D]
                            neigh = PF[:, u * SET + i * 2 * D + D:u * SET + (i + 1) * 2 * D]
                            ins = nc.tensor.matmul(mine, HT[:, at], w_of[w_self], start=True, stop=b_own is None)
                            if typed:
                                nc.tensor.matmul(mine, AG[:, at], ident[:, :], start=False, stop=False)
                            if b_own:
                                ins = nc.tensor.matmul(mine, ones[0:1, :], b_of[b_own][0:1, :], start=False, stop=True)
                            if not typed:
                                ins = nc.tensor.matmul(neigh, AG[:, at], w_of[w_neigh], start=True, stop=True)
                        ins.then_inc(dense, 1)

        layer("L0a", 0, [("sd", 0)], "relu")
        layer("L0b", None, [("sd", 0)], "sage")
        layer("L1", 1, [("sd", 0), ("ds", 0)], "normed")
        layer("L2", 2, [("t0", 0), ("t1", 1)], "typed")

    WAYS = ({"w": "L3_gnn_W1", "a": ("L3_gnn_a_src1", "L3_gnn_a_dst1"), "b": "L3_gnn_b1", "mask": "ds", "adj": "sd"},
            {"w": "L3_gnn_W2", "a": ("L3_gnn_a_src2", "L3_gnn_a_dst2"), "b": "L3_gnn_b2", "mask": "sd", "adj": "ds"})
    with ExitStack() as ctx:
        with ExitStack() as inner_ctx:
            T1 = sb(inner_ctx, "gT1", [P, NT, D])
            T2 = sb(inner_ctx, "gT2", [P, NT, D])
            mu = sb(inner_ctx, "gmu", [P, NT])
            var = sb(inner_ctx, "gvar", [P, NT])
            std = sb(inner_ctx, "gstd", [P, NT])
            PA = pb(inner_ctx, "gPA", [P, NBANK, BANK])

            def mapped_of(w, g):
                at = (w * GROUPS + g) % 2 * SET
                return PA[:, :, :].rearrange("p b n -> p (b n)")[:, at:at + CK * 2 * D].rearrange("p (t k) -> p t k", k=2 * D)
            sd, mapped, moved, scored, stored = (sem(f"l3_{k}") for k in ("vector", "mapped", "moved", "scored", "stored"))
            reach = sb(inner_ctx, "greach", [P, 4])
            WV = sb(inner_ctx, "WV", [P, D])
            WA = sb(inner_ctx, "WA", [P, 2, 2, HEADS])
            within = sb(inner_ctx, "gwithin", [1, 4])
            reached, everywhere = sem("l3_reached"), sem("l3_everywhere")
            with nc.Block() as block:
                @block.vector
                def _(dve):
                    step = Chain(dve, sd)
                    for w, way in enumerate(WAYS):
                        for i, vec in enumerate(way["a"]):
                            step(nc.vector.tensor_tensor(WV[:, :], w_of[way["w"]], b_of[vec], ALU.mult))
                            step(nc.vector.reduce_sum(WA[:, w, i, :], WV[:, :].rearrange("p (h c) -> p h c", c=CH), axis=AX.X))
                    norm_vector(dve, 3, T1, T2, mu, var, std)
                    dve.wait_ge(mapped, 1)
                    for q in range(3):
                        ins = nc.vector.tensor_copy(HT[:, q * BANK:(q + 1) * BANK], PA[:, q, :])
                    ins.then_inc(moved, 1)
                    nc.vector.memset(GE[:, :, :, :, CH:CH1], 1.0)
                    for w, way in enumerate(WAYS):
                        for g in range(GROUPS):
                            dve.wait_ge(mapped, 2 + w * GROUPS + g)
                            tiles = slice(g * GROUPS, (g + 1) * GROUPS)
                            nc.vector.tensor_copy(ES[:, w, :, :, tiles].rearrange("p i h t -> p t (i h)"), mapped_of(w, g)[:, :, D:D + 2 * HEADS])
                            nc.vector.tensor_copy(GE[:, w, tiles, :, 0:CH],
                                                  mapped_of(w, g)[:, :, 0:D].rearrange("p t (h c) -> p t h c", c=CH)).then_inc(moved, 1)
                    dve.wait_ge(moved, 2 + 2 * GROUPS)
                    step(nc.vector.tensor_scalar(ES2[:, :, :, :], ES[:, :, 0, :, :], SLOPE, None, ALU.mult))
                    nc.vector.tensor_reduce(reach[:, 0:1], ES[:, :, 0, :, :], axis=AX.XYZ, op=ALU.max, apply_absolute_value=True).then_inc(reached, 1)
                    nc.vector.tensor_reduce(reach[:, 1:2], GE[:, :, :, :, :].rearrange("p w t h c -> p (w t h c)"), axis=AX.X, op=ALU.max,
                                            apply_absolute_value=True).then_inc(reached, 1)
                    for i in range(4):
                        dve.wait_ge(mapped, 2 + 2 * GROUPS + i)
                        nc.vector.tensor_copy(rows[0:HEADS * NT, i, :], PA[0:HEADS * NT, i, 0:P]).then_inc(scored, 1)
                    dve.wait_ge(everywhere, 1)
                    step(nc.vector.tensor_scalar(within[:, 0:1], reach[0:1, 2:3], MILD_SCORE, None, ALU.is_le))
                    step(nc.vector.tensor_scalar(within[:, 1:2], reach[0:1, 3:4], MILD_FEATURE, None, ALU.is_le))
                    step(nc.vector.tensor_copy(within[:, 2:3], flag[:, :]))
                    step(nc.vector.tensor_tensor(within[:, 3:4], within[:, 0:1], within[:, 1:2], ALU.mult))
                    step(nc.vector.tensor_tensor(path[:, MILD:MILD + 1], within[:, 2:3], within[:, 3:4], ALU.mult))
                    step(nc.vector.tensor_tensor(within[:, 0:1], within[:, 2:3], within[:, 3:4], ALU.mult))
                    step(nc.vector.tensor_tensor(path[:, HARSH:HARSH + 1], within[:, 2:3], within[:, 0:1], ALU.subtract))
                    step(nc.vector.tensor_scalar(path[:, ANY_EDGES:ANY_EDGES + 1], within[:, 2:3], -1.0, 1.0, ALU.mult, ALU.add))
                    step(nc.vector.tensor_scalar(path[:, NOT_MILD:NOT_MILD + 1], within[:, 0:1], -1.0, 1.0, ALU.mult, ALU.add))

                @block.gpsimd
                def _(pool):
                    pool.wait_ge(reached, 2)
                    nc.gpsimd.partition_all_reduce(reach[:, 2:4], reach[:, 0:2], P, bass.bass_isa.ReduceOp.max).then_inc(everywhere, 1)

                @block.scalar
                def _(act):
                    norm_scalar(act, 3, T1, T2, var, std)
                    act.wait_ge(mapped, 1)
                    for q in range(3, NBANK):
                        ins = nc.scalar.activation(HT[:, q * BANK:q * BANK + bank_cols(q)], PA[:, q, 0:bank_cols(q)], ACT.Copy)
                    ins.then_inc(moved, 1)

                @block.tensor
                def _(pe):
                    pe.wait_ge(norm["h"], 4 * GROUPS)
                    for t in range(NT):
                        ins = nc.tensor.transpose(PA[:, t // 4, (t % 4) * P:(t % 4 + 1) * P], H[:, t, :], ident[:, :])
                    ins.then_inc(mapped, 1)
                    for w, way in enumerate(WAYS):
                        for g in range(GROUPS):
                            pe.wait_ge(moved, max(2, 1 + w * GROUPS + g))
                            for i in range(GROUPS):
                                t = g * GROUPS + i
                                nc.tensor.matmul(mapped_of(w, g)[:, i, 0:D], HT[:, t * P:(t + 1) * P], w_of[way["w"]], start=True, stop=True)
                                ins = nc.tensor.matmul(mapped_of(w, g)[:, i, D:D + 2 * HEADS], HT[:, t * P:(t + 1) * P], WA[:, w, :, :].rearrange("p i h -> p (i h)"),
                                                       start=True, stop=True)
                            ins.then_inc(mapped, 1)
                    pe.wait_ge(moved, 2 + 2 * GROUPS)
                    for i in range(4):
                        nc.tensor.transpose(PA[0:HEADS * NT, i, 0:P], ES[:, i % 2, i // 2, :, :].rearrange("p h t -> p (h t)"), ident[:, :]).then_inc(mapped, 1)

                @block.sync
                def _(sp):
                    for i in range(4):
                        sp.wait_ge(scored, 1 + i)
                        sp.dma_start(rows_dram[i if i < 2 else 4 + i].rearrange("h (t q) -> (h t) q", q=P), rows[0:HEADS * NT, i, :]).then_inc(stored, 16)
                    sp.wait_ge(stored, 64)

        hidden.close()

        with ExitStack() as inner_ctx:
            ESB = sb(inner_ctx, "ESB", [P, HEADS, NPAD])
            MB = sb(inner_ctx, "MB", [P, 2, NPAD])
            FAR = sb(inner_ctx, "FAR", [P, 2, NPAD], BF16)
            junk = sb(inner_ctx, "mjunk", [P, HEADS, NPAD], BF16)
            mt = sb(inner_ctx, "mt", [P, 2, HEADS])
            bigc = sb(inner_ctx, "bigc", [P, 1])
            loaded = [sem(f"m_loaded{i}") for i in range(2)]
            rowed, far, maxed, copied, setup = (sem(f"m_{k}") for k in ("rows", "far", "maxed", "copied", "setup"))
            with nc.Block() as block:
                def blocks(eng, w, one):
                    base = w * NT
                    one(w, 0, base, base % 2, base // 2 + 1)
                    with eng.Fori(0, (NT - 1) // 2) as j:
                        for u in (1, 2):
                            one(w, j * 2 + u, j * 2 + (base + u), (base + u) % 2, j + ((base + u) // 2 + 1))

                def by_path(eng, body):
                    for which, m in ((HARSH, fast), (ANY_EDGES, general)):
                        on_path(eng, which, lambda eng: [body(eng, m, w) for w in range(2)])

                @block.sync
                def _(sp):

                    def body(sp, m, w):
                        def one(w, j, n, slot, count):
                            if isinstance(j, int):
                                for h in range(HEADS):
                                    if w:
                                        sp.wait_ge(maxed, (NT - 1) * HEADS + h + 1)
                                    sp.dma_start(ESB[:, h, :], rows_dram[w, h].partition_broadcast(P)).then_inc(rowed, 16)
                            sp.wait_ge(far, n + 1)
                            sp.dma_start(m.view(MB[:, slot, :]), adj[m, WAYS[w]["mask"]][bass.ds(j * P, P), :]).then_inc(loaded[slot], 16)
                        blocks(sp, w, one)
                    by_path(sp, body)

                @block.scalar
                def _(act):
                    act.wait_ge(setup, 1)

                    def body(act, m, w):
                        if not w:
                            act.sem_inc(far, 2)
                        def one(w, j, n, slot, count):
                            act.wait_ge(loaded[slot], count * 16)
                            act.wait_ge(copied, n + 1)
                            nc.scalar.activation(FAR[:, slot, :], m.view(MB[:, slot, :]), ACT.Relu, bias=bigc[:, 0:1], scale=-BIG).then_inc(far, 1)
                        blocks(act, w, one)
                    by_path(act, body)

                @block.vector
                def _(dve):
                    nc.vector.memset(bigc[:, :], BIG).then_inc(setup, 1)
                    dve.sem_inc(copied, 2)

                    def keep(w, j, n, slot):
                        dve.wait_ge(maxed, n * HEADS + HEADS)
                        nc.vector.tensor_copy(MX[:, w, :, bass.ds(j, 1)], mt[:, slot, :].unsqueeze(2)).then_inc(copied, 1)

                    def one(w, j, n, slot, count):
                        if not isinstance(j, int):
                            dve.wait_ge(far, n + 3)
                            keep(w, j - 1, n - 1, 1 - slot)
                        else:
                            dve.wait_ge(far, n + 3)
                            dve.wait_ge(rowed, (w + 1) * 16 * HEADS)
                        for h in range(HEADS):
                            nc.vector.tensor_tensor_reduce(out=junk[:, h, :], in0=ESB[:, h, :], in1=FAR[:, slot, :], scale=1.0,
                                                           scalar=-3.0e38, op0=ALU.subtract, op1=ALU.max, accum_out=mt[:, slot, h:h + 1]).then_inc(maxed, 1)

                    def way(dve, w):
                        blocks(dve, w, one)
                        keep(w, NT - 1, w * NT + NT - 1, (w * NT + NT - 1) % 2)
                    on_path(dve, NOT_MILD, lambda dve: [way(dve, w) for w in range(2)])

        def maxima(step, ways, z1, z2, z3):
            src, dst, greatest = ES[:, ways, 0, :, :], ES[:, ways, 1, :, :], MX[:, ways, :, :]
            z1, z2, z3 = z1[:, :, :, :], z2[:, :, :, :], z3[:, :, :, :]
            step(nc.vector.tensor_tensor(z1, greatest, src, ALU.max))
            step(nc.vector.tensor_tensor(z1, z1, dst, ALU.add))
            step(nc.vector.tensor_scalar(z2, z1, SLOPE, None, ALU.mult))
            step(nc.vector.tensor_tensor(z1, z1, z2, ALU.max))
            step(nc.vector.tensor_tensor(EM[:, ways, 0, :, :], dst, z1, ALU.subtract))
            step(nc.vector.tensor_scalar(z2, dst, SLOPE, None, ALU.mult))
            step(nc.vector.tensor_tensor(EM[:, ways, 1, :, :], z2, z1, ALU.subtract))
            step(nc.vector.tensor_tensor(z2, src, dst, ALU.add))
            step(nc.vector.tensor_scalar(z3, z2, SLOPE, None, ALU.mult))
            step(nc.vector.tensor_tensor(z2, z2, z3, ALU.max))
            step(nc.vector.tensor_tensor(z2, z2, z1, ALU.subtract))

        with ExitStack() as inner_ctx:
            Z1 = sb(inner_ctx, "Z1", [P, 2, HEADS, NT])
            Z2 = sb(inner_ctx, "Z2", [P, 2, HEADS, NT])
            Z3 = sb(inner_ctx, "Z3", [P, 2, HEADS, NT])
            PT = pb(inner_ctx, "ePT", [P, 4, BANK])
            sd, own, turned, moved, stored = (sem(f"e_{k}") for k in ("vector", "own", "turned", "moved", "stored"))
            with nc.Block() as block:
                @block.vector
                def _(dve):
                    def program_of(dve):
                        step = Chain(dve, sd)
                        maxima(step, slice(0, 2), Z1, Z2, Z3)
                        for i in range(4):
                            dve.wait_ge(turned, i + 1)
                            nc.vector.tensor_copy(rows[0:HEADS * NT, i, :], PT[0:HEADS * NT, i, 0:P]).then_inc(moved, 1)
                    on_path(dve, NOT_MILD, program_of)

                @block.scalar
                def _(act):
                    def program_of(act):
                        act.wait_ge(sd, 11)
                        for w in range(2):
                            nc.scalar.activation(XS[:, w, :, :].rearrange("p t h -> p h t"), Z2[:, w, :, :], ACT.Exp).then_inc(own, 1)
                    on_path(act, NOT_MILD, program_of)

                @block.tensor
                def _(pe):
                    def program_of(pe):
                        pe.wait_ge(sd, 7)
                        for i in range(4):
                            nc.tensor.transpose(PT[0:HEADS * NT, i, 0:P], EM[:, i // 2, i % 2, :, :].rearrange("p h t -> p (h t)"), ident[:, :]).then_inc(turned, 1)
                    on_path(pe, NOT_MILD, program_of)

                @block.sync
                def _(sp):
                    def program_of(sp):
                        for i in range(4):
                            sp.wait_ge(moved, i + 1)
                            sp.dma_start(rows_dram[2 + i].rearrange("h (t q) -> (h t) q", q=P), rows[0:HEADS * NT, i, :]).then_inc(stored, 16)
                        sp.wait_ge(stored, 64)
                    on_path(sp, NOT_MILD, program_of)

        with ExitStack() as inner_ctx:
            SLOTS = 5
            ROUNDS = NT // SLOTS
            C2 = 2 * CH1
            ROW = HEADS * C2 + HEADS * CH1
            AROW = sb(inner_ctx, "AROW", [P, 2, HEADS, CHUNK])
            shared_space = sb(inner_ctx, "shared_space", [P, SLOTS * (HEADS + 1) * CHUNK // 2])
            halves = shared_space[:, :].bitcast(F16)
            MA = halves[:, 0:SLOTS * HEADS * CHUNK].rearrange("p (s h n) -> p s h n", s=SLOTS, h=HEADS)
            AC = halves[:, SLOTS * HEADS * CHUNK:].rearrange("p (s n) -> p s n", s=SLOTS)
            V = shared_space[:, 0:NT * HEADS * C2].rearrange("p (t h c) -> p t h c", h=HEADS, c=C2)
            ESC = sb(inner_ctx, "ESC", [P, 2, HEADS, CHUNK])
            FAR = sb(inner_ctx, "fFAR", [P, SLOTS, CHUNK], F16)
            junk = sb(inner_ctx, "fjunk", [P, HEADS, CHUNK], BF16)
            tops = sb(inner_ctx, "tops", [P, SLOTS, HEADS])
            MXC = sb(inner_ctx, "MXC", [P, NCHUNK, NT, HEADS])
            Z1 = sb(inner_ctx, "fZ1", [P, 1, HEADS, NT])
            Z2 = sb(inner_ctx, "fZ2", [P, 1, HEADS, NT])
            Z3 = sb(inner_ctx, "fZ3", [P, 1, HEADS, NT])
            bigc = sb(inner_ctx, "fbigc", [P, 1])
            KEPT = NCHUNK * ROUNDS + 12
            SUMS = shared_space[:, 0:(NCHUNK - 1) * GROUPS * ROW].rearrange("p (c t n) -> p c t n", t=GROUPS, n=ROW)
            LIFT = 2.0 ** 64
            UP = sb(inner_ctx, "UP", [P, 2, HEADS, NT])
            QS = sb(inner_ctx, "QS", [P, 2, 2, NT, HEADS])
            PR = sb(inner_ctx, "PR", [P, 2, 2, NT, HEADS])
            VAL = sb(inner_ctx, "VAL", [P, 3, NT, HEADS, C2], BF16)
            F = sb(inner_ctx, "F", [P, GROUPS, ROW])
            T3 = sb(inner_ctx, "fT3", [P, GROUPS, HEADS, CH1])
            U3 = sb(inner_ctx, "fU3", [P, GROUPS, HEADS, CH1])
            RC = sb(inner_ctx, "fRC", [P, GROUPS, HEADS])
            O = sb(inner_ctx, "fO", [P, GROUPS, D])
            KZ = sb(inner_ctx, "fKZ", [P, BANK], F16)
            PN = pb(inner_ctx, "fPN", [P, GROUPS, BANK])
            VF = VAL[:, :, :, :, :].rearrange("p a t h c -> p a (t h c)")
            VH = VAL[:, :, :, :, :].rearrange("p a t h c -> p a (t h) c")
            loaded = [sem(f"f_loaded{i}") for i in range(SLOTS)]
            rowed = [sem(f"f_rows{i}") for i in range(2)]
            zeros, factors, product, high, lower, middle, valued, sd, added = (
                sem(f"f_{k}") for k in ("zeros", "factors", "product", "high", "lower", "middle", "valued", "vector", "added"))
            lifted, masked, maxed, topped, weighed, staged, spilled, reloaded, finished = (
                sem(f"f_{k}") for k in ("lifted", "masked", "maxed", "topped", "weighed", "staged", "spilled", "reloaded", "finished"))

            def chunks(eng, one, at_way=lambda w: None):
                for w in range(2):
                    at_way(w)
                    base = w * NCHUNK
                    one(w, 0, base, base % 2, base // 2 + 1)
                    with eng.Fori(0, (NCHUNK - 1) // 2) as i:
                        for u in (1, 2):
                            one(w, i * 2 + u, i * 2 + (base + u), (base + u) % 2, i + ((base + u) // 2 + 1))

            def group_of(v, g):
                return v[:, g * GROUPS:(g + 1) * GROUPS, :, :]

            with nc.Block() as block:
                @block.sync
                def _(sp):
                    def program_of(sp):
                        def chunk(w, c, n, rs, count):
                            if not (isinstance(n, int) and n == 0):
                                sp.wait_ge(weighed, (n - 1) * NT + SLOTS)
                            for h in range(HEADS):
                                sp.dma_start(AROW[:, rs, h, :], rows_dram[6 + w, h, bass.ds(c * CHUNK, CHUNK)].partition_broadcast(P)).then_inc(rowed[rs], 16)
                                sp.dma_start(ESC[:, rs, h, :], rows_dram[w, h, bass.ds(c * CHUNK, CHUNK)].partition_broadcast(P)).then_inc(rowed[rs], 16)
                            if isinstance(c, int):
                                sp.wait_ge(valued, (w + 1) * GROUPS)
                            with sp.Fori(0, ROUNDS) as j:
                                for slot in range(SLOTS):
                                    k = j * SLOTS + slot
                                    source = adj[fast, WAYS[w]["adj"]][bass.ds(k * P, P), bass.ds(c * CHUNK, CHUNK)]
                                    sp.compute_val(source.offset * mybir.dt.size(fast.dt))
                                    sp.wait_ge(weighed, n * NT + k + 1)
                                    sp.dma_start(AC[:, slot, :], source).then_inc(loaded[slot], 16)
                                    sp.dma_start(FAR[:, slot, :], adj[fast, WAYS[w]["mask"]][bass.ds(k * P, P), bass.ds(c * CHUNK, CHUNK)]).then_inc(loaded[slot], 16)
                        chunks(sp, chunk)
                    on_path(sp, MILD, program_of)

                @block.gpsimd
                def _(pool):
                    def program_of(pool):
                        flat = F[:, :, :].rearrange("p t n -> p (t n)")

                        def spill(n):
                            pool.wait_ge(staged, n + 1)
                            pool.dma_start(sums_dram[n], flat).then_inc(spilled, 16)
                        for n in range(2 * NCHUNK - 1):
                            if n >= NCHUNK:
                                pool.wait_ge(spilled, n * 16)
                                pool.dma_start(flat, sums_dram[n - NCHUNK]).then_inc(reloaded, 16)
                            spill(n)
                        pool.wait_ge(spilled, (2 * NCHUNK - 1) * 16)
                        pool.dma_start(flat, sums_dram[NCHUNK - 1]).then_inc(reloaded, 16)
                        pool.wait_ge(staged, 2 * NCHUNK)
                        for c in range(NCHUNK - 1):
                            pool.dma_start(SUMS[:, c, :, :].rearrange("p t n -> p (t n)"), sums_dram[NCHUNK + c]).then_inc(reloaded, 16)
                            pool.wait_ge(reloaded, (NCHUNK + c + 1) * 16)
                    on_path(pool, MILD, program_of)

                @block.scalar
                def _(act):
                    def program_of(act):
                        for w in range(2):
                            for i, v in enumerate((ES[:, w, 0, :, :], ES2[:, w, :, :])):
                                nc.scalar.activation(QS[:, w, i, :, :].rearrange("p t h -> p h t"), v, ACT.Exp).then_inc(factors, 1)

                        def powers(w):
                            act.wait_ge(topped, (w + 1) * KEPT + 1)
                            for i in range(2):
                                nc.scalar.activation(PR[:, w, i, :, :].rearrange("p t h -> p h t"), EM[:, w, i, :, :], ACT.Exp).then_inc(factors, 1)
                            nc.scalar.activation(XS[:, w, :, :].rearrange("p t h -> p h t"), Z2[:, 0, :, :], ACT.Exp).then_inc(factors, 1)

                        def parts(w):
                            if w:
                                act.wait_ge(weighed, NCHUNK * NT + SLOTS)
                            for g in range(GROUPS):
                                act.wait_ge(product, w * GROUPS + g + 1)
                                nc.scalar.activation(group_of(VAL[:, 0, :, :, :], g), group_of(V, g), ACT.Copy).then_inc(high, 1)
                            for g in range(GROUPS):
                                act.wait_ge(lower, w * GROUPS + g + 1)
                                nc.scalar.activation(group_of(VAL[:, 1, :, :, :], g), group_of(V, g), ACT.Copy).then_inc(middle, 1)

                        def stage(n, second):
                            act.wait_ge(weighed, n * NT + (NT + SLOTS))
                            if second:
                                act.wait_ge(finished, n - (NCHUNK - 1))
                            elif not (isinstance(n, int) and n == 0):
                                act.wait_ge(spilled, n * 16)
                            for t in range(GROUPS):
                                ins = nc.scalar.activation(F[:, t, :], PN[:, t, 0:ROW], ACT.Copy)
                            ins.then_inc(staged, 1)

                        def way(w):
                            if w:
                                stage(NCHUNK - 1, False)
                                powers(0)
                            parts(w)
                            act.wait_ge(valued, (w + 1) * GROUPS)

                        def chunk(w, c, n, rs, count):
                            def lift(k, slot, rnd):
                                act.wait_ge(weighed, n * NT + k + 1)
                                act.wait_ge(loaded[slot], (n * ROUNDS + rnd + 1) * 32)
                                nc.scalar.activation(FAR[:, slot, :].bitcast(BF16), FAR[:, slot, :], ACT.Relu, bias=bigc[:, 0:1], scale=-BIG)
                                for h in range(HEADS):
                                    ins = nc.scalar.activation(MA[:, slot, h, :].bitcast(BF16), AROW[:, rs, h, :], ACT.Relu,
                                                               bias=UP[:, w, h, bass.ds(k, 1)], scale=LIFT)
                                ins.then_inc(lifted, 1)
                            if isinstance(c, int) and not w:
                                act.wait_ge(zeros, 3)
                            act.wait_ge(rowed[rs], count * (32 * HEADS))
                            for slot in range(SLOTS):
                                if slot == SLOTS - 1 and not isinstance(c, int):
                                    stage(n - 1, w == 1)
                                lift(slot, slot, 0)
                            with act.Fori(1, ROUNDS) as j:
                                for slot in range(SLOTS):
                                    lift(j * SLOTS + slot, slot, j)
                        chunks(act, chunk, way)
                        powers(1)
                        stage(2 * NCHUNK - 1, True)
                    on_path(act, MILD, program_of)

                @block.vector
                def _(dve):
                    def program_of(dve):
                        dve.sem_inc(maxed, HEADS)
                        dve.sem_inc(topped, 1)
                        nc.vector.memset(KZ[:, :], 0.0).then_inc(zeros, 1)
                        nc.vector.memset(bigc[:, :], BIG).then_inc(zeros, 1)
                        nc.vector.tensor_scalar(UP[:, :, :, :], ES[:, :, 0, :, :], LIFT, None, ALU.mult).then_inc(zeros, 1)

                        def parts(w):
                            if w:
                                dve.wait_ge(weighed, NCHUNK * NT + SLOTS)
                            else:
                                dve.wait_ge(factors, 4)
                            for g in range(GROUPS):
                                tiles = slice(g * GROUPS, (g + 1) * GROUPS)
                                for i in range(2):
                                    ins = nc.vector.tensor_tensor(group_of(V, g)[:, :, :, i * CH1:(i + 1) * CH1], GE[:, w, tiles, :, :],
                                                                  QS[:, w, i, tiles, :].unsqueeze(3).to_broadcast([P, GROUPS, HEADS, CH1]), ALU.mult)
                                ins.then_inc(product, 1)
                            for g in range(GROUPS):
                                dve.wait_ge(high, w * GROUPS + g + 1)
                                nc.vector.tensor_tensor(group_of(V, g), group_of(V, g), group_of(VAL[:, 0, :, :, :], g), ALU.subtract).then_inc(lower, 1)
                            for g in range(GROUPS):
                                dve.wait_ge(middle, w * GROUPS + g + 1)
                                nc.vector.tensor_tensor(group_of(VAL[:, 2, :, :, :], g), group_of(V, g), group_of(VAL[:, 1, :, :, :], g), ALU.subtract).then_inc(valued, 1)

                        def chunk(w, c, n, rs, count):
                            def mask(k, slot, rnd):
                                dve.wait_ge(lifted, n * NT + k + 1)
                                dve.wait_ge(maxed, (n * NT + k + 1) * HEADS)
                                if slot == 0:
                                    dve.wait_ge(topped, n * ROUNDS + rnd + (w * (KEPT - NCHUNK * ROUNDS) + 1))

                                def clip(heads):
                                    lifts = MA[:, slot, heads, :]
                                    return nc.vector.tensor_tensor(lifts, lifts.bitcast(BF16), outer(AC[:, slot, :], lifts.shape[1]), ALU.min)
                                clip(slice(0, 1))
                                for h in range(HEADS):
                                    nc.vector.tensor_tensor_reduce(out=junk[:, h, :], in0=ESC[:, rs, h, :], in1=FAR[:, slot, :].bitcast(BF16), scale=1.0,
                                                                   scalar=-3.0e38, op0=ALU.subtract, op1=ALU.max, accum_out=tops[:, slot, h:h + 1]).then_inc(maxed, 1)
                                clip(slice(1, HEADS)).then_inc(masked, 1)

                            def keep(rnd):
                                dve.wait_ge(maxed, (n * ROUNDS + rnd + 1) * (SLOTS * HEADS) + HEADS)
                                nc.vector.tensor_copy(MXC[:, :, :, :].rearrange("p c t h -> p (c t) h")[:, bass.ds(c * NT + rnd * SLOTS, SLOTS), :], tops[:, :, :]).then_inc(topped, 1)
                            dve.wait_ge(rowed[rs], count * (32 * HEADS))
                            for slot in range(SLOTS):
                                mask(slot, slot, 0)
                            keep(0)
                            with dve.Fori(1, ROUNDS) as j:
                                for slot in range(SLOTS):
                                    mask(j * SLOTS + slot, slot, j)
                                keep(j)
                            if w:
                                if isinstance(c, int):
                                    dve.wait_ge(factors, 4 + 3)
                                dve.wait_ge(reloaded, (c + 1) * 16)
                                final(0, c, n - NCHUNK, F)

                        def final(w, c, n, sums):
                            tiles = bass.ds(c * CT_TILES, CT_TILES)
                            at = 0

                            def then(ins):
                                nonlocal at
                                at += 1
                                ins.then_inc(sd, 1)
                                dve.wait_ge(sd, n * 7 + at)

                            def by_head(v):
                                return v.unsqueeze(3).to_broadcast([P, GROUPS, HEADS, CH1])
                            chosen = sums[:, :, 0:HEADS * C2].rearrange("p t (h c) -> p t h c", c=C2)
                            every = sums[:, :, HEADS * C2:ROW].rearrange("p t (h c) -> p t h c", c=CH1)
                            then(nc.vector.tensor_tensor(T3[:, :, :, :], every, chosen[:, :, :, CH1:C2], ALU.subtract))
                            nc.vector.tensor_tensor(U3[:, :, :, :], chosen[:, :, :, 0:CH1], by_head(PR[:, w, 0, tiles, :]), ALU.mult)
                            then(nc.vector.tensor_tensor(T3[:, :, :, :], T3[:, :, :, :], by_head(PR[:, w, 1, tiles, :]), ALU.mult))
                            then(nc.vector.tensor_tensor(T3[:, :, :, :], T3[:, :, :, :], U3[:, :, :, :], ALU.add))
                            then(nc.vector.tensor_tensor(U3[:, :, :, :], GE[:, w, tiles, :, :], by_head(XS[:, w, tiles, :]), ALU.mult))
                            then(nc.vector.tensor_tensor(T3[:, :, :, :], T3[:, :, :, :], U3[:, :, :, :], ALU.add))
                            then(nc.vector.reciprocal(RC[:, :, :], T3[:, :, :, CH]))
                            then(nc.vector.tensor_tensor(O[:, :, :].rearrange("p t (h c) -> p t h c", c=CH), T3[:, :, :, 0:CH], RC[:, :, :].unsqueeze(3).to_broadcast([P, GROUPS, HEADS, CH]), ALU.mult))
                            nc.vector.tensor_tensor(O[:, :, :], O[:, :, :], outer(b_of[WAYS[w]["b"]], GROUPS), ALU.add).then_inc(added, 1)
                            dve.wait_ge(added, n + 1)
                            nc.vector.scalar_tensor_tensor(out=X[:, tiles, :], in0=O[:, :, :], scalar=0.5, in1=X[:, tiles, :], op0=ALU.mult, op1=ALU.add).then_inc(finished, 1)

                        def finish_maxima(w):
                            step = Chain(dve, topped)
                            step.n = w * KEPT + NCHUNK * ROUNDS + 1
                            dve.wait_ge(topped, step.n)
                            step(nc.vector.reduce_max(MX[:, w, :, :], MXC[:, :, :, :].rearrange("p c t h -> p h t c"), axis=AX.X))
                            maxima(step, slice(w, w + 1), Z1, Z2, Z3)

                        def way(w):
                            if w:
                                finish_maxima(0)
                            parts(w)
                        chunks(dve, chunk, way)
                        finish_maxima(1)
                        dve.wait_ge(factors, 4 + 6)
                        for c in range(NCHUNK):
                            if c < NCHUNK - 1:
                                dve.wait_ge(reloaded, (NCHUNK + c + 1) * 16)
                            else:
                                dve.wait_ge(staged, 2 * NCHUNK)
                            final(1, c, NCHUNK + c, SUMS[:, c, :, :] if c < NCHUNK - 1 else F)
                    on_path(dve, MILD, program_of)

                @block.tensor
                def _(pe):
                    def program_of(pe):
                        pe.sem_inc(weighed, SLOTS)

                        def chunk(w, c, n, rs, count):
                            if not (isinstance(n, int) and n == 0):
                                pe.wait_ge(staged, n)
                            for t in range(GROUPS):
                                nc.tensor.matmul(PN[:, t, 0:ROW], KZ[:, 0:P], KZ[:, 0:ROW], start=True, stop=True)
                            with pe.Fori(0, ROUNDS) as j:
                                for slot in range(SLOTS):
                                    k = j * SLOTS + slot
                                    pe.wait_ge(masked, n * NT + k + 1)
                                    for t in range(GROUPS):
                                        at = slice(t * P, (t + 1) * P)
                                        for h in range(HEADS):
                                            for part in range(3):
                                                nc.tensor.matmul(PN[:, t, h * C2:(h + 1) * C2], MA[:, slot, h, at], VF[:, part, bass.ds(k * (HEADS * C2) + h * C2, C2)],
                                                                 start=False, stop=False, skip_group_check=True)
                                        for part in range(3):
                                            ins = nc.tensor.matmul(PN[:, t, HEADS * C2:ROW].rearrange("p (h c) -> p h c", c=CH1), AC[:, slot, at],
                                                                   VH[:, part, bass.ds(k * HEADS, HEADS), CH1:C2], start=False, stop=False, skip_group_check=True)
                                    ins.then_inc(weighed, 1)

                        def way(w):
                            if not w:
                                pe.wait_ge(zeros, 1)
                            pe.wait_ge(valued, (w + 1) * GROUPS)
                        chunks(pe, chunk, way)
                    on_path(pe, MILD, program_of)

        with ExitStack() as inner_ctx:
            SLOTS = 5
            ROUNDS = NT // SLOTS
            EMB = sb(inner_ctx, "EMB", [P, 2, 2, HEADS, CHUNK])
            AC = sb(inner_ctx, "AC", [P, SLOTS, CHUNK])
            Z = sb(inner_ctx, "Z", [P, SLOTS, HEADS, CHUNK])
            NUM = sb(inner_ctx, "NUM", [P, HEADS, CHUNK])
            T3 = sb(inner_ctx, "T3", [P, GROUPS, HEADS, CH1])
            RC = sb(inner_ctx, "RC", [P, GROUPS, HEADS])
            O = sb(inner_ctx, "O", [P, GROUPS, D])
            PN = pb(inner_ctx, "PN", [P, 2 * HEADS, BANK])
            under, exponent, exps, weight, turned, sd = (
                sem(f"b_{k}") for k in ("under", "exponent", "exps", "weight", "turned", "vector"))

            def chunks(eng, one):
                for w in range(2):
                    base = w * NCHUNK
                    one(w, 0, base, base % 2, base // 2 + 1)
                    with eng.Fori(0, (NCHUNK - 1) // 2) as i:
                        for u in (1, 2):
                            one(w, i * 2 + u, i * 2 + (base + u), (base + u) % 2, i + ((base + u) // 2 + 1))

            def before(w, c, n):
                if isinstance(c, int):
                    return (w - 1, NCHUNK - 1, n - 1) if w else None
                return (w, c - 1, n - 1)

            def staggered(eng, front, back, between):
                front(0, 0)
                for u in range(SLOTS):
                    front(u + 1, (u + 1) % SLOTS)
                    back(u, u, 0)
                    if u == 2:
                        between()
                with eng.Fori(1, ROUNDS - 1) as j:
                    for u in range(SLOTS):
                        front(j * SLOTS + (u + 1), (u + 1) % SLOTS)
                        back(j * SLOTS + u, u, j)
                for k in range(NT - SLOTS, NT):
                    if k + 1 < NT:
                        front(k + 1, (k + 1) % SLOTS)
                    back(k, k % SLOTS, k // SLOTS)

            with nc.Block() as block:
                @block.sync
                def _(sp):
                    def program_of(sp, m):
                        def body(sp, m):
                            def chunk(w, c, n, rs, count):
                                sp.wait_ge(finished, n + 1)
                                for kind in range(2):
                                    for h in range(HEADS):
                                        sp.dma_start(EMB[:, rs, kind, h, :], rows_dram[2 + 2 * w + kind, h, bass.ds(c * CHUNK, CHUNK)].partition_broadcast(P)).then_inc(rowed[rs], 16)
                                with sp.Fori(0, ROUNDS) as j:
                                    for slot in range(SLOTS):
                                        k = j * SLOTS + slot
                                        source = adj[m, WAYS[w]["adj"]][bass.ds(k * P, P), bass.ds(c * CHUNK, CHUNK)]
                                        sp.compute_val(source.offset * mybir.dt.size(m.dt))
                                        sp.wait_ge(weight, n * NT + k + 1)
                                        a_c = AC[:, slot, :]
                                        a_c = a_c if not m.fast else a_c.bitcast(F16)[:, 0:CHUNK]
                                        sp.dma_start(a_c, source).then_inc(loaded[slot], 16)
                            chunks(sp, chunk)
                        body(sp, m)
                    on_path(sp, HARSH, lambda sp: program_of(sp, fast))
                    on_path(sp, ANY_EDGES, lambda sp: program_of(sp, general))

                @block.scalar
                def _(act):
                    def program_of(act):
                        def stage(n):
                            act.wait_ge(weighed, n * NT + (NT + SLOTS))
                            for i in range(2 * HEADS):
                                ins = nc.scalar.activation(NUM[0:CH1, i // 2, (i % 2) * MMC:(i % 2 + 1) * MMC], PN[0:CH1, i, 0:MMC], ACT.Copy)
                            ins.then_inc(staged, 1)

                        def chunk(w, c, n, rs, count):
                            def low(k, slot):
                                act.wait_ge(weighed, n * NT + k + 1)
                                for h in range(HEADS):
                                    ins = nc.scalar.activation(Z[:, slot, h, :], EMB[:, rs, 1, h, :], ACT.Identity, bias=ES2[:, w, h, bass.ds(k, 1)])
                                ins.then_inc(under, 1)

                            def exp(k, slot, rnd):
                                act.wait_ge(exponent, n * NT + k + 1)
                                nc.scalar.activation(Z[:, slot, :, :], Z[:, slot, :, :], ACT.Exp).then_inc(exps, 1)
                            act.wait_ge(rowed[rs], count * (16 * 2 * HEADS))
                            last = before(w, c, n)
                            staggered(act, low, exp, lambda: stage(last[2]) if last else None)
                        chunks(act, chunk)
                        stage(2 * NCHUNK - 1)
                    on_path(act, NOT_MILD, program_of)

                @block.vector
                def _(dve):
                    def program_of(dve, m):
                        dve.sem_inc(finished, 2)
                        dve.sem_inc(weight, SLOTS)

                        def body(dve, m):
                            def chunk(w, c, n, rs, count):
                                def top_of(k, slot):
                                    dve.wait_ge(under, n * NT + k + 1)
                                    for h in range(HEADS):
                                        ins = nc.vector.scalar_tensor_tensor(out=Z[:, slot, h, :], in0=EMB[:, rs, 0, h, :], scalar=ES[:, w, 0, h, bass.ds(k, 1)],
                                                                             in1=Z[:, slot, h, :], op0=ALU.add, op1=ALU.max)
                                    ins.then_inc(exponent, 1)

                                def times(k, slot, rnd):
                                    dve.wait_ge(exps, n * NT + k + 1)
                                    dve.wait_ge(loaded[slot], (n * ROUNDS + rnd + 1) * 16)
                                    a_c = AC[:, slot, :]
                                    a_c = a_c if not m.fast else a_c.bitcast(F16)[:, 0:CHUNK]
                                    nc.vector.scalar_tensor_tensor(out=Z[:, slot, :, :], in0=Z[:, slot, :, :], scalar=1.0, in1=outer(a_c, HEADS),
                                                                   op0=ALU.min, op1=ALU.mult).then_inc(weight, 1)
                                dve.wait_ge(rowed[rs], count * (16 * 2 * HEADS))
                                last = before(w, c, n)
                                staggered(dve, top_of, times, lambda: final(*last) if last else None)

                            def final(w, c, n):
                                tiles = bass.ds(c * CT_TILES, CT_TILES)
                                nc.vector.tensor_tensor(T3[:, :, :, :], GE[:, w, tiles, :, :], XS[:, w, tiles, :].unsqueeze(3).to_broadcast([P, GROUPS, HEADS, CH1]), ALU.mult).then_inc(sd, 1)
                                dve.wait_ge(sd, n * 5 + 1)
                                dve.wait_ge(turned, n + 1)
                                nc.vector.tensor_tensor(T3[:, :, :, :], PN[:, 0:GROUPS, 0:HEADS * CH1].rearrange("p t (h c) -> p t h c", c=CH1), T3[:, :, :, :], ALU.add).then_inc(sd, 1)
                                dve.wait_ge(sd, n * 5 + 2)
                                nc.vector.reciprocal(RC[:, :, :], T3[:, :, :, CH]).then_inc(sd, 1)
                                dve.wait_ge(sd, n * 5 + 3)
                                nc.vector.tensor_tensor(O[:, :, :].rearrange("p t (h c) -> p t h c", c=CH), T3[:, :, :, 0:CH], RC[:, :, :].unsqueeze(3).to_broadcast([P, GROUPS, HEADS, CH]), ALU.mult).then_inc(sd, 1)
                                dve.wait_ge(sd, n * 5 + 4)
                                nc.vector.tensor_tensor(O[:, :, :], O[:, :, :], outer(b_of[WAYS[w]["b"]], GROUPS), ALU.add).then_inc(sd, 1)
                                dve.wait_ge(sd, n * 5 + 5)
                                nc.vector.scalar_tensor_tensor(out=X[:, tiles, :], in0=O[:, :, :], scalar=0.5, in1=X[:, tiles, :], op0=ALU.mult, op1=ALU.add).then_inc(finished, 1)
                            chunks(dve, chunk)
                            final(1, NCHUNK - 1, 2 * NCHUNK - 1)
                        body(dve, m)
                    on_path(dve, HARSH, lambda dve: program_of(dve, fast))
                    on_path(dve, ANY_EDGES, lambda dve: program_of(dve, general))

                @block.tensor
                def _(pe):
                    def program_of(pe):
                        pe.sem_inc(weighed, SLOTS)

                        def chunk(w, c, n, rs, count):
                            pe.wait_ge(finished, n + 2)
                            for k in range(NT):
                                pe.wait_ge(weight, n * NT + k + (1 + SLOTS))
                                for h in range(HEADS):
                                    for half in range(2):
                                        ins = nc.tensor.matmul(PN[0:CH1, 2 * h + half, 0:MMC], GE[:, w, k, h, :], Z[:, k % SLOTS, h, half * MMC:(half + 1) * MMC],
                                                               start=(k == 0), stop=(k == NT - 1))
                                ins.then_inc(weighed, 1)
                            pe.wait_ge(staged, n + 1)
                            for t in range(GROUPS):
                                for h in range(HEADS):
                                    turned_to, num, unit = PN[:, t, h * CH1:(h + 1) * CH1], NUM[0:CH1, h, t * P:(t + 1) * P], ident[0:CH1, 0:CH1]
                                    if t == h == 0:
                                        nc.tensor.matmul(turned_to, num, unit, start=True, stop=True)
                                    else:
                                        ins = nc.tensor.transpose(turned_to, num, unit)
                            ins.then_inc(turned, 1)
                        chunks(pe, chunk)
                    on_path(pe, NOT_MILD, program_of)

    with ExitStack() as ctx:
        done = sem("stored")
        with nc.Block() as block:
            @block.sync
            def _(sp):
                sp.dma_start(out[0:(NT - 1) * P, :].rearrange("(t p) d -> p t d", p=P), X[:, 0:NT - 1, :]).then_inc(done, 16)
                sp.dma_start(out[(NT - 1) * P:N, :], X[0:N - (NT - 1) * P, NT - 1, :]).then_inc(done, 16)
                sp.wait_ge(done, 32)
    top.close()


_INS = ["x", "src", "dst", "edge_type_2", "L0_gnn_W_self1", "L0_gnn_W_neigh1", "L0_gnn_b1", "L0_gnn_W_self2",
        "L0_gnn_W_neigh2", "L0_gnn_b2", "L1_gnn_W_self", "L1_gnn_W_neigh", "L2_gnn_W_data", "L2_gnn_b_data",
        "L2_gnn_W_control", "L2_gnn_b_control", "L2_gnn_W_self", "L2_gnn_b_self", "L3_gnn_W1", "L3_gnn_a_src1",
        "L3_gnn_a_dst1", "L3_gnn_b1", "L3_gnn_W2", "L3_gnn_a_src2", "L3_gnn_a_dst2", "L3_gnn_b2"]


def kernel(**inputs):
    import concourse.bacc as _bacc
    from concourse.bass_utils import run_bass_kernel_spmd as _run

    nc = _bacc.Bacc("TRN2", target_bir_lowering=False, num_devices=1)
    arrays, aps = {}, {}
    for name in _INS:
        v = np.ascontiguousarray(inputs[name])
        arrays[f"in_{name}_dram"] = v
        aps[name] = nc.dram_tensor(f"in_{name}_dram", v.shape, mybir.dt.from_np(v.dtype), kind="ExternalInput").ap()
    out = nc.dram_tensor("out_0_dram", (N, D), F32, kind="ExternalOutput").ap()
    program(nc, aps, out)
    r = _run(nc, [arrays], core_ids=[0])
    return r.results[0]["out_0_dram"]
```
